# Optimizing a Trainium2 kernel written in Bass

```python
import numpy as np
import jax
import jax.numpy as jnp

def _softmax(x, axis=-1):
    return jax.nn.softmax(x, axis=axis)

def _gelu(x):
    return jax.nn.gelu(x, approximate=True)

def _silu(x):
    return jax.nn.silu(x)

def _sigmoid(x):
    return jax.nn.sigmoid(x)

def _layernorm(x, axis=-1, eps=1e-05):
    m = jnp.mean(x, axis=axis, keepdims=True)
    v = jnp.var(x, axis=axis, keepdims=True)
    return (x - m) / jnp.sqrt(v + eps)

def _scatter_add(tgt, idx, src, axis=0):
    return tgt.at[idx].add(src)

def _segment_sum(src, seg, n):
    return jax.ops.segment_sum(src, seg, n)
kernel_name = 'mk_recurrent_d2_jaxref_r8_34a7ce'

def setup_inputs(seed: int=0):
    np.random.seed(seed)
    _w = jnp.asarray

    def _L0_attn_setup():
        import jax, jax.numpy as jnp
        import numpy as np
        B, N, W = (4, 512, 128)
        H, A, P = (16, 64, 64)
        key = jax.random.key(seed)
        ks = jax.random.split(key, 11)
        u = lambda k, shape: jax.random.uniform(k, shape, jnp.float32, -0.05, 0.05)
        glorot_v = (2.0 / (W + A)) ** 0.5
        return {'x': jax.random.normal(ks[0], (B, N, W), jnp.float32), 'k1': u(ks[1], (H, W)), 'k2': u(ks[2], (H, W)), 'k3': u(ks[3], (H, W)), 'a1': u(ks[4], (H, P, 1)), 'a2': u(ks[5], (H, P, 1)), 'b1': u(ks[6], (H, P, 1)), 'b2': u(ks[7], (H, P, 1)), 'c': u(ks[8], (H, P, 1)), 'value_weight': jax.random.normal(ks[9], (H, W, A), jnp.float32) * glorot_v, 'output_weight': jax.random.normal(ks[10], (H, W, A), jnp.float32) * glorot_v}
    _L0_attn_in = _L0_attn_setup()

    def _L0_ffn_setup():
        import jax, jax.numpy as jnp
        import numpy as np
        LOOPS = 2
        NUM_GROUPS = 4
        EXPERTS_PER_GROUP = 2
        NUM_EXPERTS = NUM_GROUPS * EXPERTS_PER_GROUP
        GROUPS_TOP_K = 2
        TOP_K = 1
        RMS_EPS = 1e-06
        EPS = 1e-09

        def _rmsnorm(x, w):
            return x * jax.lax.rsqrt(jnp.mean(x * x, axis=-1, keepdims=True) + RMS_EPS) * w

        def _combine_weights(x_flat, w_macro, w_micro):
            T = x_flat.shape[0]
            macro = jax.nn.softmax(x_flat @ w_macro.T, axis=-1)
            mvals, midx = jax.lax.top_k(macro, GROUPS_TOP_K)
            mvals = mvals / (jnp.sum(mvals, axis=-1, keepdims=True) + EPS)
            micro = jax.nn.softmax(jnp.einsum('td,ged->tge', x_flat, w_micro), axis=-1)
            uvals, uidx = jax.lax.top_k(micro, TOP_K)
            uvals = uvals / (jnp.sum(uvals, axis=-1, keepdims=True) + EPS)
            tok = jnp.arange(T)
            combine = jnp.zeros((T, NUM_EXPERTS), x_flat.dtype)
            for s in range(GROUPS_TOP_K):
                g = midx[:, s]
                wg = mvals[:, s:s + 1]
                li = uidx[tok, g]
                lv = uvals[tok, g]
                eidx = g[:, None] * EXPERTS_PER_GROUP + li
                combine = combine.at[tok[:, None], eidx].add(lv * wg)
            return combine
        key = jax.random.key(seed)
        ks = jax.random.split(key, 6)
        B, S, D, F = (2, 128, 128, 256)
        return {'z': jax.random.normal(ks[0], (B, S, D), jnp.float32), 'norm_w': jnp.ones((D,), jnp.float32), 'w_macro': jax.random.normal(ks[1], (NUM_GROUPS, D), jnp.float32) * D ** (-0.5), 'w_micro': jax.random.normal(ks[2], (NUM_GROUPS, EXPERTS_PER_GROUP, D), jnp.float32) * D ** (-0.5), 'w1': jax.random.normal(ks[3], (NUM_EXPERTS, F, D), jnp.float32) * D ** (-0.5), 'w2': jax.random.normal(ks[4], (NUM_EXPERTS, D, F), jnp.float32) * F ** (-0.5)}
    _L0_ffn_in = _L0_ffn_setup()

    def _L1_attn_setup():
        import jax, jax.numpy as jnp
        import numpy as np
        import math
        D_MODEL = 128
        N_HEADS = 16
        D_K = D_MODEL // N_HEADS
        BATCH = 4
        SEQ = 256
        TRAINING_PROGRESS = 0.25
        CONVERGENCE_PHASE = 0.5
        TENSION = abs(1.0 - 1.0)

        def _pos_encoding(seq_len, d, yellow):
            phase_mod = 0.1 * math.sin(2.0 * math.pi * TRAINING_PROGRESS)
            i_even = jnp.arange(0, d, 2, dtype=jnp.float32)
            denom = jnp.power(10000.0, 2.0 * i_even / d) * (1.0 + yellow * phase_mod)
            pos = jnp.arange(seq_len, dtype=jnp.float32)
            ang = pos[:, None] / denom[None, :]
            pe = jnp.zeros((seq_len, d), jnp.float32)
            pe = pe.at[:, 0::2].set(jnp.sin(ang))
            pe = pe.at[:, 1::2].set(jnp.cos(ang))
            return pe
        key = jax.random.key(seed)
        ks = jax.random.split(key, 8)
        x = jax.random.normal(ks[0], (BATCH, SEQ, D_MODEL), dtype=jnp.float32)
        rby = jax.random.uniform(ks[1], (3,), dtype=jnp.float32)
        s = 0.02
        Wq = jax.random.normal(ks[2], (D_MODEL, D_MODEL), dtype=jnp.float32) * s
        Wk = jax.random.normal(ks[3], (D_MODEL, D_MODEL), dtype=jnp.float32) * s
        Wv = jax.random.normal(ks[4], (D_MODEL, D_MODEL), dtype=jnp.float32) * s
        Wo = jax.random.normal(ks[5], (D_MODEL, D_MODEL), dtype=jnp.float32) * s
        bq = jnp.zeros((D_MODEL,), jnp.float32)
        bk = jnp.zeros((D_MODEL,), jnp.float32)
        bv = jnp.zeros((D_MODEL,), jnp.float32)
        bo = jnp.zeros((D_MODEL,), jnp.float32)
        ln_gamma = jnp.ones((D_MODEL,), jnp.float32)
        ln_beta = jnp.zeros((D_MODEL,), jnp.float32)
        return {'x': x, 'rby': rby, 'Wq': Wq, 'bq': bq, 'Wk': Wk, 'bk': bk, 'Wv': Wv, 'bv': bv, 'Wo': Wo, 'bo': bo, 'ln_gamma': ln_gamma, 'ln_beta': ln_beta}
    _L1_attn_in = _L1_attn_setup()

    def _L1_ffn_setup():
        import jax, jax.numpy as jnp
        import numpy as np
        DIM = 128
        DEPTH = 2
        HEADS = 8
        DIM_HEAD = 64
        WINDOW = 64
        INNER = HEADS * DIM_HEAD
        HID = int(DIM * 4 * 2 / 3)
        B, N = (2, 1024)
        QK_SCALE = 8.0

        def shift_token(t):
            t1, t2 = jnp.split(t, 2, axis=-1)
            t2 = jnp.pad(t2, ((0, 0), (1, 0), (0, 0)))[:, :-1]
            return jnp.concatenate([t1, t2], axis=-1)

        def l2norm(t):
            return t / jnp.clip(jnp.linalg.norm(t, axis=-1, keepdims=True), 1e-12)

        def rotate_half(x):
            x1, x2 = jnp.split(x, 2, axis=-1)
            return jnp.concatenate([-x2, x1], axis=-1)

        def rotary_xpos(q, k):
            n = q.shape[-2]
            half_idx = jnp.arange(0, DIM_HEAD, 2, dtype=jnp.float32)
            inv_freq = 1.0 / 10000.0 ** (half_idx / DIM_HEAD)
            t = jnp.arange(n, dtype=jnp.float32)
            freqs = t[:, None] * inv_freq[None, :]
            freqs = jnp.concatenate([freqs, freqs], axis=-1)
            base = (half_idx + 0.4 * DIM_HEAD) / (1.4 * DIM_HEAD)
            power = (t - n // 2) / float(WINDOW // 2)
            scale = base[None, :] ** power[:, None]
            scale = jnp.concatenate([scale, scale], axis=-1)
            cos, sin = (jnp.cos(freqs), jnp.sin(freqs))
            q = q * cos * scale + rotate_half(q) * sin * scale
            k = k * cos / scale + rotate_half(k) * sin / scale
            return (q, k)

        def local_attention(q, k, v):
            b, h, n, d = q.shape
            w = n // WINDOW
            bq = q.reshape(b, h, w, WINDOW, d) * QK_SCALE
            bk = k.reshape(b, h, w, WINDOW, d)
            bv = v.reshape(b, h, w, WINDOW, d)

            def look_around(t):
                p = jnp.pad(t, ((0, 0), (0, 0), (1, 0), (0, 0), (0, 0)))
                return jnp.concatenate([p[:, :, :w], p[:, :, 1:]], axis=3)
            bk, bv = (look_around(bk), look_around(bv))
            bt = jnp.arange(n).reshape(w, WINDOW)
            btp = jnp.pad(bt, ((1, 0), (0, 0)), constant_values=-1)
            btk = jnp.concatenate([btp[:w], btp[1:]], axis=1)
            sim = jnp.einsum('bhwid,bhwjd->bhwij', bq, bk)
            i = bt[:, :, None]
            j = btk[:, None, :]
            mask = (i < j) | (i > j + WINDOW) | (j == -1)
            sim = jnp.where(mask, -jnp.finfo(sim.dtype).max, sim)
            attn = jax.nn.softmax(sim, axis=-1)
            out = jnp.einsum('bhwij,bhwjd->bhwid', attn, bv)
            return out.reshape(b, h, n, d)

        def _layer(x, wqkv, qs, ksc, wo, lg, lb, w1, b1, w2, b2):
            b, n, _ = x.shape
            h = shift_token(x)
            qkv = h @ wqkv
            q, k, v = jnp.split(qkv, 3, axis=-1)
            to_heads = lambda t: t.reshape(b, n, HEADS, DIM_HEAD).transpose(0, 2, 1, 3)
            q, k, v = (to_heads(q), to_heads(k), to_heads(v))
            q = l2norm(q) * qs
            k = l2norm(k) * ksc
            q, k = rotary_xpos(q, k)
            o = local_attention(q, k, v)
            o = o.transpose(0, 2, 1, 3).reshape(b, n, INNER)
            x = x + o @ wo
            h = shift_token(x)
            mu = h.mean(-1, keepdims=True)
            var = h.var(-1, keepdims=True)
            h = (h - mu) / jnp.sqrt(var + 1e-05) * lg + lb
            h = h @ w1 + b1
            a, g = jnp.split(h, 2, axis=-1)
            h = a * jax.nn.gelu(g, approximate=False)
            x = x + h @ w2 + b2
            return x
        key = jax.random.key(seed)
        ks = jax.random.split(key, 6)
        return {'x': jax.random.normal(ks[0], (B, N, DIM), jnp.float32), 'wqkv': jax.random.normal(ks[1], (DEPTH, DIM, 3 * INNER), jnp.float32) * 0.02, 'q_scale': jnp.ones((DEPTH, DIM_HEAD), jnp.float32), 'k_scale': jnp.ones((DEPTH, DIM_HEAD), jnp.float32), 'wo': jax.random.normal(ks[2], (DEPTH, INNER, DIM), jnp.float32) * 0.02, 'ln_g': jnp.ones((DEPTH, DIM), jnp.float32), 'ln_b': jnp.zeros((DEPTH, DIM), jnp.float32), 'w1': jax.random.normal(ks[3], (DEPTH, DIM, 2 * HID), jnp.float32) * 0.02, 'b1': jnp.zeros((DEPTH, 2 * HID), jnp.float32), 'w2': jax.random.normal(ks[4], (DEPTH, HID, DIM), jnp.float32) * 0.02, 'b2': jnp.zeros((DEPTH, DIM), jnp.float32)}
    _L1_ffn_in = _L1_ffn_setup()
    _d = {'L0_attn_x': _L0_attn_in['x'], 'L0_attn_k1': _L0_attn_in['k1'], 'L0_attn_k2': _L0_attn_in['k2'], 'L0_attn_k3': _L0_attn_in['k3'], 'L0_attn_a1': _L0_attn_in['a1'], 'L0_attn_a2': _L0_attn_in['a2'], 'L0_attn_b1': _L0_attn_in['b1'], 'L0_attn_b2': _L0_attn_in['b2'], 'L0_attn_c': _L0_attn_in['c'], 'L0_attn_value_weight': _L0_attn_in['value_weight'], 'L0_attn_output_weight': _L0_attn_in['output_weight'], 'L0_ffn_norm_w': _L0_ffn_in['norm_w'], 'L0_ffn_w_macro': _L0_ffn_in['w_macro'], 'L0_ffn_w_micro': _L0_ffn_in['w_micro'], 'L0_ffn_w1': _L0_ffn_in['w1'], 'L0_ffn_w2': _L0_ffn_in['w2'], 'L1_attn_rby': _L1_attn_in['rby'], 'L1_attn_Wq': _L1_attn_in['Wq'], 'L1_attn_bq': _L1_attn_in['bq'], 'L1_attn_Wk': _L1_attn_in['Wk'], 'L1_attn_bk': _L1_attn_in['bk'], 'L1_attn_Wv': _L1_attn_in['Wv'], 'L1_attn_bv': _L1_attn_in['bv'], 'L1_attn_Wo': _L1_attn_in['Wo'], 'L1_attn_bo': _L1_attn_in['bo'], 'L1_attn_ln_gamma': _L1_attn_in['ln_gamma'], 'L1_attn_ln_beta': _L1_attn_in['ln_beta'], 'L1_ffn_wqkv': _L1_ffn_in['wqkv'], 'L1_ffn_q_scale': _L1_ffn_in['q_scale'], 'L1_ffn_k_scale': _L1_ffn_in['k_scale'], 'L1_ffn_wo': _L1_ffn_in['wo'], 'L1_ffn_ln_g': _L1_ffn_in['ln_g'], 'L1_ffn_ln_b': _L1_ffn_in['ln_b'], 'L1_ffn_w1': _L1_ffn_in['w1'], 'L1_ffn_b1': _L1_ffn_in['b1'], 'L1_ffn_w2': _L1_ffn_in['w2'], 'L1_ffn_b2': _L1_ffn_in['b2']}
    _x0 = _d['L0_attn_x']
    _d['L0_attn_x'] = jax.random.normal(jax.random.fold_in(jax.random.key(seed), 1), (4, 1024, 128), dtype=_x0.dtype)
    del _x0
    return _d

def reference(L0_attn_x, L0_attn_k1, L0_attn_k2, L0_attn_k3, L0_attn_a1, L0_attn_a2, L0_attn_b1, L0_attn_b2, L0_attn_c, L0_attn_value_weight, L0_attn_output_weight, L0_ffn_norm_w, L0_ffn_w_macro, L0_ffn_w_micro, L0_ffn_w1, L0_ffn_w2, L1_attn_rby, L1_attn_Wq, L1_attn_bq, L1_attn_Wk, L1_attn_bk, L1_attn_Wv, L1_attn_bv, L1_attn_Wo, L1_attn_bo, L1_attn_ln_gamma, L1_attn_ln_beta, L1_ffn_wqkv, L1_ffn_q_scale, L1_ffn_k_scale, L1_ffn_wo, L1_ffn_ln_g, L1_ffn_ln_b, L1_ffn_w1, L1_ffn_b1, L1_ffn_w2, L1_ffn_b2):

    def _L0_attn_ref(x, k1, k2, k3, a1, a2, b1, b2, c, value_weight, output_weight):
        import jax, jax.numpy as jnp
        import numpy as np
        B, N, W = (4, 512, 128)
        H, A, P = (16, 64, 64)
        n = jnp.linspace(0.0, 1.0, x.shape[-2])
        p1 = jnp.sum(jnp.sin(a1 * n + b1) * c, axis=-2)
        p2 = jnp.sum(jnp.sin(a2 * n + b2) * c, axis=-2)
        cross = jnp.einsum('bnw,hw->bhn', x, k1) + p1
        diag = jnp.einsum('bnw,hw->bhn', x, k2)
        extra = jnp.einsum('bnw,hw->bhn', x, k3)
        values = jnp.einsum('bnw,hwa->bhna', x, value_weight)
        cexp = lambda z: jnp.exp(jnp.clip(z, -20.0, 20.0))[..., None]
        cross, diag, extra = (cexp(cross), cexp(diag), cexp(extra))
        p2e = cexp(p2)
        num = jnp.cumsum(cross * values, axis=2) * p2e * extra + values * diag
        den = jnp.cumsum(cross, axis=2) * p2e * extra + diag
        out = num / den
        return jnp.einsum('bhna,hwa->bnw', out, output_weight)

    def _L0_ffn_ref(z, norm_w, w_macro, w_micro, w1, w2):
        import jax, jax.numpy as jnp
        import numpy as np
        LOOPS = 2
        NUM_GROUPS = 4
        EXPERTS_PER_GROUP = 2
        NUM_EXPERTS = NUM_GROUPS * EXPERTS_PER_GROUP
        GROUPS_TOP_K = 2
        TOP_K = 1
        RMS_EPS = 1e-06
        EPS = 1e-09

        def _rmsnorm(x, w):
            return x * jax.lax.rsqrt(jnp.mean(x * x, axis=-1, keepdims=True) + RMS_EPS) * w

        def _combine_weights(x_flat, w_macro, w_micro):
            T = x_flat.shape[0]
            macro = jax.nn.softmax(x_flat @ w_macro.T, axis=-1)
            mvals, midx = jax.lax.top_k(macro, GROUPS_TOP_K)
            mvals = mvals / (jnp.sum(mvals, axis=-1, keepdims=True) + EPS)
            micro = jax.nn.softmax(jnp.einsum('td,ged->tge', x_flat, w_micro), axis=-1)
            uvals, uidx = jax.lax.top_k(micro, TOP_K)
            uvals = uvals / (jnp.sum(uvals, axis=-1, keepdims=True) + EPS)
            tok = jnp.arange(T)
            combine = jnp.zeros((T, NUM_EXPERTS), x_flat.dtype)
            for s in range(GROUPS_TOP_K):
                g = midx[:, s]
                wg = mvals[:, s:s + 1]
                li = uidx[tok, g]
                lv = uvals[tok, g]
                eidx = g[:, None] * EXPERTS_PER_GROUP + li
                combine = combine.at[tok[:, None], eidx].add(lv * wg)
            return combine
        B, S, D = z.shape
        T = B * S
        for _ in range(LOOPS):
            zn = _rmsnorm(z, norm_w)
            x = zn.reshape(T, D)
            combine = _combine_weights(x, w_macro, w_micro)
            h = jax.nn.silu(jnp.einsum('td,efd->tef', x, w1))
            y = jnp.einsum('tef,edf->ted', h, w2)
            mixed = jnp.einsum('ted,te->td', y, combine)
            z = z + mixed.reshape(B, S, D)
        return z

    def _L1_attn_ref(x, rby, Wq, bq, Wk, bk, Wv, bv, Wo, bo, ln_gamma, ln_beta):
        import jax, jax.numpy as jnp
        import numpy as np
        import math
        D_MODEL = 128
        N_HEADS = 16
        D_K = D_MODEL // N_HEADS
        BATCH = 4
        SEQ = 256
        TRAINING_PROGRESS = 0.25
        CONVERGENCE_PHASE = 0.5
        TENSION = abs(1.0 - 1.0)

        def _pos_encoding(seq_len, d, yellow):
            phase_mod = 0.1 * math.sin(2.0 * math.pi * TRAINING_PROGRESS)
            i_even = jnp.arange(0, d, 2, dtype=jnp.float32)
            denom = jnp.power(10000.0, 2.0 * i_even / d) * (1.0 + yellow * phase_mod)
            pos = jnp.arange(seq_len, dtype=jnp.float32)
            ang = pos[:, None] / denom[None, :]
            pe = jnp.zeros((seq_len, d), jnp.float32)
            pe = pe.at[:, 0::2].set(jnp.sin(ang))
            pe = pe.at[:, 1::2].set(jnp.cos(ang))
            return pe
        B, S, d = x.shape
        red, blue, yellow = (rby[0], rby[1], rby[2])
        x = x + _pos_encoding(S, d, yellow)[None, :, :]

        def proj(W, b):
            return (x @ W.T + b).reshape(B, S, N_HEADS, D_K).transpose(0, 2, 1, 3)
        Q, K, V = (proj(Wq, bq), proj(Wk, bk), proj(Wv, bv))
        scale = jnp.sqrt(D_K * (1.0 + TENSION * red))
        logits = jnp.einsum('bhqd,bhkd->bhqk', Q, K) / scale
        scale_matrix = 1.0 + red * 0.1 + blue * 0.05 + yellow * 0.15
        logits = logits * scale_matrix
        attn = jax.nn.softmax(logits, axis=-1)
        eps_adaptive = 0.1 * math.sin(2.0 * math.pi * CONVERGENCE_PHASE)
        out = jnp.einsum('bhqk,bhkd->bhqd', attn, V) * (1.0 + yellow * eps_adaptive)
        out = out.transpose(0, 2, 1, 3).reshape(B, S, d)
        out = out @ Wo.T + bo
        x = x + out
        mean = jnp.mean(x, axis=-1, keepdims=True)
        var = jnp.var(x, axis=-1, keepdims=True)
        eps_rby = 1e-05 * (1.0 + blue * 0.1)
        gamma_rby = ln_gamma * (1.0 + red * 0.1 + yellow * 0.05)
        normalized = (x - mean) / jnp.sqrt(var + eps_rby)
        return normalized * gamma_rby + ln_beta

    def _L1_ffn_ref(x, wqkv, q_scale, k_scale, wo, ln_g, ln_b, w1, b1, w2, b2):
        import jax, jax.numpy as jnp
        import numpy as np
        DIM = 128
        DEPTH = 2
        HEADS = 8
        DIM_HEAD = 64
        WINDOW = 64
        INNER = HEADS * DIM_HEAD
        HID = int(DIM * 4 * 2 / 3)
        B, N = (2, 1024)
        QK_SCALE = 8.0

        def shift_token(t):
            t1, t2 = jnp.split(t, 2, axis=-1)
            t2 = jnp.pad(t2, ((0, 0), (1, 0), (0, 0)))[:, :-1]
            return jnp.concatenate([t1, t2], axis=-1)

        def l2norm(t):
            return t / jnp.clip(jnp.linalg.norm(t, axis=-1, keepdims=True), 1e-12)

        def rotate_half(x):
            x1, x2 = jnp.split(x, 2, axis=-1)
            return jnp.concatenate([-x2, x1], axis=-1)

        def rotary_xpos(q, k):
            n = q.shape[-2]
            half_idx = jnp.arange(0, DIM_HEAD, 2, dtype=jnp.float32)
            inv_freq = 1.0 / 10000.0 ** (half_idx / DIM_HEAD)
            t = jnp.arange(n, dtype=jnp.float32)
            freqs = t[:, None] * inv_freq[None, :]
            freqs = jnp.concatenate([freqs, freqs], axis=-1)
            base = (half_idx + 0.4 * DIM_HEAD) / (1.4 * DIM_HEAD)
            power = (t - n // 2) / float(WINDOW // 2)
            scale = base[None, :] ** power[:, None]
            scale = jnp.concatenate([scale, scale], axis=-1)
            cos, sin = (jnp.cos(freqs), jnp.sin(freqs))
            q = q * cos * scale + rotate_half(q) * sin * scale
            k = k * cos / scale + rotate_half(k) * sin / scale
            return (q, k)

        def local_attention(q, k, v):
            b, h, n, d = q.shape
            w = n // WINDOW
            bq = q.reshape(b, h, w, WINDOW, d) * QK_SCALE
            bk = k.reshape(b, h, w, WINDOW, d)
            bv = v.reshape(b, h, w, WINDOW, d)

            def look_around(t):
                p = jnp.pad(t, ((0, 0), (0, 0), (1, 0), (0, 0), (0, 0)))
                return jnp.concatenate([p[:, :, :w], p[:, :, 1:]], axis=3)
            bk, bv = (look_around(bk), look_around(bv))
            bt = jnp.arange(n).reshape(w, WINDOW)
            btp = jnp.pad(bt, ((1, 0), (0, 0)), constant_values=-1)
            btk = jnp.concatenate([btp[:w], btp[1:]], axis=1)
            sim = jnp.einsum('bhwid,bhwjd->bhwij', bq, bk)
            i = bt[:, :, None]
            j = btk[:, None, :]
            mask = (i < j) | (i > j + WINDOW) | (j == -1)
            sim = jnp.where(mask, -jnp.finfo(sim.dtype).max, sim)
            attn = jax.nn.softmax(sim, axis=-1)
            out = jnp.einsum('bhwij,bhwjd->bhwid', attn, bv)
            return out.reshape(b, h, n, d)

        def _layer(x, wqkv, qs, ksc, wo, lg, lb, w1, b1, w2, b2):
            b, n, _ = x.shape
            h = shift_token(x)
            qkv = h @ wqkv
            q, k, v = jnp.split(qkv, 3, axis=-1)
            to_heads = lambda t: t.reshape(b, n, HEADS, DIM_HEAD).transpose(0, 2, 1, 3)
            q, k, v = (to_heads(q), to_heads(k), to_heads(v))
            q = l2norm(q) * qs
            k = l2norm(k) * ksc
            q, k = rotary_xpos(q, k)
            o = local_attention(q, k, v)
            o = o.transpose(0, 2, 1, 3).reshape(b, n, INNER)
            x = x + o @ wo
            h = shift_token(x)
            mu = h.mean(-1, keepdims=True)
            var = h.var(-1, keepdims=True)
            h = (h - mu) / jnp.sqrt(var + 1e-05) * lg + lb
            h = h @ w1 + b1
            a, g = jnp.split(h, 2, axis=-1)
            h = a * jax.nn.gelu(g, approximate=False)
            x = x + h @ w2 + b2
            return x
        for l in range(DEPTH):
            x = _layer(x, wqkv[l], q_scale[l], k_scale[l], wo[l], ln_g[l], ln_b[l], w1[l], b1[l], w2[l], b2[l])
        return x
    x = L0_attn_x
    xn = _layernorm(x, axis=-1)
    s = _L0_attn_ref(xn, L0_attn_k1, L0_attn_k2, L0_attn_k3, L0_attn_a1, L0_attn_a2, L0_attn_b1, L0_attn_b2, L0_attn_c, L0_attn_value_weight, L0_attn_output_weight)
    g = _silu(_L0_ffn_ref(xn, L0_ffn_norm_w, L0_ffn_w_macro, L0_ffn_w_micro, L0_ffn_w1, L0_ffn_w2))
    x = x + s * g
    xn = _layernorm(x, axis=-1)
    s = _L1_attn_ref(xn, L1_attn_rby, L1_attn_Wq, L1_attn_bq, L1_attn_Wk, L1_attn_bk, L1_attn_Wv, L1_attn_bv, L1_attn_Wo, L1_attn_bo, L1_attn_ln_gamma, L1_attn_ln_beta)
    g = _silu(_L1_ffn_ref(xn, L1_ffn_wqkv, L1_ffn_q_scale, L1_ffn_k_scale, L1_ffn_wo, L1_ffn_ln_g, L1_ffn_ln_b, L1_ffn_w1, L1_ffn_b1, L1_ffn_w2, L1_ffn_b2))
    x = x + s * g
    return x

_drawn_inputs = setup_inputs


def setup_inputs(seed=0):
    import zlib

    import numpy as np

    out = dict(_drawn_inputs(seed))
    spreads = {'L0_ffn_norm_w': (1.0, 0.2),
     'L1_attn_bq': (0.0, 0.8),
     'L1_attn_bk': (0.0, 2.0),
     'L1_attn_bv': (0.0, 0.8),
     'L1_attn_bo': (0.0, 0.32),
     'L1_attn_ln_gamma': (1.0, 0.2),
     'L1_attn_ln_beta': (0.0, 0.1),
     'L1_ffn_q_scale': (1.0, 0.6),
     'L1_ffn_k_scale': (1.0, 0.6),
     'L1_ffn_ln_g': (1.0, 0.6),
     'L1_ffn_ln_b': (0.0, 0.8),
     'L1_ffn_b1': (0.0, 0.8),
     'L1_ffn_b2': (0.0, 0.8)}
    factors = {'L0_attn_k2': 3.059,
     'L0_attn_k3': 3.014,
     'L0_attn_a1': 8.0,
     'L0_attn_a2': 24.348,
     'L0_attn_b1': 8.0,
     'L0_attn_b2': 8.0,
     'L0_attn_c': 8.0,
     'L1_attn_Wq': 8.0,
     'L1_attn_Wk': 8.0,
     'L1_attn_Wv': 6.906,
     'L1_attn_Wo': 5.688,
     'L1_ffn_wqkv': 4.405,
     'L1_ffn_wo': 4.527,
     'L1_ffn_w1': 8.0,
     'L1_ffn_w2': 8.0}
    for name, (base, spread) in spreads.items():
        noise = np.random.default_rng([zlib.crc32(name.encode()), seed]).standard_normal(out[name].shape)
        drawn = base * np.exp(spread * noise) if base else spread * noise
        out[name] = jnp.asarray(drawn.astype(out[name].dtype))
    for name, factor in factors.items():
        out[name] = (out[name] * factor).astype(out[name].dtype)
    return out
```

```python
from contextlib import ExitStack

import numpy as np
import concourse.bass as bass
from concourse import mybir
from concourse.alu_op_type import AluOpType as ALU

ACT = mybir.ActivationFunctionType
F32 = mybir.dt.float32
BF16 = mybir.dt.bfloat16
I32 = mybir.dt.int32
AX = mybir.AxisListType.X

B, N, W = 4, 1024, 128
P = 128
T = N // P
HALF = 512
H0, A0 = 16, 64
NPOS = 64
HA = H0 * A0
CH = HA // P
E, F = 8, 256
NG, EPG = 4, 2
LOOPS = 2
FC = E * F // P
H1, DK = 16, 8
GH, NGRP = 4, 4
TERMS = 9
KM = 96
MROW = 96
HL, DL, WIN = 8, 64, 64
INNER = HL * DL
HID = W * 4 * 2 // 3
DEPTH = 2
HC = [(c, min(P, HID - c)) for c in range(0, HID, P)]
KEYS = WIN + P
TWO_PI = 2.0 * np.pi
MAGIC = 1.5 * 2.0 ** 23
RSQRT_SEED = float(0x5F3759DF)
PM = 0.1 * float(np.sin(2.0 * np.pi * 0.25))
EPS_ADAPTIVE = 0.1 * float(np.sin(2.0 * np.pi * 0.5))

ENGINES = 4


def build(nc, d, out):
    with ExitStack() as ctx:
        def sb(name, shape, dt=F32):
            return ctx.enter_context(nc.sbuf_tensor(name, shape, dt))

        def sem(name):
            return ctx.enter_context(nc.semaphore(name))

        PS = ctx.enter_context(nc.psum_tensor("PS", [P, 8, HALF], F32))

        def pair(i):
            return PS[:, i:i + 2, :].rearrange("p a n -> p (a n)")

        res = {}
        for name, shape, dt in RESIDENT:
            res[name] = sb(name, [P] + list(shape), dt)
        ident, upper, last_row, ones = res["ident"], res["upper"], res["last_row"], res["ones"]
        shift, shift_in = res["shift"], res["shift_in"]

        identb = sb("identb", [P, P], BF16)
        band = sb("band", [P, 2, KEYS], BF16)

        p1 = sb("p1", [P, T, H0])
        p2e = sb("p2e", [P, T, H0])
        pe_tok = sb("pe_tok", [P, T, W])
        rot_c = sb("rot_c", [P, DEPTH, T, 2, DL])
        rot_s = sb("rot_s", [P, DEPTH, T, 2, DL])
        sc = sb("sc", [P, 16])
        cq, ofac, epsr = sc[:, 0:1], sc[:, 1:2], sc[:, 2:3]
        bqc = sc[:, 4:5]
        gam = sb("gam", [P, W])

        x_in = sb("x_in", [P, T, W])
        xn = sb("xn", [P, T, W])
        s_at = sb("s_at", [P, T, W])
        zz = sb("zz", [P, T, W])
        x1 = sb("x1", [P, T, W])
        xn2 = sb("xn2", [P, T, W])
        tmp = sb("tmp", [P, T, W])
        tmp2 = sb("tmp2", [P, T, W])
        xa, s1, xf = s_at, zz, xn
        xT = sb("xT", [P, N])
        st6 = sb("st6", [P, T, 6])
        mv = sb("mv", [P, T, 2])
        var = sb("var", [P, T])
        nr_y = sb("nr_y", [P, T])
        nr_t = sb("nr_t", [P, T])
        nmr = sb("nmr", [P, T])

        arena = sb("arena", [P, 22528])
        used = [0]

        def take(shape, dt=F32, at=None):
            n = int(np.prod(shape))
            words = n if dt == F32 else (n + 1) // 2
            if at is None:
                at = used[0]
                used[0] += words
            assert at + words <= 22528, (shape, at, words)
            v = arena[:, at:at + words]
            if dt == BF16:
                v = v.bitcast(BF16)
            names = " ".join(f"d{i}" for i in range(len(shape)))
            return v.rearrange(f"p ({names}) -> p {names}", **{f"d{i}": s for i, s in enumerate(shape)})

        nrow = take([N])
        u_a = take([2, N])
        u_k = take([2, N])
        sinb = take([2, N])
        ang = take([T, W // 2])
        ang_k = take([T, W // 2])
        rot_src = take([T, 4, DL])
        p2s = take([T, H0])
        band_f = take([2, KEYS])
        used[0] = 0
        cl = take([T, 48])
        ex = take([T, 48])
        rsum = take([T, H0])
        alpha = take([T, H0])
        den0 = take([T, H0])
        Aw = take([T, H0])
        Bw = take([T, H0])
        cv = take([HA])
        csb = take([2, HA])
        ub = take([2, HA])
        t1 = take([2, HA])
        oT = take([2, CH, P])
        used[0] = 0
        hs = take([4, N])
        ym = take([2, T, W])
        lr = take([T, 12])
        re = take([T, 12])
        rp = take([T, 12])
        rsm = take([T, 5])
        rinv = take([T, 5])
        cmp1 = take([T, NG, NG])
        cmp2 = take([T, NG, NG])
        rank = take([T, NG])
        selw = take([T, NG])
        sw = take([T])
        um = take([T, NG])
        ue = take([T, NG])
        first = take([T, NG])
        comb = take([T, NG, EPG])
        used[0] = 0
        QS = take([2, GH, N], BF16)
        KS = take([2, GH, N], BF16)
        vaug = take([T, H1, 32])
        pb_at = used[0]
        pb = take([8, N])
        at = pb_at
        qkf = take([2, N], F32, at); at += 2 * N
        qkr = take([2, N], F32, at); at += 2 * N
        qk3 = take([2, 3, N], BF16, at)
        on = tmp[:].rearrange("p t w -> p (t w)")
        den_t = tmp2[:].rearrange("p t w -> p (t w)")
        o_t = xT[:]
        mxp = take([2, GH, T, 2])
        mneg = take([2, GH * T])
        mrs = take([2, P])
        msp = take([2, 3, P], BF16)
        used[0] = 0
        qk_a = take([2, 2 * INNER])
        qk_b = take([2, 2 * INNER])
        qk_sq = tmp2[:].rearrange("p t w -> p (t w)")
        ssq = take([2, 2 * HL])
        rq = take([2, 2 * HL])
        rqt = take([2, 2 * HL])
        qT = take([2, 4, P])
        kz = take([HL, WIN + N])
        vl = take([2, HL, DL + 1])
        vp = take([3, HL, DL + 1])
        pl = take([2, 4, KEYS])
        ml = take([2, 4])
        ptA = take([2, 4, P])
        ptB = take([2, 4, P])
        rl = take([2, 4])
        ol = take([2, INNER])
        olT = take([2, 4, P])
        used[0] = 0
        gl = take([2, N])
        hg = take([3, N])

        names = """x_loaded xn_tile xnT_ps xnT lg clipped ex rs den_ps ab v_ps cv u cum_ps csb t1 o oT_ps oT s_ps s
        xr xrT_ps xrT rt rt_read rt_in rt_ex up_ps hs y ym z g0 x1 xn2
        xa xaT_ps xaT q_ps k_ps v1_ps qkf bf1 r1 bf2 bf3 vaug scr_w scr_done qs_loaded mx_ps mx mneg mT_ps msp m_scr m_row
        st_ps p pv on on_moved otn op_ps x2 s1
        sh_ps hcp_v hcp_a hT_ps hT qkv_ps sq rotb rqe qkr kq_ps kq vl_ready s_lps s_max p_sub p_exp pt_ps pt o_lps ol olT_ps olT ol_ps xf
        ffn_tile f_ps g_ps a_ps gl hg y2_ps xb gfin obuf out_done
        cleared dve_step act_step pool_step arrive""".split()
        S = {n: sem(n) for n in names}
        go = sem("go")
        S0 = {n: sem(n) for n in "w_loaded k_loaded dve0 pool0 act0 u_ready sn p_ps p_read2".split()}

        def stepper(eng, s):
            n = [0]

            def link(ins):
                n[0] += 1
                ins.then_inc(s, 1)
                eng.wait_ge(s, n[0])
            return link

        def bc(v, shape, axis):
            return v.unsqueeze(axis).broadcast_to(shape)

        def meet(eng, b):
            eng.drain().then_inc(S["arrive"], 1)
            eng.wait_ge(go, b + 1)

        block = ctx.enter_context(nc.Block())

        @block.sync
        def _(sp):
            for name, _, _ in RESIDENT:
                sp.dma_start(res[name][:], d[name]).then_inc(S0["w_loaded"], 16)
            sp.dma_start(nrow, d["nrow"]).then_inc(S0["k_loaded"], 16)
            sp.dma_start(rot_src, d["rot_src"]).then_inc(S0["k_loaded"], 16)
            sp.dma_start(band_f, d["band"]).then_inc(S0["k_loaded"], 16)

            scr_qk, scr_m = d["scr_qk"], d["scr_m"]
            with sp.Fori(0, B) as b:
                xb_ = d["x"][bass.ds(b, 1)].rearrange("a (t p) w -> p (a t) w", p=P)
                ob_ = out[bass.ds(b, 1)].rearrange("a (t p) w -> p (a t) w", p=P)
                sp.dma_start(x_in[:], xb_).then_inc(S["x_loaded"], 16)
                for qk in range(2):
                    for i in range(3):
                        sp.wait_ge(S["bf%d" % (i + 1)], qk + 1)
                        sp.dma_start(scr_qk[qk, i], qk3[:, qk, i, :]).then_inc(S["scr_w"], 16)
                sp.wait_ge(S["scr_w"], 96)

                def load_group(g):
                    if g >= 2:
                        sp.wait_ge(S["on"], g - 1)
                    for qk, dst in ((0, QS), (1, KS)):
                        for i in range(3):
                            for j in range(3):
                                part = i if qk == 0 else j
                                src = scr_qk[qk, part].rearrange("(h c) n -> c h n", c=DK)
                                row = DK * (3 * i + j)
                                sp.dma_start(dst[row:row + DK, g % 2], src[:, GH * g:GH * g + GH])\
                                    .then_inc(S["qs_loaded"], 16)

                def load_max(g):
                    sp.wait_ge(S["msp"], g + 1)
                    sp.dma_start(scr_m[g % 2].rearrange("i (r c) -> r i c", c=P), msp[0:GH * T, g % 2])\
                        .then_inc(S["m_scr"], 16)
                    sp.wait_ge(S["m_scr"], 16 * (g + 1))
                    sp.dma_start(QS[MROW:MROW + 3, g % 2], scr_m[g % 2].rearrange("i (h n) -> i h n", n=N))\
                        .then_inc(S["m_row"], 16)

                def move_out(g):
                    sp.wait_ge(S["on"], g + 1)
                    for j in range(GH):
                        h = GH * g + j
                        sp.dma_start(o_t[DK * h:DK * h + DK], on[32 * j:32 * j + DK]).then_inc(S["on_moved"], 16)
                        sp.dma_start(den_t[DK * h:DK * h + DK], on[32 * j + DK:32 * j + 2 * DK])\
                            .then_inc(S["on_moved"], 16)

                sp.wait_ge(S["cleared"], 4)
                load_group(0)
                load_max(0)
                load_group(1)
                for g in range(NGRP):
                    if g + 1 < NGRP:
                        load_max(g + 1)
                    move_out(g)
                    if g + 2 < NGRP:
                        load_group(g + 2)
                sp.wait_ge(S["obuf"], 1)
                sp.dma_start(ob_, tmp2[:]).then_inc(S["out_done"], 16)
                sp.wait_ge(S["out_done"], 16)
                sp.wait_ge(S["arrive"], ENGINES)
                for n in names:
                    sp.sem_clear(S[n])
                sp.sem_inc(go, 1)

        @block.gpsimd
        def _(pool):
            with pool.Fori(0, B) as b:
                for l in range(LOOPS):
                    for e in range(E):
                        pool.wait_ge(S["ym"], l * E + e + 1)
                        if l * E + e:
                            pool.wait_ge(S["z"], l * E + e)
                        src = xn if l == 0 and e == 0 else zz
                        pool.tensor_tensor(zz[:], src[:], ym[:, e % 2], ALU.add).then_inc(S["z"], 1)
                pool.wait_ge(S["x1"], 1)
                pool.memset(QS[64:P], 0.0).then_inc(S["cleared"], 1)
                pool.wait_ge(S["cleared"], 1)
                pool.memset(KS[64:96], 0.0).then_inc(S["cleared"], 1)
                pool.wait_ge(S["cleared"], 2)
                pool.memset(KS[96:P], 1.0).then_inc(S["cleared"], 1)
                pool.wait_ge(S["cleared"], 3)
                pool.memset(vaug[:, :, :, DK:32], 1.0).then_inc(S["cleared"], 1)
                pool.wait_ge(S["cleared"], 4)
                pool.wait_ge(S["s1"], 1)
                pool.memset(vp[0:WIN, 2, :, 0:DL], 0.0).then_inc(S["cleared"], 1)
                pool.wait_ge(S["cleared"], 5)
                pool.memset(vl[:, :, :, DL:DL + 1], 1.0).then_inc(S["cleared"], 1)
                pool.wait_ge(S["cleared"], 6)
                pool.memset(vp[:, :, :, DL:DL + 1], 1.0).then_inc(S["cleared"], 1)
                pool.wait_ge(S["cleared"], 7)
                pool.memset(kz, 0.0).then_inc(S["cleared"], 1)
                pool.wait_ge(S["cleared"], 8)
                for l in range(DEPTH):
                    for t in range(T):
                        u = l * T + t
                        pool.wait_ge(S["rotb"], u + 1)
                        pool.tensor_tensor(qk_a[:, u % 2], qk_a[:, u % 2], qk_b[:, u % 2], ALU.add)\
                            .then_inc(S["pool_step"], 1)
                        pool.wait_ge(S["pool_step"], u + 1)
                        pool.wait_ge(S["rqe"], u + 1)
                        v = qk_a[:, u % 2].rearrange("p (h c) -> p h c", c=DL)
                        pool.tensor_tensor(v, v, bc(rq[:, u % 2], [P, 2 * HL, DL], 2), ALU.mult)\
                            .then_inc(S["qkr"], 1)
                    pool.wait_ge(S["xf"], (2 * l + 1) * T)
                    pool.wait_ge(S["hT"], 4 * l + 4)
                    pool.tensor_tensor(tmp2[:], xf[:], bc(res["b2f"][:, l], [P, T, W], 1), ALU.add)\
                        .then_inc(S["xb"], 1)
                meet(pool, b)

        @block.scalar
        def _(act):
            act.wait_ge(S0["dve0"], 1)
            for i in range(2):
                for c in range(CH):
                    n = i * CH + c
                    act.wait_ge(S0["u_ready"], n + 1)
                    if n >= 2:
                        act.wait_ge(S0["p_ps"], n - 1)
                    act.activation(sinb[:, n % 2], u_a[:, n % 2], ACT.Sin, scale=6.283185).then_inc(S0["sn"], 1)
            act.wait_ge(S0["u_ready"], 2 * CH + 1)
            act.activation(pe_tok.rearrange("p t (f s) -> p t f s", s=2)[:, :, :, 0], ang, ACT.Sin)\
                .then_inc(S0["act0"], 1)
            act.activation(pe_tok.rearrange("p t (f s) -> p t f s", s=2)[:, :, :, 1], ang_k, ACT.Sin)\
                .then_inc(S0["act0"], 1)
            act.wait_ge(S0["p_read2"], 1)
            act.activation(p2e[:], p2s, ACT.Exp).then_inc(S0["act0"], 1)
            act.wait_ge(S0["act0"], 3)

            with act.Fori(0, B) as b:
                link = stepper(act, S["act_step"])

                for i in range(2):
                    act.wait_ge(S["xnT_ps"], 4 * i + 4)
                    act.copy(xT[:, i * HALF:i * HALF + HALF], PS[:, i, :]).then_inc(S["xnT"], 1)
                act.wait_ge(S["clipped"], 1)
                act.activation(ex, cl, ACT.Exp).then_inc(S["ex"], 1)
                for t in range(T + 1):
                    if t < T:
                        act.wait_ge(S["cum_ps"], t + 1)
                        if t >= 2:
                            act.wait_ge(S["t1"], t - 1)
                        act.copy(csb[:, t % 2], pair(2 * (t % 2))).then_inc(S["csb"], 1)
                    if t >= 1:
                        k = t - 1
                        for hf in range(2):
                            act.wait_ge(S["oT_ps"], 2 * k + hf + 1)
                            if k >= 2 and hf == 0:
                                act.wait_ge(S["s_ps"], k - 1)
                            act.copy(oT[:, k % 2, 4 * hf:4 * hf + 4, :].rearrange("p c n -> p (c n)"), PS[:, 6, :])\
                                .then_inc(S["oT"], 1)
                        act.wait_ge(S["s_ps"], k + 1)
                        act.copy(s_at[:, k, :], PS[:, 7, 0:W]).then_inc(S["s"], 1)
                for l in range(LOOPS):
                    for i in range(2):
                        act.wait_ge(S["xrT_ps"], 8 * l + 4 * i + 4)
                        act.activation(xT[:, i * HALF:i * HALF + HALF], PS[:, i, :], ACT.Identity,
                                       scale=res["norm_w"][:, 0:1]).then_inc(S["xrT"], 1)
                    act.wait_ge(S["rt_in"], l + 1)
                    act.activation(re, re, ACT.Exp).then_inc(S["rt_ex"], 1)
                    for c in range(FC):
                        n = l * FC + c
                        act.wait_ge(S["up_ps"], n + 1)
                        if n >= 4:
                            act.wait_ge(S["y"], n // 2 - 1)
                        act.activation(hs[:, c % 4], pair(2 * (c % 2)), ACT.Silu).then_inc(S["hs"], 1)
                act.wait_ge(S["z"], LOOPS * E)
                act.activation(tmp[:], zz[:], ACT.Silu).then_inc(S["g0"], 1)
                for i in range(2):
                    act.wait_ge(S["xaT_ps"], 4 * i + 4)
                    act.copy(xT[:, i * HALF:i * HALF + HALF], PS[:, i, :]).then_inc(S["xaT"], 1)
                for qk in range(2):
                    act.wait_ge(S["q_ps" if qk == 0 else "k_ps"], 1)
                    if qk == 0:
                        act.activation(qkf[:, 0], pair(2), ACT.Identity, bias=bqc, scale=cq).then_inc(S["qkf"], 1)
                    else:
                        act.activation(qkf[:, 1], pair(4), ACT.Identity, bias=res["bk"][:, 0:1]).then_inc(S["qkf"], 1)
                for qk in range(2):
                    act.wait_ge(S["qkf"], qk + 1)
                    act.copy(qk3[:, qk, 0], qkf[:, qk]).then_inc(S["bf1"], 1)
                for qk in range(2):
                    act.wait_ge(S["r1"], qk + 1)
                    act.copy(qk3[:, qk, 1], qkr[:, qk]).then_inc(S["bf2"], 1)
                act.wait_ge(S["scr_w"], 96)
                for g in range(NGRP):
                    for kt in range(T):
                        for j in range(GH):
                            n = (g * T + kt) * GH + j
                            act.wait_ge(S["st_ps"], n + 1)
                            if n >= 8:
                                act.wait_ge(S["pv"], n // GH - 1)
                            act.activation(pb[:, n % 8], pair(2 * (n % 2)), ACT.Exp).then_inc(S["p"], 1)
                    act.wait_ge(S["pv"], (g + 1) * T)
                    if g:
                        act.wait_ge(S["on_moved"], 128 * g)
                    act.copy(on, pair(4)).then_inc(S["on"], 1)
                act.wait_ge(S["s1"], 1)
                for l in range(DEPTH):
                    src = xn2 if l == 0 else xf
                    if l:
                        act.wait_ge(S["xf"], 2 * T * l)
                    act.copy(tmp[:, :, 0:64], src[:, :, 0:64]).then_inc(S["hcp_a"], 1)
                    for i in range(2):
                        act.wait_ge(S["hT_ps"], 16 * l + 4 * i + 4)
                        act.copy(xT[:, i * HALF:i * HALF + HALF], PS[:, 1 + i, :]).then_inc(S["hT"], 1)

                    def qkv(t):
                        u = l * T + t
                        act.wait_ge(S["qkv_ps"], u + 1)
                        act.wait_ge(S["rotb"], u + 1)
                        act.activation(qk_sq, pair(0), ACT.Square).then_inc(S["sq"], 1)
                        if u >= 2:
                            act.wait_ge(S["o_lps"], 2 * u - 2)
                        act.copy(vl[:, u % 2, :, 0:DL], PS[:, 2, :].rearrange("p (h c) -> p h c", c=DL))\
                            .then_inc(S["vl_ready"], 1)
                        act.copy(vp[0:WIN, u % 3, :, 0:DL], PS[WIN:P, 2, :].rearrange("p (h c) -> p h c", c=DL))\
                            .then_inc(S["vl_ready"], 1)

                    def kq(t):
                        u = l * T + t
                        act.wait_ge(S["kq_ps"], 2 * u + 1)
                        if u >= 2:
                            act.wait_ge(S["s_lps"], 2 * u - 2)
                        act.copy(qT[:, u % 2], PS[:, 3, :].rearrange("p (c n) -> p c n", c=4)).then_inc(S["kq"], 1)
                        act.wait_ge(S["kq_ps"], 2 * u + 2)
                        for r in range(2):
                            act.copy(kz.rearrange("p (c r) n -> p r c n", r=2)[64 * r:64 * r + 64, r, :,
                                                                               WIN + P * t:WIN + P * t + P],
                                     PS[64 * r:64 * r + 64, 3, :].rearrange("p (c n) -> p c n", c=4))\
                                .then_inc(S["kq"], 1)

                    act.wait_ge(S["cleared"], 8)
                    qkv(0)
                    kq(0)
                    for u in range(2 * T):
                        t, hf = u // 2, u % 2
                        n = 2 * T * l + u
                        if hf == 0 and t + 1 < T:
                            qkv(t + 1)
                        if hf == 1 and t + 1 < T:
                            kq(t + 1)
                        act.wait_ge(S["p_sub"], n + 1)
                        act.activation(pl[:, n % 2], pl[:, n % 2], ACT.Exp).then_inc(S["p_exp"], 1)
                        if n >= 2:
                            act.wait_ge(S["o_lps"], n - 1)
                        act.wait_ge(S["pt_ps"], 2 * n + 1)
                        act.copy(ptA[0:WIN, n % 2], PS[0:WIN, 6, :].rearrange("p (c n) -> p c n", c=4))\
                            .then_inc(S["pt"], 1)
                        act.wait_ge(S["pt_ps"], 2 * n + 2)
                        act.copy(ptB[:, n % 2], PS[:, 6, :].rearrange("p (c n) -> p c n", c=4)).then_inc(S["pt"], 1)
                        if hf == 1:
                            q = l * T + t
                            act.wait_ge(S["olT_ps"], q + 1)
                            act.copy(olT[:, q % 2], PS[:, 6, :].rearrange("p (c n) -> p c n", c=4))\
                                .then_inc(S["olT"], 1)
                    act.wait_ge(S["xf"], (2 * l + 1) * T)
                    act.wait_ge(S["hT_ps"], 16 * l + 8)
                    act.copy(tmp[:, :, 0:64], xf[:, :, 0:64]).then_inc(S["hcp_a"], 1)
                    for i in range(2):
                        act.wait_ge(S["hT_ps"], 16 * l + 8 + 4 * i + 4)
                        act.activation(xT[:, i * HALF:i * HALF + HALF], PS[:, 1 + i, :], ACT.Identity,
                                       bias=res["ln_b"][:, l:l + 1], scale=res["ln_g"][:, l:l + 1])\
                            .then_inc(S["hT"], 1)
                    for i, (c, m) in enumerate(HC):
                        n = l * 3 + i
                        act.wait_ge(S["g_ps"], n + 1)
                        if n >= 2:
                            act.wait_ge(S["hg"], n - 1)
                        act.activation(gl[0:m, n % 2], PS[0:m, 3:5, :].rearrange("p a n -> p (a n)"), ACT.Gelu,
                                       bias=res["b1g"][0:m, l * 3 + i:l * 3 + i + 1]).then_inc(S["gl"], 1)
                act.wait_ge(S["xf"], 2 * T * DEPTH)
                act.activation(tmp[:], xf[:], ACT.Silu).then_inc(S["gfin"], 1)
                meet(act, b)

        @block.vector
        def _(dve):
            dve.memset(sc[:], 0.0).then_inc(S0["dve0"], 1)
            dve.wait_ge(S0["dve0"], 1)
            dve.wait_ge(S0["w_loaded"], 16 * len(RESIDENT))
            dve.wait_ge(S0["k_loaded"], 48)
            k0 = [1]

            def link(ins):
                k0[0] += 1
                ins.then_inc(S0["dve0"], 1)
                dve.wait_ge(S0["dve0"], k0[0])

            link(dve.tensor_copy(identb[:], ident[:]))
            link(dve.tensor_copy(band[:], band_f))
            pa = res["pos_ab"]
            link(dve.tensor_scalar(pa[:], pa[:], 1.0 / TWO_PI, None, ALU.mult))
            for i in range(2):
                for c in range(CH):
                    n = i * CH + c
                    if n >= 2:
                        dve.wait_ge(S0["sn"], n - 1)
                    a, o = pa[:, 2 * i, c:c + 1], pa[:, 2 * i + 1, c:c + 1]
                    link(dve.tensor_scalar(u_a[:, n % 2], nrow, a, o, ALU.mult, ALU.add))
                    link(dve.tensor_scalar(u_k[:, n % 2], u_a[:, n % 2], MAGIC, MAGIC, ALU.add, ALU.subtract))
                    dve.tensor_tensor(u_a[:, n % 2], u_a[:, n % 2], u_k[:, n % 2], ALU.subtract)\
                        .then_inc(S0["u_ready"], 1)
            rby = res["rby"]
            link(dve.tensor_scalar(sc[:, 5:6], rby[:, 2:3], PM, 1.0, ALU.mult, ALU.add))
            link(dve.tensor_scalar(res["pe_base"][:], res["pe_base"][:], sc[:, 5:6], None, ALU.mult))
            link(dve.reciprocal(res["pe_base"][:], res["pe_base"][:]))
            link(dve.tensor_tensor(ang, bc(res["pos"][:], [P, T, W // 2], 2), bc(res["pe_base"][:], [P, T, W // 2], 1),
                                   ALU.mult))
            link(dve.tensor_scalar(ang_k, ang, 1.0 / TWO_PI, MAGIC, ALU.mult, ALU.add))
            link(dve.tensor_scalar(ang_k, ang_k, MAGIC, None, ALU.subtract))
            link(dve.scalar_tensor_tensor(ang, ang_k, -6.28125, ang, ALU.mult, ALU.add))
            link(dve.scalar_tensor_tensor(ang, ang_k, -(TWO_PI - 6.28125), ang, ALU.mult, ALU.add))
            link(dve.tensor_scalar(ang, ang, 3.1415925, -3.1415925, ALU.min, ALU.max))
            link(dve.tensor_scalar(ang_k, ang, -1.0, None, ALU.mult))
            link(dve.tensor_tensor(ang_k, ang_k, ang, ALU.min))
            dve.tensor_scalar(ang_k, ang_k, float(np.pi / 2), None, ALU.add).then_inc(S0["u_ready"], 1)
            link(dve.tensor_scalar(sc[:, 6:7], rby[:, 0:1], 0.1, 1.0, ALU.mult, ALU.add))
            link(dve.tensor_scalar(sc[:, 7:8], rby[:, 1:2], 0.05, None, ALU.mult))
            link(dve.tensor_tensor(sc[:, 8:9], sc[:, 6:7], sc[:, 7:8], ALU.add))
            link(dve.tensor_scalar(sc[:, 9:10], rby[:, 2:3], 0.15, None, ALU.mult))
            link(dve.tensor_tensor(sc[:, 8:9], sc[:, 8:9], sc[:, 9:10], ALU.add))
            link(dve.tensor_scalar(cq, sc[:, 8:9], 1.0 / float(np.sqrt(DK)), None, ALU.mult))
            link(dve.tensor_scalar(bqc, res["bq"][:, 0:1], cq, None, ALU.mult))
            link(dve.tensor_scalar(ofac, rby[:, 2:3], EPS_ADAPTIVE, 1.0, ALU.mult, ALU.add))
            link(dve.tensor_scalar(epsr, rby[:, 1:2], 0.1, 1.0, ALU.mult, ALU.add))
            link(dve.tensor_scalar(epsr, epsr, 1e-5, None, ALU.mult))
            link(dve.tensor_scalar(sc[:, 10:11], rby[:, 2:3], 0.05, None, ALU.mult))
            link(dve.tensor_tensor(sc[:, 10:11], sc[:, 10:11], sc[:, 6:7], ALU.add))
            link(dve.tensor_scalar(gam[:], res["ln_gamma"][:], sc[:, 10:11], None, ALU.mult))
            for l in range(DEPTH):
                for qk in range(2):
                    link(dve.tensor_tensor(rot_c[:, l, :, qk], rot_src[:, :, 2 * qk],
                                           bc(res["qk_scale"][:, l, qk, 0], [P, T, DL], 1), ALU.mult))
                    link(dve.tensor_tensor(rot_s[:, l, :, qk], rot_src[:, :, 2 * qk + 1],
                                           bc(res["qk_scale"][:, l, qk, 1], [P, T, DL], 1), ALU.mult))
            dve.wait_ge(S0["p_ps"], 2 * CH)
            link(dve.tensor_copy(p1.rearrange("p t h -> p (t h)"), PS[:, 0, 0:T * H0]))
            dve.tensor_scalar(p2s.rearrange("p t h -> p (t h)"), PS[:, 1, 0:T * H0], 20.0, -20.0, ALU.min, ALU.max)\
                .then_inc(S0["p_read2"], 1)
            dve.wait_ge(S0["act0"], 3)

            with dve.Fori(0, B) as b:
                link = stepper(dve, S["dve_step"])

                def rsqrt(v, y, t_, steps=3):
                    link(dve.tensor_scalar(t_.bitcast(I32), v.bitcast(I32), 1, None, ALU.logical_shift_right))
                    link(dve.tensor_scalar(y.bitcast(I32), t_.bitcast(I32), -1.0, RSQRT_SEED, ALU.mult, ALU.add))
                    for _ in range(steps):
                        link(dve.scalar_tensor_tensor(t_, y, -0.5, y, ALU.mult, ALU.mult))
                        link(dve.tensor_tensor(t_, t_, v, ALU.mult))
                        link(dve.scalar_tensor_tensor(y, t_, 1.5, y, ALU.add, ALU.mult))

                def layer_norm(src, dst, eps, done):
                    for t in range(T):
                        ins = dve.bn_stats(st6[:, t], src[:, t])
                    link(ins)
                    for t in range(T):
                        ins = dve.bn_aggr(mv[:, t], st6[:, t])
                    link(ins)
                    link(dve.tensor_scalar(var[:], mv[:, :, 1], eps, None, ALU.add))
                    rsqrt(var[:], nr_y[:], nr_t[:])
                    link(dve.scalar_tensor_tensor(nmr[:], mv[:, :, 0], -1.0, nr_y[:], ALU.mult, ALU.mult))
                    for t in range(T):
                        dve.tensor_scalar(dst[:, t], src[:, t], nr_y[:, t:t + 1], nmr[:, t:t + 1],
                                          ALU.mult, ALU.add).then_inc(S[done], 1)

                dve.wait_ge(S["x_loaded"], 16)
                layer_norm(x_in, xn, 1e-5, "xn_tile")

                dve.wait_ge(S["lg"], 1)
                lg = PS[:, 2, 0:T * 48].rearrange("p (t c) -> p t c", c=48)
                link(dve.tensor_tensor(cl[:, :, 0:16], lg[:, :, 0:16], p1[:], ALU.add))
                link(dve.tensor_scalar(cl[:, :, 16:48], lg[:, :, 16:48], 20.0, -20.0, ALU.min, ALU.max))
                dve.tensor_scalar(cl[:, :, 0:16], cl[:, :, 0:16], 20.0, -20.0, ALU.min, ALU.max)\
                    .then_inc(S["clipped"], 1)
                dve.wait_ge(S["ex"], 1)
                cross, diag, extra = ex[:, :, 0:16], ex[:, :, 16:32], ex[:, :, 32:48]
                link(dve.memset(rsum[:, 0], 0.0))
                for t in range(T - 1):
                    ins = dve.tensor_tensor(rsum[:, t + 1], rsum[:, t], cross[:, t], ALU.add)
                    if t < T - 2:
                        link(ins)
                ins.then_inc(S["rs"], 1)
                link(dve.tensor_tensor(alpha, p2e[:], extra, ALU.mult))
                dve.wait_ge(S["den_ps"], 1)
                link(dve.tensor_tensor(den0, PS[:, 3, 0:T * H0].rearrange("p (t h) -> p t h", h=H0), alpha, ALU.mult))
                link(dve.tensor_tensor(den0, den0, diag, ALU.add))
                link(dve.reciprocal(den0, den0))
                link(dve.tensor_tensor(Aw, alpha, den0, ALU.mult))
                dve.tensor_tensor(Bw, diag, den0, ALU.mult).then_inc(S["ab"], 1)
                dve.wait_ge(S["ab"], 1)

                def heads(v):
                    return v.rearrange("p (h a) -> p h a", a=A0)
                full = [P, H0, A0]
                for t in range(T + 1):
                    if t < T:
                        dve.wait_ge(S["v_ps"], t + 1)
                        if t >= 1:
                            dve.wait_ge(S["cum_ps"], t)
                        dve.tensor_tensor(heads(cv), heads(pair(4)), bc(cross[:, t], full, 2), ALU.mult)\
                            .then_inc(S["cv"], 1)
                        dve.tensor_tensor(heads(ub[:, t % 2]), heads(pair(4)), bc(Bw[:, t], full, 2), ALU.mult)\
                            .then_inc(S["u"], 1)
                    if t >= 1:
                        k = t - 1
                        dve.wait_ge(S["csb"], k + 1)
                        if k >= 2:
                            dve.wait_ge(S["oT_ps"], 2 * k - 2)
                        dve.tensor_tensor(heads(t1[:, k % 2]), heads(csb[:, k % 2]), bc(Aw[:, k], full, 2), ALU.mult)\
                            .then_inc(S["t1"], 1)
                        dve.wait_ge(S["t1"], k + 1)
                        dve.wait_ge(S["u"], k + 1)
                        dve.tensor_tensor(t1[:, k % 2], t1[:, k % 2], ub[:, k % 2], ALU.add).then_inc(S["o"], 1)
                        dve.wait_ge(S["o"], k + 1)

                for l in range(LOOPS):
                    zs = xn if l == 0 else zz
                    if l:
                        dve.wait_ge(S["z"], E * l)
                    else:
                        dve.wait_ge(S["s"], T)
                    for t in range(T):
                        ins = dve.tensor_tensor_reduce(tmp[:, t], zs[:, t], zs[:, t], 1.0, 0.0, ALU.mult, ALU.add,
                                                       var[:, t:t + 1])
                    link(ins)
                    link(dve.tensor_scalar(var[:], var[:], 1.0 / W, 1e-6, ALU.mult, ALU.add))
                    rsqrt(var[:], nr_y[:], nr_t[:])
                    for t in range(T):
                        dve.tensor_scalar(tmp2[:, t], zs[:, t], nr_y[:, t:t + 1], None, ALU.mult)\
                            .then_inc(S["xr"], 1)
                    dve.wait_ge(S["rt"], l + 1)
                    dve.tensor_copy(lr.rearrange("p t c -> p (t c)"), PS[:, 2, 0:T * 12]).then_inc(S["rt_read"], 1)
                    dve.wait_ge(S["rt_read"], l + 1)
                    mac, mic = lr[:, :, 0:NG], lr[:, :, NG:12].rearrange("p t (g e) -> p t g e", e=EPG)
                    emac, emic = re[:, :, 0:NG], re[:, :, NG:12].rearrange("p t (g e) -> p t g e", e=EPG)
                    pmac, pmic = rp[:, :, 0:NG], rp[:, :, NG:12].rearrange("p t (g e) -> p t g e", e=EPG)
                    link(dve.tensor_reduce(rsm[:, :, 0], mac, AX, ALU.max))
                    link(dve.tensor_reduce(rsm[:, :, 1:5], mic, AX, ALU.max))
                    link(dve.tensor_tensor(emac, mac, bc(rsm[:, :, 0], [P, T, NG], 2), ALU.subtract))
                    dve.tensor_tensor(emic, mic, bc(rsm[:, :, 1:5], [P, T, NG, EPG], 3), ALU.subtract)\
                        .then_inc(S["rt_in"], 1)
                    dve.wait_ge(S["rt_ex"], l + 1)
                    link(dve.tensor_reduce(rsm[:, :, 0], emac, AX, ALU.add))
                    link(dve.tensor_reduce(rsm[:, :, 1:5], emic, AX, ALU.add))
                    link(dve.reciprocal(rinv, rsm))
                    link(dve.tensor_tensor(pmac, emac, bc(rinv[:, :, 0], [P, T, NG], 2), ALU.mult))
                    link(dve.tensor_tensor(pmic, emic, bc(rinv[:, :, 1:5], [P, T, NG, EPG], 3), ALU.mult))
                    sq4 = [P, T, NG, NG]
                    link(dve.tensor_tensor(cmp1, bc(pmac, sq4, 2), bc(pmac, sq4, 3), ALU.is_gt))
                    link(dve.tensor_tensor(cmp2, bc(pmac, sq4, 2), bc(pmac, sq4, 3), ALU.is_equal))
                    link(dve.tensor_tensor(cmp2, cmp2, bc(res["before"][:], sq4, 1), ALU.mult))
                    link(dve.tensor_tensor(cmp1, cmp1, cmp2, ALU.add))
                    link(dve.tensor_reduce(rank, cmp1, AX, ALU.add))
                    link(dve.tensor_scalar(rank, rank, 2.0, None, ALU.is_lt))
                    link(dve.tensor_tensor(selw, pmac, rank, ALU.mult))
                    link(dve.tensor_reduce(sw, selw, AX, ALU.add))
                    link(dve.tensor_scalar(sw, sw, 1e-9, None, ALU.add))
                    link(dve.reciprocal(sw, sw))
                    link(dve.tensor_tensor(selw, selw, bc(sw, [P, T, NG], 2), ALU.mult))
                    link(dve.tensor_reduce(um, pmic, AX, ALU.max))
                    link(dve.tensor_scalar(ue, um, 1e-9, None, ALU.add))
                    link(dve.reciprocal(ue, ue))
                    link(dve.tensor_tensor(um, um, ue, ALU.mult))
                    link(dve.tensor_tensor(selw, selw, um, ALU.mult))
                    link(dve.tensor_tensor(first, pmic[:, :, :, 0], pmic[:, :, :, 1], ALU.is_ge))
                    link(dve.tensor_tensor(comb[:, :, :, 0], selw, first, ALU.mult))
                    link(dve.tensor_tensor(comb[:, :, :, 1], selw, comb[:, :, :, 0], ALU.subtract))
                    for e in range(E):
                        n = l * E + e
                        dve.wait_ge(S["y"], n + 1)
                        if n >= 2:
                            dve.wait_ge(S["z"], n - 1)
                        dve.tensor_tensor(ym[:, e % 2], pair(4 + 2 * (e % 2)).rearrange("p (t w) -> p t w", w=W),
                                          bc(comb[:, :, e // EPG, e % EPG], [P, T, W], 2), ALU.mult)\
                            .then_inc(S["ym"], 1)

                dve.wait_ge(S["g0"], 1)
                link(dve.tensor_tensor(tmp[:], tmp[:], s_at[:], ALU.mult))
                dve.tensor_tensor(x1[:], x_in[:], tmp[:], ALU.add).then_inc(S["x1"], 1)
                dve.wait_ge(S["x1"], 1)
                layer_norm(x1, xn2, 1e-5, "xn2")
                dve.wait_ge(S["xn2"], T)

                dve.tensor_tensor(xa[:], xn2[:], pe_tok[:], ALU.add).then_inc(S["xa"], 1)
                for qk in range(2):
                    dve.wait_ge(S["bf1"], qk + 1)
                    dve.tensor_tensor(qkr[:, qk], qkf[:, qk], qk3[:, qk, 0], ALU.subtract).then_inc(S["r1"], 1)
                for i in range(2):
                    dve.wait_ge(S["v1_ps"], 1)
                    dve.wait_ge(S["cleared"], 4)
                    dve.tensor_tensor(vaug[:, 4 * i:4 * i + 4, :, 0:DK],
                                      PS[:, 6 + i, :].rearrange("p (t h c) -> p t h c", t=4, c=DK),
                                      bc(res["bv"].rearrange("p (h c) -> p h c", c=DK), [P, 4, H1, DK], 1), ALU.add)\
                        .then_inc(S["vaug"], 1)
                for qk in range(2):
                    dve.wait_ge(S["bf2"], qk + 1)
                    dve.tensor_tensor(qk3[:, qk, 2], qkr[:, qk], qk3[:, qk, 1], ALU.subtract).then_inc(S["bf3"], 1)
                for g in range(NGRP):
                    for n in range(GH * T * 2):
                        j, t, hf = n // (2 * T), n // 2 % T, n % 2
                        dve.wait_ge(S["mx_ps"], g * 64 + n + 1)
                        dve.tensor_reduce(mxp[:, g % 2, j, t, hf:hf + 1], PS[:, 6 + n % 2, :], AX, ALU.max)\
                            .then_inc(S["mx"], 1)
                    dve.wait_ge(S["mx"], (g + 1) * 64)
                    link(dve.tensor_reduce(mneg[:, g % 2], mxp[:, g % 2].rearrange("p j t f -> p (j t) f"),
                                           AX, ALU.max))
                    dve.tensor_scalar(mneg[:, g % 2], mneg[:, g % 2], -1.0, None, ALU.mult).then_inc(S["mneg"], 1)
                    dve.wait_ge(S["mT_ps"], g + 1)
                    if g >= 2:
                        dve.wait_ge(S["m_scr"], 16 * (g - 1))
                    rows = slice(0, GH * T)
                    link(dve.tensor_copy(mrs[rows, 0], PS[rows, 6, 0:P]))
                    link(dve.tensor_copy(msp[rows, g % 2, 0], mrs[rows, 0]))
                    link(dve.tensor_tensor(mrs[rows, 1], mrs[rows, 0], msp[rows, g % 2, 0], ALU.subtract))
                    link(dve.tensor_copy(msp[rows, g % 2, 1], mrs[rows, 1]))
                    dve.tensor_tensor(msp[rows, g % 2, 2], mrs[rows, 1], msp[rows, g % 2, 1], ALU.subtract)\
                        .then_inc(S["msp"], 1)
                dve.wait_ge(S["msp"], NGRP)
                dve.wait_ge(S["on_moved"], 128 * NGRP)
                link(dve.reciprocal(den_t, den_t))
                dve.scalar_tensor_tensor(o_t, o_t, ofac, den_t, ALU.mult, ALU.mult).then_inc(S["otn"], 1)
                dve.wait_ge(S["op_ps"], 1)
                link(dve.tensor_tensor(tmp.rearrange("p t w -> p (t w)"), pair(0), xa.rearrange("p t w -> p (t w)"),
                                       ALU.add))
                link(dve.tensor_tensor(tmp[:], tmp[:], bc(res["bo"][:], [P, T, W], 1), ALU.add))
                layer_norm(tmp, tmp2, epsr, "x2")
                dve.wait_ge(S["x2"], T)
                link(dve.tensor_tensor(tmp2[:], tmp2[:], bc(gam[:], [P, T, W], 1), ALU.mult))
                dve.tensor_tensor(s1[:], tmp2[:], bc(res["ln_beta"][:], [P, T, W], 1), ALU.add).then_inc(S["s1"], 1)
                dve.wait_ge(S["s1"], 1)

                for l in range(DEPTH):
                    xs = xn2 if l == 0 else xf
                    dve.wait_ge(S["sh_ps"], 2 * l + 1)
                    dve.tensor_copy(tmp[:, :, 64:W], PS[:, 0, :].rearrange("p (t c) -> p t c", c=64))\
                        .then_inc(S["hcp_v"], 1)

                    def rotate(t):
                        u = l * T + t
                        dve.wait_ge(S["qkv_ps"], u + 1)
                        if u >= 2:
                            dve.wait_ge(S["kq_ps"], 2 * u - 2)
                        qk_ps = pair(0)
                        shape = [P, 2, HL, DL]
                        dve.tensor_tensor(qk_a[:, u % 2].rearrange("p (q h c) -> p q h c", q=2, c=DL),
                                          qk_ps.rearrange("p (q h c) -> p q h c", q=2, c=DL),
                                          bc(rot_c[:, l, t], shape, 2), ALU.mult)
                        for hf in range(2):
                            o = qk_b[:, u % 2].rearrange("p (q h f c) -> p q h f c", q=2, h=HL, f=2)[:, :, :, hf]
                            v = qk_ps.rearrange("p (q h f c) -> p q h f c", q=2, h=HL, f=2)[:, :, :, 1 - hf]
                            w = rot_s[:, l, t].rearrange("p q (f c) -> p q f c", f=2)[:, :, hf]
                            ins = dve.tensor_tensor(o, v, bc(w, [P, 2, HL, DL // 2], 2), ALU.mult)
                        ins.then_inc(S["rotb"], 1)

                    def norms(t):
                        u = l * T + t
                        dve.wait_ge(S["sq"], u + 1)
                        link(dve.tensor_reduce(ssq[:, u % 2], qk_sq.rearrange("p (h c) -> p h c", c=DL), AX, ALU.add))
                        link(dve.tensor_scalar(ssq[:, u % 2], ssq[:, u % 2], 1e-24, None, ALU.max))
                        rsqrt(ssq[:, u % 2], rq[:, u % 2], rqt[:, u % 2])
                        dve.tensor_scalar(rq[:, u % 2, 0:HL], rq[:, u % 2, 0:HL], 8.0, None, ALU.mult)\
                            .then_inc(S["rqe"], 1)

                    rotate(0)
                    norms(0)
                    for u in range(2 * T):
                        t, hf = u // 2, u % 2
                        n = 2 * T * l + u
                        if hf == 0 and t + 1 < T:
                            rotate(t + 1)
                            norms(t + 1)
                        sv = PS[:, 4:6, 0:2 * KEYS].rearrange("p a (h c) -> p a h c", h=2)
                        plv = pl[:, n % 2].rearrange("p (a h) c -> p a h c", a=2)
                        dve.wait_ge(S["s_lps"], n + 1)
                        if n >= 2:
                            dve.wait_ge(S["pt_ps"], 2 * n - 2)
                        link(dve.tensor_reduce(ml[:, n % 2].rearrange("p (a h) -> p a h", a=2), sv, AX, ALU.max))
                        for a in range(2):
                            ins = dve.tensor_tensor(plv[:, a], sv[:, a],
                                                    bc(ml[:, n % 2, 2 * a:2 * a + 2], [P, 2, KEYS], 2), ALU.subtract)
                            if a == 0:
                                link(ins)
                        ins.then_inc(S["p_sub"], 1)
                        dve.wait_ge(S["o_lps"], n + 1)
                        ov = PS[:, 7, 0:4 * (DL + 1)].rearrange("p (h c) -> p h c", c=DL + 1)
                        link(dve.reciprocal(rl[:, n % 2], ov[:, :, DL]))
                        q = l * T + t
                        if q >= 2:
                            dve.wait_ge(S["olT_ps"], q - 1)
                        dve.tensor_tensor(ol[:, q % 2, 256 * hf:256 * hf + 256].rearrange("p (h c) -> p h c", c=DL),
                                          ov[:, :, 0:DL], bc(rl[:, n % 2], [P, 4, DL], 2), ALU.mult)\
                            .then_inc(S["ol"], 1)
                        if hf == 1:
                            dve.wait_ge(S["ol_ps"], q + 1)
                            dve.tensor_tensor(xf[:, t], xs[:, t], PS[:, 7, 0:W], ALU.add).then_inc(S["xf"], 1)
                    dve.wait_ge(S["sh_ps"], 2 * l + 2)
                    dve.tensor_copy(tmp[:, :, 64:W], PS[:, 0, :].rearrange("p (t c) -> p t c", c=64))\
                        .then_inc(S["hcp_v"], 1)
                    dve.wait_ge(S["hcp_v"], 2 * l + 2)
                    dve.wait_ge(S["hcp_a"], 2 * l + 2)
                    layer_norm(tmp, s_at, 1e-5, "ffn_tile")
                    for i, (c, m) in enumerate(HC):
                        n = l * 3 + i
                        dve.wait_ge(S["gl"], n + 1)
                        dve.wait_ge(S["a_ps"], n + 1)
                        dve.scalar_tensor_tensor(hg[0:m, i], PS[0:m, 5:7, :].rearrange("p a n -> p (a n)"),
                                                 res["b1a"][0:m, n:n + 1], gl[0:m, n % 2], ALU.add, ALU.mult)\
                            .then_inc(S["hg"], 1)
                    dve.wait_ge(S["xb"], l + 1)
                    for i in range(2):
                        dve.wait_ge(S["y2_ps"], 2 * l + i + 1)
                        v = tmp2[:, 4 * i:4 * i + 4].rearrange("p t w -> p (t w)")
                        o = xf[:, 4 * i:4 * i + 4].rearrange("p t w -> p (t w)")
                        dve.tensor_tensor(o, v, PS[:, 7 if i == 0 else 0, :], ALU.add).then_inc(S["xf"], T // 2)
                    dve.wait_ge(S["xf"], 2 * T * (l + 1))
                dve.wait_ge(S["gfin"], 1)
                link(dve.tensor_tensor(tmp[:], tmp[:], s1[:], ALU.mult))
                dve.tensor_tensor(tmp2[:], tmp[:], x1[:], ALU.add).then_inc(S["obuf"], 1)
                meet(dve, b)

        @block.tensor
        def _(pe):
            def mm(o, w, v, start=True, stop=True, **kw):
                return pe.matmul(o, w, v, start=start, stop=stop, **kw)

            pe.wait_ge(S0["w_loaded"], 16 * len(RESIDENT))
            for i in range(2):
                for c in range(CH):
                    n = i * CH + c
                    pe.wait_ge(S0["sn"], n + 1)
                    for t in range(T):
                        ins = mm(PS[:, i, H0 * t:H0 * t + H0], sinb[:, n % 2, P * t:P * t + P], res["c_blk"][:, c],
                                 start=(c == 0 and t == 0), stop=(c == CH - 1), skip_group_check=True)
                    ins.then_inc(S0["p_ps"], 1)
            pe.wait_ge(S0["p_read2"], 1)

            def transposes(src, bank, ready, done, base=0):
                for t in range(T):
                    if ready:
                        pe.wait_ge(S[ready], base + t + 1)
                    pe.transpose(PS[:, bank + t // 4, P * (t % 4):P * (t % 4) + P], src[:, t], ident[:])\
                        .then_inc(S[done], 1)

            with pe.Fori(0, B) as b:
                transposes(xn, 0, "xn_tile", "xnT_ps")
                pe.wait_ge(S["xnT"], 2)
                for t in range(T):
                    ins = mm(PS[:, 2, 48 * t:48 * t + 48], xT[:, P * t:P * t + P], res["k123"][:])
                ins.then_inc(S["lg"], 1)
                pe.wait_ge(S["rs"], 1)
                mm(PS[:, 3, 0:T * H0], upper[:], ex[:, :, 0:16], stop=False)
                mm(PS[:, 3, 0:T * H0], ones[:], rsum, start=False).then_inc(S["den_ps"], 1)
                pe.wait_ge(S["ab"], 1)
                for t in range(T + 1):
                    if t < T:
                        if t >= 1:
                            pe.wait_ge(S["u"], t)
                        mm(PS[:, 4, :], xT[:, P * t:P * t + P], res["vw"][:, 0:HALF])
                        mm(PS[:, 5, :], xT[:, P * t:P * t + P], res["vw"][:, HALF:HA]).then_inc(S["v_ps"], 1)
                        pe.wait_ge(S["cv"], t + 1)
                        if t >= 2:
                            pe.wait_ge(S["csb"], t - 1)
                        bank = 2 * (t % 2)
                        for hf in range(2):
                            ins = mm(PS[:, bank + hf, :], upper[:], cv[:, HALF * hf:HALF * hf + HALF], stop=(t == 0))
                        if t:
                            pe.wait_ge(S["csb"], t)
                            for hf in range(2):
                                ins = mm(PS[:, bank + hf, :], last_row[:],
                                         csb[:, (t - 1) % 2, HALF * hf:HALF * hf + HALF], start=False)
                        ins.then_inc(S["cum_ps"], 1)
                    if t >= 1:
                        k = t - 1
                        pe.wait_ge(S["o"], k + 1)
                        for hf in range(2):
                            if 2 * k + hf:
                                pe.wait_ge(S["oT"], 2 * k + hf)
                            for c in range(4):
                                ins = pe.transpose(PS[:, 6, P * c:P * c + P],
                                                   t1[:, k % 2, P * (4 * hf + c):P * (4 * hf + c) + P], ident[:])
                            ins.then_inc(S["oT_ps"], 1)
                        pe.wait_ge(S["oT"], 2 * k + 2)
                        if k:
                            pe.wait_ge(S["s"], k)
                        for c in range(CH):
                            ins = mm(PS[:, 7, 0:W], oT[:, k % 2, c], res["wo0"][:, c], start=(c == 0), stop=(c == CH - 1))
                        ins.then_inc(S["s_ps"], 1)

                for l in range(LOOPS):
                    transposes(tmp2, 0, "xr", "xrT_ps", base=T * l)
                    pe.wait_ge(S["xrT"], 2 * l + 2)
                    for t in range(T):
                        ins = mm(PS[:, 2, 12 * t:12 * t + 12], xT[:, P * t:P * t + P], res["w_route"][:])
                    ins.then_inc(S["rt"], 1)

                    def up(c):
                        n = l * FC + c
                        if n >= 2:
                            pe.wait_ge(S["hs"], n - 1)
                        if c == 1:
                            pe.wait_ge(S["rt_read"], l + 1)
                        for i in range(2):
                            ins = mm(PS[:, 2 * (c % 2) + i, :], res["w1e"][:, P * c:P * c + P],
                                     xT[:, HALF * i:HALF * i + HALF])
                        ins.then_inc(S["up_ps"], 1)

                    def down(e):
                        n = l * E + e
                        pe.wait_ge(S["hs"], 2 * n + 2)
                        if n >= 2:
                            pe.wait_ge(S["ym"], n - 1)
                        for t in range(T):
                            for i in range(2):
                                c = 2 * e + i
                                ins = mm(PS[:, 4 + 2 * (e % 2) + t // 4, W * (t % 4):W * (t % 4) + W],
                                         hs[:, c % 4, P * t:P * t + P], res["w2e"][:, c], start=(i == 0), stop=(i == 1))
                        ins.then_inc(S["y"], 1)

                    up(0)
                    up(1)
                    for e in range(E):
                        if e + 1 < E:
                            up(2 * e + 2)
                            up(2 * e + 3)
                        down(e)

                pe.wait_ge(S["xa"], 1)
                transposes(xa, 0, None, "xaT_ps")
                pe.wait_ge(S["xaT"], 2)
                for i in range(2):
                    ins = mm(PS[:, 2 + i, :], res["wq"][:], xT[:, HALF * i:HALF * i + HALF])
                ins.then_inc(S["q_ps"], 1)
                for i in range(2):
                    ins = mm(PS[:, 4 + i, :], res["wk"][:], xT[:, HALF * i:HALF * i + HALF])
                ins.then_inc(S["k_ps"], 1)
                for t in range(T):
                    ins = mm(PS[:, 6 + t // 4, W * (t % 4):W * (t % 4) + W], xT[:, P * t:P * t + P], res["wv"][:])
                ins.then_inc(S["v1_ps"], 1)
                pe.wait_ge(S["vaug"], 2)
                pe.wait_ge(S["qkf"], 2)

                def maxima(g, lo, hi):
                    for n in range(lo, hi):
                        j, t, hf = n // (2 * T), n // 2 % T, n % 2
                        if n == 0:
                            pe.wait_ge(S["qs_loaded"], 16 * 18 * (g + 1))
                        if g * 64 + n >= 2:
                            pe.wait_ge(S["mx"], g * 64 + n - 1)
                        if n == 0 and g:
                            pe.wait_ge(S["msp"], g)
                        mm(PS[:, 6 + n % 2, :], QS[0:KM, g % 2, j, P * t:P * t + P],
                           KS[0:KM, g % 2, j, HALF * hf:HALF * hf + HALF]).then_inc(S["mx_ps"], 1)
                    if hi == 64:
                        pe.wait_ge(S["mneg"], g + 1)
                        pe.transpose(PS[0:GH * T, 6, 0:P], mneg[:, g % 2], ident[:]).then_inc(S["mT_ps"], 1)

                maxima(0, 0, 64)
                for g in range(NGRP):
                    pe.wait_ge(S["m_row"], 16 * (g + 1))
                    for kt in range(T + 1):
                        if kt < T:
                            for j in range(GH):
                                n = (g * T + kt) * GH + j
                                if n >= 2:
                                    pe.wait_ge(S["p"], n - 1)
                                for i in range(2):
                                    ins = mm(PS[:, 2 * (n % 2) + i, :], KS[:, g % 2, j, P * kt:P * kt + P],
                                             QS[:, g % 2, j, HALF * i:HALF * i + HALF])
                                ins.then_inc(S["st_ps"], 1)
                            if g + 1 < NGRP:
                                maxima(g + 1, 8 * kt, 8 * kt + 8)
                        if kt >= 1:
                            k = kt - 1
                            pe.wait_ge(S["p"], (g * T + k + 1) * GH)
                            if k == 0 and g:
                                pe.wait_ge(S["on"], g)
                            for i in range(2):
                                for j in range(GH):
                                    n = (g * T + k) * GH + j
                                    ins = mm(PS[32 * j:32 * j + 32, 4 + i, :], vaug[:, k, GH * g + j],
                                             pb[:, n % 8, HALF * i:HALF * i + HALF], start=(k == 0), stop=(k == T - 1),
                                             tile_position=(0, 32 * j))
                            ins.then_inc(S["pv"], 1)
                pe.wait_ge(S["otn"], 1)
                pe.wait_ge(S["p"], NGRP * T * GH)
                for t in range(T):
                    ins = mm(PS[:, t // 4, W * (t % 4):W * (t % 4) + W], o_t[:, P * t:P * t + P], res["wo1"][:])
                ins.then_inc(S["op_ps"], 1)

                pe.wait_ge(S["s1"], 1)
                for l in range(DEPTH):
                    xs = xn2 if l == 0 else xf

                    def shifted(src):
                        for t in range(T):
                            o = PS[:, 0, 64 * t:64 * t + 64]
                            ins = mm(o, shift[:], src[:, t, 64:W], stop=(t == 0))
                            if t:
                                ins = mm(o, shift_in[:], src[:, t - 1, 64:W], start=False)
                        ins.then_inc(S["sh_ps"], 1)

                    if l:
                        pe.wait_ge(S["xf"], 2 * T * l)
                    shifted(xs)
                    pe.wait_ge(S["hcp_v"], 2 * l + 1)
                    pe.wait_ge(S["hcp_a"], 2 * l + 1)
                    transposes(tmp, 1, None, "hT_ps")
                    pe.wait_ge(S["hT"], 4 * l + 2)

                    def qkv(t):
                        u = l * T + t
                        if u:
                            pe.wait_ge(S["sq"], u)
                            pe.wait_ge(S["vl_ready"], 2 * u)
                        w = res["wqkv"][:, l]
                        for i in range(3):
                            ins = mm(PS[:, i, :], xT[:, P * t:P * t + P], w[:, HALF * i:HALF * i + HALF])
                        ins.then_inc(S["qkv_ps"], 1)

                    def kq(t):
                        u = l * T + t
                        pe.wait_ge(S["qkr"], u + 1)
                        for i in range(2):
                            if 3 * u + i:
                                pe.wait_ge(S["kq"], 3 * u + i)
                            for c in range(4):
                                ins = pe.transpose(PS[:, 3, P * c:P * c + P],
                                                   qk_a[:, u % 2, HALF * i + P * c:HALF * i + P * c + P], ident[:])
                            ins.then_inc(S["kq_ps"], 1)

                    def scores(u):
                        t, hf = u // 2, u % 2
                        n = 2 * T * l + u
                        pe.wait_ge(S["kq"], 3 * (l * T + t) + 3)
                        if n:
                            pe.wait_ge(S["p_sub"], n)
                        for k in range(4):
                            h = 4 * hf + k
                            o = PS[:, 4 + k // 2, KEYS * (k % 2):KEYS * (k % 2) + KEYS]
                            mm(o, qT[:, (l * T + t) % 2, h // 2], kz[:, h, P * t:P * t + KEYS], stop=False)
                            ins = mm(o, identb[:], band[:, 0 if t == 0 else 1], start=False)
                        ins.then_inc(S["s_lps"], 1)

                    qkv(0)
                    kq(0)
                    scores(0)
                    for u in range(2 * T):
                        t, hf = u // 2, u % 2
                        n = 2 * T * l + u
                        q = l * T + t
                        if hf == 0 and t + 1 < T:
                            qkv(t + 1)
                        if hf == 1 and t + 1 < T:
                            kq(t + 1)
                        if u + 1 < 2 * T:
                            scores(u + 1)
                        pe.wait_ge(S["p_exp"], n + 1)
                        if q:
                            pe.wait_ge(S["olT"], q)
                        if n:
                            pe.wait_ge(S["pt"], 2 * n)
                        for k in range(4):
                            ins = pe.transpose(PS[0:WIN, 6, P * k:P * k + P], pl[:, n % 2, k, 0:WIN], ident[:])
                        ins.then_inc(S["pt_ps"], 1)
                        pe.wait_ge(S["pt"], 2 * n + 1)
                        for k in range(4):
                            ins = pe.transpose(PS[:, 6, P * k:P * k + P], pl[:, n % 2, k, WIN:KEYS], ident[:])
                        ins.then_inc(S["pt_ps"], 1)
                        pe.wait_ge(S["pt"], 2 * n + 2)
                        pe.wait_ge(S["vl_ready"], 2 * q + 2)
                        if n:
                            pe.wait_ge(S["ol"], n)
                        if q and hf == 0:
                            pe.wait_ge(S["xf"], 2 * T * l + t)
                        for k in range(4):
                            h = 4 * hf + k
                            o = PS[:, 7, (DL + 1) * k:(DL + 1) * (k + 1)]
                            mm(o, ptA[0:WIN, n % 2, k], vp[0:WIN, (q + 2) % 3, h], stop=False)
                            ins = mm(o, ptB[:, n % 2, k], vl[:, q % 2, h], start=False)
                        ins.then_inc(S["o_lps"], 1)
                        if hf == 1:
                            pe.wait_ge(S["ol"], n + 1)
                            for c in range(4):
                                ins = pe.transpose(PS[:, 6, P * c:P * c + P], ol[:, q % 2, P * c:P * c + P], ident[:])
                            ins.then_inc(S["olT_ps"], 1)
                            pe.wait_ge(S["olT"], q + 1)
                            for c in range(4):
                                ins = mm(PS[:, 7, 0:W], olT[:, q % 2, c], res["wol"][:, l, c],
                                         start=(c == 0), stop=(c == 3))
                            ins.then_inc(S["ol_ps"], 1)
                    pe.wait_ge(S["xf"], (2 * l + 1) * T)
                    shifted(xf)
                    transposes(s_at, 1, "ffn_tile", "hT_ps", base=T * l)
                    pe.wait_ge(S["hT"], 4 * l + 4)
                    for i, (c, m) in enumerate(HC):
                        n = l * 3 + i
                        if n:
                            pe.wait_ge(S["gl"], n)
                            pe.wait_ge(S["hg"], n)
                        for part, bank, done in ((HID, 3, "g_ps"), (0, 5, "a_ps")):
                            for k in range(2):
                                ins = mm(PS[0:m, bank + k, :], res["wf1"][:, l, part + c:part + c + m],
                                         xT[:, HALF * k:HALF * k + HALF])
                            ins.then_inc(S[done], 1)
                    pe.wait_ge(S["hg"], 3 * l + 3)
                    for i in range(2):
                        for t in range(4 * i, 4 * i + 4):
                            for k, (c, m) in enumerate(HC):
                                ins = mm(PS[:, 7 if i == 0 else 0, W * (t % 4):W * (t % 4) + W],
                                         hg[0:m, k, P * t:P * t + P], res["wf2"][0:m, l, k],
                                         start=(k == 0), stop=(k == 2))
                        ins.then_inc(S["y2_ps"], 1)
                meet(pe, b)


RESIDENT = [
    ("ident", (P,), F32), ("upper", (P,), F32), ("last_row", (P,), F32), ("ones", (P,), F32),
    ("shift", (P,), F32), ("shift_in", (P,), F32), ("before", (NG, NG), F32),
    ("pos", (T,), F32), ("pe_base", (W // 2,), F32),
    ("k123", (48,), F32), ("vw", (HA,), F32), ("wo0", (CH, W), F32), ("pos_ab", (4, CH), F32), ("c_blk", (CH, H0), F32),
    ("norm_w", (1,), F32), ("w_route", (12,), F32), ("w1e", (E * F,), F32), ("w2e", (FC, W), F32),
    ("rby", (3,), F32), ("wq", (W,), F32), ("wk", (W,), F32), ("wv", (W,), F32), ("wo1", (W,), F32),
    ("bq", (1,), F32), ("bk", (1,), F32), ("bv", (W,), F32), ("bo", (W,), F32),
    ("ln_gamma", (W,), F32), ("ln_beta", (W,), F32),
    ("wqkv", (DEPTH, 3 * INNER), F32), ("qk_scale", (DEPTH, 2, 2, DL), F32), ("wol", (DEPTH, 4, W), F32),
    ("ln_g", (DEPTH,), F32), ("ln_b", (DEPTH,), F32), ("wf1", (DEPTH, 2 * HID), F32), ("wf2", (DEPTH, 3, W), F32),
    ("b1a", (DEPTH * 3,), F32), ("b1g", (DEPTH * 3,), F32), ("b2f", (DEPTH, W), F32),
]


def constants():
    c = {}
    f = np.float32
    c["ident"] = np.eye(P, dtype=f)
    c["upper"] = np.triu(np.ones((P, P), f))
    c["last_row"] = np.zeros((P, P), f)
    c["last_row"][P - 1] = 1
    c["ones"] = np.ones((P, P), f)
    c["shift"] = np.eye(P, k=1, dtype=f)
    c["shift_in"] = np.zeros((P, P), f)
    c["shift_in"][P - 1, 0] = 1
    q, k = np.arange(P)[:, None], np.arange(KEYS)[None, :]
    seen = (k >= q) & (k <= q + WIN)
    band = np.stack([seen & (k >= WIN), seen], 1)
    c["band"] = np.where(band, 0.0, -3e38).astype(f)
    g = np.arange(NG)
    c["before"] = np.broadcast_to((g[None, :] < g[:, None]).astype(f), (P, NG, NG)).copy()
    c["pos"] = (np.arange(T)[None, :] * P + np.arange(P)[:, None]).astype(f)
    i_even = np.arange(0, W, 2).astype(f)
    c["pe_base"] = np.broadcast_to(np.power(f(10000.0), f(2.0) * i_even / f(W)).astype(f), (P, W // 2)).copy()
    c["nrow"] = np.broadcast_to(np.linspace(0.0, 1.0, N, dtype=f), (P, N)).copy()
    half = np.arange(0, DL, 2).astype(f)
    inv = (f(1.0) / np.power(f(10000.0), half / f(DL))).astype(f)
    t = np.arange(N).astype(f)
    fr = (t[:, None] * inv[None, :]).astype(np.float64)
    fr = np.concatenate([fr, fr], -1)
    base = ((half + f(0.4 * DL)) / f(1.4 * DL)).astype(np.float64)
    power = ((t - N // 2) / f(WIN // 2)).astype(np.float64)
    s = base[None, :] ** power[:, None]
    s = np.concatenate([s, s], -1)
    sign = np.concatenate([-np.ones(DL // 2), np.ones(DL // 2)])
    tab = np.stack([np.cos(fr) * s, np.sin(fr) * s * sign, np.cos(fr) / s, np.sin(fr) / s * sign], 1)
    c["rot_src"] = np.ascontiguousarray(tab.astype(f).reshape(T, P, 4, DL).transpose(1, 0, 2, 3))
    return c


def layouts(i):
    f = np.float32

    def rows(v):
        return np.broadcast_to(np.asarray(v)[None], (P,) + np.asarray(v).shape).copy()

    def chunks(v, n):
        return np.ascontiguousarray(v.reshape((n, P) + v.shape[1:]).swapaxes(0, 1))

    a = {k: np.asarray(v) for k, v in i.items()}
    r = {}
    r["x"] = a["L0_attn_x"]
    r["k123"] = np.concatenate([a["L0_attn_k1"], a["L0_attn_k2"], a["L0_attn_k3"]], 0).T
    r["vw"] = a["L0_attn_value_weight"].transpose(1, 0, 2).reshape(W, HA)
    r["wo0"] = chunks(a["L0_attn_output_weight"].transpose(0, 2, 1).reshape(HA, W), CH)
    r["pos_ab"] = np.stack([a[f"L0_attn_{n}"].reshape(CH, P).T for n in ("a1", "b1", "a2", "b2")], 1)
    cb = np.zeros((P, CH, H0), f)
    cc = a["L0_attn_c"].reshape(H0, NPOS)
    for h in range(H0):
        cb[NPOS * (h % 2):NPOS * (h % 2) + NPOS, h // 2, h] = cc[h]
    r["c_blk"] = cb
    r["norm_w"] = a["L0_ffn_norm_w"][:, None]
    r["w_route"] = np.concatenate([a["L0_ffn_w_macro"], a["L0_ffn_w_micro"].reshape(E, W)], 0).T
    r["w1e"] = a["L0_ffn_w1"].reshape(E * F, W).T
    r["w2e"] = chunks(a["L0_ffn_w2"].transpose(0, 2, 1).reshape(E * F, W), FC)
    r["rby"] = rows(a["L1_attn_rby"])
    for n in "qkv":
        r["w" + n] = a["L1_attn_W" + n].T
    r["wo1"] = a["L1_attn_Wo"].T
    r["bq"], r["bk"] = a["L1_attn_bq"][:, None], a["L1_attn_bk"][:, None]
    r["bv"], r["bo"] = rows(a["L1_attn_bv"]), rows(a["L1_attn_bo"])
    r["ln_gamma"], r["ln_beta"] = rows(a["L1_attn_ln_gamma"]), rows(a["L1_attn_ln_beta"])
    r["wqkv"] = a["L1_ffn_wqkv"].transpose(1, 0, 2)
    qs = np.stack([a["L1_ffn_q_scale"], a["L1_ffn_k_scale"]], 1)
    r["qk_scale"] = rows(np.stack([qs, np.roll(qs, DL // 2, -1)], 2))
    r["wol"] = a["L1_ffn_wo"].reshape(DEPTH, 4, P, W).transpose(2, 0, 1, 3)
    r["ln_g"], r["ln_b"] = a["L1_ffn_ln_g"].T, a["L1_ffn_ln_b"].T
    r["wf1"] = a["L1_ffn_w1"].transpose(1, 0, 2)
    w2 = np.zeros((DEPTH, 3 * P, W), f)
    w2[:, :HID] = a["L1_ffn_w2"]
    r["wf2"] = w2.reshape(DEPTH, 3, P, W).transpose(2, 0, 1, 3)
    for n, lo in (("b1a", 0), ("b1g", HID)):
        v = np.zeros((DEPTH, 3 * P), f)
        v[:, :HID] = a["L1_ffn_b1"][:, lo:lo + HID]
        r[n] = v.reshape(DEPTH * 3, P).T
    r["b2f"] = rows(a["L1_ffn_b2"])
    return {k: np.ascontiguousarray(v) for k, v in r.items()}


def kernel(**inputs):
    import concourse.bacc as _bacc
    from concourse.bass_utils import run_bass_kernel_spmd as _run

    nc = _bacc.Bacc("TRN2", target_bir_lowering=False, num_devices=1)
    arrays, d = {}, {}
    for name, v in {**constants(), **layouts(inputs)}.items():
        arrays[f"in_{name}"] = v
        d[name] = nc.dram_tensor(f"in_{name}", v.shape, mybir.dt.from_np(v.dtype), kind="ExternalInput").ap()
    d["scr_qk"] = nc.dram_tensor("scr_qk", (2, 3, P, N), BF16, kind="Internal").ap()
    d["scr_m"] = nc.dram_tensor("scr_m", (2, 3, GH * N), BF16, kind="Internal").ap()
    out = nc.dram_tensor("out_x", (B, N, W), F32, kind="ExternalOutput").ap()
    build(nc, d, out)
    r = _run(nc, [arrays], core_ids=[0])
    return r.results[0]["out_x"]
```

```python
from contextlib import ExitStack

import numpy as np
import concourse.bass as bass
from concourse import mybir
from concourse.alu_op_type import AluOpType as ALU

ACT = mybir.ActivationFunctionType
F32 = mybir.dt.float32
BF16 = mybir.dt.bfloat16
I32 = mybir.dt.int32
AX = mybir.AxisListType.X

B, N, W = 4, 1024, 128
P = 128
T = N // P
HALF = 512
H0, A0 = 16, 64
NPOS = 64
HA = H0 * A0
CH = HA // P
E, F = 8, 256
NG, EPG = 4, 2
LOOPS = 2
FC = E * F // P
H1, DK = 16, 8
GH, NGRP = 4, 4
TERMS = 9
KM = 96
MROW = 96
HL, DL, WIN = 8, 64, 64
INNER = HL * DL
HID = W * 4 * 2 // 3
DEPTH = 2
HC = [(c, min(P, HID - c)) for c in range(0, HID, P)]
KEYS = WIN + P
TWO_PI = 2.0 * np.pi
MAGIC = 1.5 * 2.0 ** 23
RSQRT_SEED = float(0x5F3759DF)
PM = 0.1 * float(np.sin(2.0 * np.pi * 0.25))
EPS_ADAPTIVE = 0.1 * float(np.sin(2.0 * np.pi * 0.5))

ENGINES = 4


def build(nc, d, out):
    with ExitStack() as ctx:
        def sb(name, shape, dt=F32):
            return ctx.enter_context(nc.sbuf_tensor(name, shape, dt))

        def sem(name):
            return ctx.enter_context(nc.semaphore(name))

        PS = ctx.enter_context(nc.psum_tensor("PS", [P, 8, HALF], F32))

        def pair(i):
            return PS[:, i:i + 2, :].rearrange("p a n -> p (a n)")

        res = {}
        for name, shape, dt in RESIDENT:
            res[name] = sb(name, [P] + list(shape), dt)
        ident, upper, last_row, ones = res["ident"], res["upper"], res["last_row"], res["ones"]
        shift, shift_in = res["shift"], res["shift_in"]

        identb = sb("identb", [P, P], BF16)
        band = sb("band", [P, 2, 2 * KEYS], BF16)

        p1 = sb("p1", [P, T, H0])
        p2e = sb("p2e", [P, T, H0])
        pe_tok = sb("pe_tok", [P, T, W])
        rot_c = sb("rot_c", [P, DEPTH, T, 2, DL])
        rot_s = sb("rot_s", [P, DEPTH, T, 2, DL])
        sc = sb("sc", [P, 16])
        cq, ofac, epsr = sc[:, 0:1], sc[:, 1:2], sc[:, 2:3]
        bqc = sc[:, 4:5]
        gam = sb("gam", [P, W])

        x_in = sb("x_in", [P, T, W])
        xn = sb("xn", [P, T, W])
        s_at = sb("s_at", [P, T, W])
        zz = sb("zz", [P, T, W])
        x1 = sb("x1", [P, T, W])
        xn2 = sb("xn2", [P, T, W])
        tmp = sb("tmp", [P, T, W])
        tmp2 = sb("tmp2", [P, T, W])
        xa, s1, xf = s_at, zz, xn
        xT = sb("xT", [P, N])
        st6 = sb("st6", [P, T, 6])
        mv = sb("mv", [P, T, 2])
        var = sb("var", [P, T])
        nr_y = sb("nr_y", [P, T])
        nr_t = sb("nr_t", [P, T])
        nmr = sb("nmr", [P, T])

        arena = sb("arena", [P, 22528])
        used = [0]

        def take(shape, dt=F32, at=None):
            n = int(np.prod(shape))
            words = n if dt == F32 else (n + 1) // 2
            if at is None:
                at = used[0]
                used[0] += words
            assert at + words <= 22528, (shape, at, words)
            v = arena[:, at:at + words]
            if dt == BF16:
                v = v.bitcast(BF16)
            names = " ".join(f"d{i}" for i in range(len(shape)))
            return v.rearrange(f"p ({names}) -> p {names}", **{f"d{i}": s for i, s in enumerate(shape)})

        nrow = take([N])
        u_a = take([2, N])
        u_k = take([2, N])
        sinb = take([2, N])
        ang = take([T, W // 2])
        ang_k = take([T, W // 2])
        rot_src = take([T, 4, DL])
        p2s = take([T, H0])
        band_f = take([2, 2 * KEYS])
        used[0] = 0
        cl = take([T, 48])
        ex = take([T, 48])
        rsum = take([T, H0])
        alpha = take([T, H0])
        den0 = take([T, H0])
        Aw = take([T, H0])
        Bw = take([T, H0])
        cv = take([2, HA])
        csb = take([2, HA])
        ub = take([2, HA])
        o_all = take([T, HA])
        oT = take([2, CH, P])
        used[0] = 0
        hs = take([4, N])
        ym = take([2, T, W])
        lr = take([T, 12])
        re = take([T, 12])
        rp = take([T, 12])
        rsm = take([T, 5])
        rinv = take([T, 5])
        cmp1 = take([T, NG, NG])
        cmp2 = take([T, NG, NG])
        rank = take([T, NG])
        selw = take([T, NG])
        sw = take([T])
        um = take([T, NG])
        ue = take([T, NG])
        first = take([T, NG])
        comb = take([T, NG, EPG])
        used[0] = 0
        QS = take([2, GH, N], BF16)
        KS = take([2, GH, N], BF16)
        vaug = take([T, H1, 32])
        pb_at = used[0]
        pb = take([8, N])
        at = pb_at
        qkf = take([2, N], F32, at); at += 2 * N
        qkr = take([2, N], F32, at); at += 2 * N
        qk3 = take([2, 3, N], BF16, at)
        on = tmp[:].rearrange("p t w -> p (t w)")
        den_t = tmp2[:].rearrange("p t w -> p (t w)")
        o_t = xT[:]
        mxp = take([2, GH, T, 2])
        mneg = take([2, GH * T])
        mrs = take([2, P])
        msp = take([2, 3, P], BF16)
        used[0] = 0
        kz = take([HL, WIN + N])
        qT = take([4, N])
        vl = take([T, INNER])
        ssq = take([4, 2 * HL])
        rq = take([4, 2 * HL])
        rqt = take([4, 2 * HL])
        ml = take([2, 4])
        sl = take([2, 4])
        rl = take([2, 4])
        after = used[0]
        pl = take([2, WIN + 4 * KEYS])
        ptA = take([2, 4, P])
        ptB = take([2, 4, P])
        olT = take([2, 4, P])
        part = [take([2 * INNER], F32, after + i * 2 * INNER) for i in range(4)]
        flat = [v[:].rearrange("p t w -> p (t w)") for v in (tmp, x_in, s_at, tmp2)]
        qk_a = part[0:2] + flat[0:2]
        qk_b = flat[2:4]
        qk_sq = part[2:4]
        used[0] = HL * (WIN + N)
        gl = take([2, N])
        hg = take([3, N])

        names = """x_loaded xn_tile xnT_ps xnT lg clipped ex rs den_ps ab v_ps cv u cum_ps csb t1 o oT_ps oT s_ps s
        xr xrT_ps xrT rt rt_read rt_in rt_ex up_ps hs y ym z g0 x1 xn2
        xa xaT_ps xaT q_ps k_ps v1_ps qkf bf1 r1 bf2 bf3 vaug scr_w scr_done qs_loaded mx_ps mx mneg mT_ps msp m_scr m_row
        st_ps p pv on on_moved otn op_ps x2 s1
        sh_ps hcp_v hcp_a hT_ps hT qkv_ps sq rotb rqe qkr kq_ps kq vl s_lps ml p_exp pn ssq rq0 rot padded pt_ps pt o_lps ol olT_ps olT ol_ps xf
        ffn_tile f_ps g_ps a_ps gl hg y2_ps xb gfin obuf out_done
        cleared dve_step act_step pool_step arrive""".split()
        S = {n: sem(n) for n in names}
        go = sem("go")
        S0 = {n: sem(n) for n in "w_loaded k_loaded dve0 pool0 act0 u_ready sn p_ps p_read2".split()}

        def stepper(eng, s):
            n = [0]

            def link(ins):
                n[0] += 1
                ins.then_inc(s, 1)
                eng.wait_ge(s, n[0])
            return link

        def bc(v, shape, axis):
            return v.unsqueeze(axis).broadcast_to(shape)

        def meet(eng, b):
            eng.drain().then_inc(S["arrive"], 1)
            eng.wait_ge(go, b + 1)

        block = ctx.enter_context(nc.Block())

        @block.sync
        def _(sp):
            for name, _, _ in RESIDENT:
                sp.dma_start(res[name][:], d[name]).then_inc(S0["w_loaded"], 16)
            sp.dma_start(nrow, d["nrow"]).then_inc(S0["k_loaded"], 16)
            sp.dma_start(rot_src, d["rot_src"]).then_inc(S0["k_loaded"], 16)
            sp.dma_start(band_f, d["band"]).then_inc(S0["k_loaded"], 16)

            scr_qk, scr_m = d["scr_qk"], d["scr_m"]
            with sp.Fori(0, B) as b:
                xb_ = d["x"][bass.ds(b, 1)].rearrange("a (t p) w -> p (a t) w", p=P)
                ob_ = out[bass.ds(b, 1)].rearrange("a (t p) w -> p (a t) w", p=P)
                sp.dma_start(x_in[:], xb_).then_inc(S["x_loaded"], 16)
                for qk in range(2):
                    for i in range(3):
                        sp.wait_ge(S["bf%d" % (i + 1)], qk + 1)
                        sp.dma_start(scr_qk[qk, i], qk3[:, qk, i, :]).then_inc(S["scr_w"], 16)
                sp.wait_ge(S["scr_w"], 96)

                def load_group(g):
                    if g >= 2:
                        sp.wait_ge(S["on"], g - 1)
                    for qk, dst in ((0, QS), (1, KS)):
                        for i in range(3):
                            for j in range(3):
                                part = i if qk == 0 else j
                                src = scr_qk[qk, part].rearrange("(h c) n -> c h n", c=DK)
                                row = DK * (3 * i + j)
                                sp.dma_start(dst[row:row + DK, g % 2], src[:, GH * g:GH * g + GH])\
                                    .then_inc(S["qs_loaded"], 16)

                def load_max(g):
                    sp.wait_ge(S["msp"], g + 1)
                    sp.dma_start(scr_m[g % 2].rearrange("i (r c) -> r i c", c=P), msp[0:GH * T, g % 2])\
                        .then_inc(S["m_scr"], 16)
                    sp.wait_ge(S["m_scr"], 16 * (g + 1))
                    sp.dma_start(QS[MROW:MROW + 3, g % 2], scr_m[g % 2].rearrange("i (h n) -> i h n", n=N))\
                        .then_inc(S["m_row"], 16)

                def move_out(g):
                    sp.wait_ge(S["on"], g + 1)
                    for j in range(GH):
                        h = GH * g + j
                        sp.dma_start(o_t[DK * h:DK * h + DK], on[32 * j:32 * j + DK]).then_inc(S["on_moved"], 16)
                        sp.dma_start(den_t[DK * h:DK * h + DK], on[32 * j + DK:32 * j + 2 * DK])\
                            .then_inc(S["on_moved"], 16)

                sp.wait_ge(S["cleared"], 4)
                load_group(0)
                load_max(0)
                load_group(1)
                for g in range(NGRP):
                    if g + 1 < NGRP:
                        load_max(g + 1)
                    move_out(g)
                    if g + 2 < NGRP:
                        load_group(g + 2)
                sp.wait_ge(S["obuf"], 1)
                sp.dma_start(ob_, tmp2[:]).then_inc(S["out_done"], 16)
                sp.wait_ge(S["out_done"], 16)
                sp.wait_ge(S["arrive"], ENGINES)
                for n in names:
                    sp.sem_clear(S[n])
                sp.sem_inc(go, 1)

        @block.gpsimd
        def _(pool):
            with pool.Fori(0, B) as b:
                for t in range(T):
                    pool.wait_ge(S["t1"], t + 1)
                    pool.wait_ge(S["u"], t + 1)
                    pool.tensor_tensor(o_all[:, t], o_all[:, t], ub[:, t % 2], ALU.add).then_inc(S["o"], 1)
                for l in range(LOOPS):
                    for e in range(E):
                        pool.wait_ge(S["ym"], l * E + e + 1)
                        if l * E + e:
                            pool.wait_ge(S["z"], l * E + e)
                        src = xn if l == 0 and e == 0 else zz
                        pool.tensor_tensor(zz[:], src[:], ym[:, e % 2], ALU.add).then_inc(S["z"], 1)
                pool.wait_ge(S["x1"], 1)
                pool.memset(QS[64:P], 0.0).then_inc(S["cleared"], 1)
                pool.wait_ge(S["cleared"], 1)
                pool.memset(KS[64:96], 0.0).then_inc(S["cleared"], 1)
                pool.wait_ge(S["cleared"], 2)
                pool.memset(KS[96:P], 1.0).then_inc(S["cleared"], 1)
                pool.wait_ge(S["cleared"], 3)
                pool.memset(vaug[:, :, :, DK:32], 1.0).then_inc(S["cleared"], 1)
                pool.wait_ge(S["cleared"], 4)
                pool.wait_ge(S["s1"], 1)
                pool.memset(kz, 0.0).then_inc(S["cleared"], 1)
                pool.wait_ge(S["cleared"], 5)
                for l in range(DEPTH):
                    for t in range(T + 2):
                        u = l * T + t
                        if t < T:
                            v = qk_a[u % 4]
                            pool.wait_ge(S["rotb"], u + 1)
                            pool.tensor_tensor(v, v, qk_b[u % 2], ALU.add).then_inc(S["rot"], 1)
                        if t >= 2:
                            k = u - 2
                            pool.wait_ge(S["rot"], k + 1)
                            pool.wait_ge(S["rqe"], k + 1)
                            v = qk_a[k % 4].rearrange("p (h c) -> p h c", c=DL)
                            pool.tensor_tensor(v, v, bc(rq[:, k % 4], [P, 2 * HL, DL], 2), ALU.mult)\
                                .then_inc(S["qkr"], 1)
                    pool.wait_ge(S["kq_ps"], 2 * T * (l + 1))
                    pool.memset(pl[:, :, 0:WIN], 0.0).then_inc(S["padded"], 1)
                    pool.wait_ge(S["padded"], 2 * l + 1)
                    pool.memset(ptA[0:WIN], 0.0).then_inc(S["padded"], 1)
                    pool.wait_ge(S["xf"], (2 * l + 1) * T)
                    pool.wait_ge(S["hT"], 4 * l + 4)
                    pool.tensor_tensor(tmp2[:], xf[:], bc(res["b2f"][:, l], [P, T, W], 1), ALU.add)\
                        .then_inc(S["xb"], 1)
                meet(pool, b)

        @block.scalar
        def _(act):
            act.wait_ge(S0["dve0"], 1)
            for i in range(2):
                for c in range(CH):
                    n = i * CH + c
                    act.wait_ge(S0["u_ready"], n + 1)
                    if n >= 2:
                        act.wait_ge(S0["p_ps"], n - 1)
                    act.activation(sinb[:, n % 2], u_a[:, n % 2], ACT.Sin, scale=6.283185).then_inc(S0["sn"], 1)
            act.wait_ge(S0["u_ready"], 2 * CH + 1)
            act.activation(pe_tok.rearrange("p t (f s) -> p t f s", s=2)[:, :, :, 0], ang, ACT.Sin)\
                .then_inc(S0["act0"], 1)
            act.activation(pe_tok.rearrange("p t (f s) -> p t f s", s=2)[:, :, :, 1], ang_k, ACT.Sin)\
                .then_inc(S0["act0"], 1)
            act.wait_ge(S0["p_read2"], 1)
            act.activation(p2e[:], p2s, ACT.Exp).then_inc(S0["act0"], 1)
            act.wait_ge(S0["act0"], 3)

            with act.Fori(0, B) as b:
                link = stepper(act, S["act_step"])

                for i in range(2):
                    act.wait_ge(S["xnT_ps"], 4 * i + 4)
                    act.copy(xT[:, i * HALF:i * HALF + HALF], PS[:, 6 + i, :]).then_inc(S["xnT"], 1)
                act.wait_ge(S["clipped"], 1)
                act.activation(ex, cl, ACT.Exp).then_inc(S["ex"], 1)
                for t in range(T):
                    act.wait_ge(S["cum_ps"], t + 1)
                    if t >= 2:
                        act.wait_ge(S["t1"], t - 1)
                    act.copy(csb[:, t % 2], pair(4 + 2 * (t % 2))).then_inc(S["csb"], 1)
                for t in range(T):
                    act.wait_ge(S["oT_ps"], t + 1)
                    if t >= 2:
                        act.wait_ge(S["s_ps"], t - 1)
                    act.copy(oT[:, t % 2].rearrange("p c n -> p (c n)"), pair(2 * (t % 2))).then_inc(S["oT"], 1)
                    if t % 4 == 3:
                        act.wait_ge(S["s_ps"], t + 1)
                        act.copy(s_at[:, t - 3:t + 1].rearrange("p t w -> p (t w)"), PS[:, 4 + t // 4, :])\
                            .then_inc(S["s"], 4)
                for l in range(LOOPS):
                    for i in range(2):
                        act.wait_ge(S["xrT_ps"], 8 * l + 4 * i + 4)
                        act.activation(xT[:, i * HALF:i * HALF + HALF], PS[:, i, :], ACT.Identity,
                                       scale=res["norm_w"][:, 0:1]).then_inc(S["xrT"], 1)
                    act.wait_ge(S["rt_in"], l + 1)
                    act.activation(re, re, ACT.Exp).then_inc(S["rt_ex"], 1)
                    for c in range(FC):
                        n = l * FC + c
                        act.wait_ge(S["up_ps"], n + 1)
                        if n >= 4:
                            act.wait_ge(S["y"], n // 2 - 1)
                        act.activation(hs[:, c % 4], pair(2 * (c % 2)), ACT.Silu).then_inc(S["hs"], 1)
                act.wait_ge(S["z"], LOOPS * E)
                act.activation(tmp[:], zz[:], ACT.Silu).then_inc(S["g0"], 1)
                for i in range(2):
                    act.wait_ge(S["xaT_ps"], 4 * i + 4)
                    act.copy(xT[:, i * HALF:i * HALF + HALF], PS[:, i, :]).then_inc(S["xaT"], 1)
                for qk in range(2):
                    act.wait_ge(S["q_ps" if qk == 0 else "k_ps"], 1)
                    if qk == 0:
                        act.activation(qkf[:, 0], pair(2), ACT.Identity, bias=bqc, scale=cq).then_inc(S["qkf"], 1)
                    else:
                        act.activation(qkf[:, 1], pair(4), ACT.Identity, bias=res["bk"][:, 0:1]).then_inc(S["qkf"], 1)
                for qk in range(2):
                    act.wait_ge(S["qkf"], qk + 1)
                    act.copy(qk3[:, qk, 0], qkf[:, qk]).then_inc(S["bf1"], 1)
                for qk in range(2):
                    act.wait_ge(S["r1"], qk + 1)
                    act.copy(qk3[:, qk, 1], qkr[:, qk]).then_inc(S["bf2"], 1)
                act.wait_ge(S["scr_w"], 96)
                for g in range(NGRP):
                    for kt in range(T):
                        for j in range(GH):
                            n = (g * T + kt) * GH + j
                            act.wait_ge(S["st_ps"], n + 1)
                            if n >= 8:
                                act.wait_ge(S["pv"], n // GH - 1)
                            act.activation(pb[:, n % 8], pair(2 * (n % 2)), ACT.Exp).then_inc(S["p"], 1)
                    act.wait_ge(S["pv"], (g + 1) * T)
                    if g:
                        act.wait_ge(S["on_moved"], 128 * g)
                    act.copy(on, pair(4)).then_inc(S["on"], 1)
                act.wait_ge(S["s1"], 1)
                for l in range(DEPTH):
                    src = xn2 if l == 0 else xf
                    if l:
                        act.wait_ge(S["xf"], 2 * T * l)
                    act.copy(tmp[:, :, 0:64], src[:, :, 0:64]).then_inc(S["hcp_a"], 1)
                    for i in range(2):
                        act.wait_ge(S["hT_ps"], 16 * l + 4 * i + 4)
                        act.copy(xT[:, i * HALF:i * HALF + HALF], PS[:, 1 + i, :]).then_inc(S["hT"], 1)

                    if l == 0:
                        act.wait_ge(S["cleared"], 5)
                    for t in range(T + 3):
                        u = l * T + t
                        if t < T:
                            act.wait_ge(S["rotb"], u + 1)
                            if u >= 2:
                                act.wait_ge(S["ssq"], u - 1)
                            act.activation(qk_sq[u % 2], pair(2 * (t % 2)), ACT.Square).then_inc(S["sq"], 1)
                            act.copy(vl[:, t], PS[:, 4 + t % 2, :]).then_inc(S["vl"], 1)
                        if 1 <= t <= T:
                            k = (u - 1) % 4
                            act.wait_ge(S["ssq"], u)
                            act.activation(rqt[:, k], ssq[:, k], ACT.Ln).then_inc(S["act_step"], 1)
                            act.wait_ge(S["act_step"], u)
                            act.activation(rq[:, k], rqt[:, k], ACT.Exp, scale=-0.5).then_inc(S["rq0"], 1)
                        if t >= 3:
                            k, tt = u - 3, t - 3
                            act.wait_ge(S["kq_ps"], 2 * k + 1)
                            act.copy(qT[:, :, P * tt:P * tt + P], PS[:, 6, :].rearrange("p (c n) -> p c n", c=4))\
                                .then_inc(S["kq"], 1)
                            act.wait_ge(S["kq_ps"], 2 * k + 2)
                            for r in range(2):
                                act.copy(kz.rearrange("p (c r) n -> p r c n", r=2)[64 * r:64 * r + 64, r, :,
                                                                                   WIN + P * tt:WIN + P * tt + P],
                                         PS[64 * r:64 * r + 64, 7, :].rearrange("p (c n) -> p c n", c=4))\
                                    .then_inc(S["kq"], 1)
                    act.wait_ge(S["padded"], 2 * (l + 1))
                    for u in range(2 * T + 2):
                        n = 2 * T * l + u
                        if u < 2 * T:
                            act.wait_ge(S["ml"], n + 1)
                            if n >= 2:
                                act.wait_ge(S["pt_ps"], 2 * n - 2)
                            for k in range(4):
                                act.activation(pl[:, n % 2, WIN + KEYS * k:WIN + KEYS * (k + 1)],
                                               PS[:, 2 * (n % 2) + k // 2, KEYS * (k % 2):KEYS * (k % 2) + KEYS],
                                               ACT.Exp, bias=ml[:, n % 2, k:k + 1],
                                               accum_out=sl[:, n % 2, k:k + 1]).then_inc(S["p_exp"], 1)
                        if 1 <= u <= 2 * T:
                            m = n - 1
                            if m >= 2:
                                act.wait_ge(S["o_lps"], m - 1)
                            act.wait_ge(S["pt_ps"], 2 * m + 1)
                            act.copy(ptA[WIN:P, m % 2], PS[WIN:P, 4, :].rearrange("p (c n) -> p c n", c=4))\
                                .then_inc(S["pt"], 1)
                            act.wait_ge(S["pt_ps"], 2 * m + 2)
                            act.copy(ptB[:, m % 2], PS[:, 5, :].rearrange("p (c n) -> p c n", c=4)).then_inc(S["pt"], 1)
                        if u >= 2 and u % 2 == 1:
                            q = (n - 2) // 2
                            act.wait_ge(S["o_lps"], n - 1)
                            if q >= 2:
                                act.wait_ge(S["ol_ps"], q - 1)
                            act.copy(olT[:, q % 2], PS[:, 6, :].rearrange("p (c n) -> p c n", c=4))\
                                .then_inc(S["olT"], 1)
                    act.wait_ge(S["xf"], (2 * l + 1) * T)
                    act.wait_ge(S["hT_ps"], 16 * l + 8)
                    act.copy(tmp[:, :, 0:64], xf[:, :, 0:64]).then_inc(S["hcp_a"], 1)
                    for i in range(2):
                        act.wait_ge(S["hT_ps"], 16 * l + 8 + 4 * i + 4)
                        act.activation(xT[:, i * HALF:i * HALF + HALF], PS[:, 1 + i, :], ACT.Identity,
                                       bias=res["ln_b"][:, l:l + 1], scale=res["ln_g"][:, l:l + 1])\
                            .then_inc(S["hT"], 1)
                    for i, (c, m) in enumerate(HC):
                        n = l * 3 + i
                        act.wait_ge(S["g_ps"], n + 1)
                        if n >= 2:
                            act.wait_ge(S["hg"], n - 1)
                        act.activation(gl[0:m, n % 2], PS[0:m, 3:5, :].rearrange("p a n -> p (a n)"), ACT.Gelu,
                                       bias=res["b1g"][0:m, l * 3 + i:l * 3 + i + 1]).then_inc(S["gl"], 1)
                act.wait_ge(S["xf"], 2 * T * DEPTH)
                act.activation(tmp[:], xf[:], ACT.Silu).then_inc(S["gfin"], 1)
                meet(act, b)

        @block.vector
        def _(dve):
            dve.memset(sc[:], 0.0).then_inc(S0["dve0"], 1)
            dve.wait_ge(S0["dve0"], 1)
            dve.wait_ge(S0["w_loaded"], 16 * len(RESIDENT))
            dve.wait_ge(S0["k_loaded"], 48)
            k0 = [1]

            def link(ins):
                k0[0] += 1
                ins.then_inc(S0["dve0"], 1)
                dve.wait_ge(S0["dve0"], k0[0])

            link(dve.tensor_copy(identb[:], ident[:]))
            link(dve.tensor_copy(band[:], band_f))
            pa = res["pos_ab"]
            link(dve.tensor_scalar(pa[:], pa[:], 1.0 / TWO_PI, None, ALU.mult))
            for i in range(2):
                for c in range(CH):
                    n = i * CH + c
                    if n >= 2:
                        dve.wait_ge(S0["sn"], n - 1)
                    a, o = pa[:, 2 * i, c:c + 1], pa[:, 2 * i + 1, c:c + 1]
                    link(dve.tensor_scalar(u_a[:, n % 2], nrow, a, o, ALU.mult, ALU.add))
                    link(dve.tensor_scalar(u_k[:, n % 2], u_a[:, n % 2], MAGIC, MAGIC, ALU.add, ALU.subtract))
                    dve.tensor_tensor(u_a[:, n % 2], u_a[:, n % 2], u_k[:, n % 2], ALU.subtract)\
                        .then_inc(S0["u_ready"], 1)
            rby = res["rby"]
            link(dve.tensor_scalar(sc[:, 5:6], rby[:, 2:3], PM, 1.0, ALU.mult, ALU.add))
            link(dve.tensor_scalar(res["pe_base"][:], res["pe_base"][:], sc[:, 5:6], None, ALU.mult))
            link(dve.reciprocal(res["pe_base"][:], res["pe_base"][:]))
            link(dve.tensor_tensor(ang, bc(res["pos"][:], [P, T, W // 2], 2), bc(res["pe_base"][:], [P, T, W // 2], 1),
                                   ALU.mult))
            link(dve.tensor_scalar(ang_k, ang, 1.0 / TWO_PI, MAGIC, ALU.mult, ALU.add))
            link(dve.tensor_scalar(ang_k, ang_k, MAGIC, None, ALU.subtract))
            link(dve.scalar_tensor_tensor(ang, ang_k, -6.28125, ang, ALU.mult, ALU.add))
            link(dve.scalar_tensor_tensor(ang, ang_k, -(TWO_PI - 6.28125), ang, ALU.mult, ALU.add))
            link(dve.tensor_scalar(ang, ang, 3.1415925, -3.1415925, ALU.min, ALU.max))
            link(dve.tensor_scalar(ang_k, ang, -1.0, None, ALU.mult))
            link(dve.tensor_tensor(ang_k, ang_k, ang, ALU.min))
            dve.tensor_scalar(ang_k, ang_k, float(np.pi / 2), None, ALU.add).then_inc(S0["u_ready"], 1)
            link(dve.tensor_scalar(sc[:, 6:7], rby[:, 0:1], 0.1, 1.0, ALU.mult, ALU.add))
            link(dve.tensor_scalar(sc[:, 7:8], rby[:, 1:2], 0.05, None, ALU.mult))
            link(dve.tensor_tensor(sc[:, 8:9], sc[:, 6:7], sc[:, 7:8], ALU.add))
            link(dve.tensor_scalar(sc[:, 9:10], rby[:, 2:3], 0.15, None, ALU.mult))
            link(dve.tensor_tensor(sc[:, 8:9], sc[:, 8:9], sc[:, 9:10], ALU.add))
            link(dve.tensor_scalar(cq, sc[:, 8:9], 1.0 / float(np.sqrt(DK)), None, ALU.mult))
            link(dve.tensor_scalar(bqc, res["bq"][:, 0:1], cq, None, ALU.mult))
            link(dve.tensor_scalar(ofac, rby[:, 2:3], EPS_ADAPTIVE, 1.0, ALU.mult, ALU.add))
            link(dve.tensor_scalar(epsr, rby[:, 1:2], 0.1, 1.0, ALU.mult, ALU.add))
            link(dve.tensor_scalar(epsr, epsr, 1e-5, None, ALU.mult))
            link(dve.tensor_scalar(sc[:, 10:11], rby[:, 2:3], 0.05, None, ALU.mult))
            link(dve.tensor_tensor(sc[:, 10:11], sc[:, 10:11], sc[:, 6:7], ALU.add))
            link(dve.tensor_scalar(gam[:], res["ln_gamma"][:], sc[:, 10:11], None, ALU.mult))
            for l in range(DEPTH):
                for qk in range(2):
                    link(dve.tensor_tensor(rot_c[:, l, :, qk], rot_src[:, :, 2 * qk],
                                           bc(res["qk_scale"][:, l, qk, 0], [P, T, DL], 1), ALU.mult))
                    link(dve.tensor_tensor(rot_s[:, l, :, qk], rot_src[:, :, 2 * qk + 1],
                                           bc(res["qk_scale"][:, l, qk, 1], [P, T, DL], 1), ALU.mult))
            dve.wait_ge(S0["p_ps"], 2 * CH)
            link(dve.tensor_copy(p1.rearrange("p t h -> p (t h)"), PS[:, 0, 0:T * H0]))
            dve.tensor_scalar(p2s.rearrange("p t h -> p (t h)"), PS[:, 1, 0:T * H0], 20.0, -20.0, ALU.min, ALU.max)\
                .then_inc(S0["p_read2"], 1)
            dve.wait_ge(S0["act0"], 3)

            with dve.Fori(0, B) as b:
                link = stepper(dve, S["dve_step"])

                def rsqrt(v, y, t_, steps=3):
                    link(dve.tensor_scalar(t_.bitcast(I32), v.bitcast(I32), 1, None, ALU.logical_shift_right))
                    link(dve.tensor_scalar(y.bitcast(I32), t_.bitcast(I32), -1.0, RSQRT_SEED, ALU.mult, ALU.add))
                    for _ in range(steps):
                        link(dve.scalar_tensor_tensor(t_, y, -0.5, y, ALU.mult, ALU.mult))
                        link(dve.tensor_tensor(t_, t_, v, ALU.mult))
                        link(dve.scalar_tensor_tensor(y, t_, 1.5, y, ALU.add, ALU.mult))

                def layer_norm(src, dst, eps, done):
                    for t in range(T):
                        ins = dve.bn_stats(st6[:, t], src[:, t])
                    link(ins)
                    for t in range(T):
                        ins = dve.bn_aggr(mv[:, t], st6[:, t])
                    link(ins)
                    link(dve.tensor_scalar(var[:], mv[:, :, 1], eps, None, ALU.add))
                    rsqrt(var[:], nr_y[:], nr_t[:])
                    link(dve.scalar_tensor_tensor(nmr[:], mv[:, :, 0], -1.0, nr_y[:], ALU.mult, ALU.mult))
                    for t in range(T):
                        dve.tensor_scalar(dst[:, t], src[:, t], nr_y[:, t:t + 1], nmr[:, t:t + 1],
                                          ALU.mult, ALU.add).then_inc(S[done], 1)

                dve.wait_ge(S["x_loaded"], 16)
                layer_norm(x_in, xn, 1e-5, "xn_tile")

                dve.wait_ge(S["lg"], 1)
                lg = PS[:, 4, 0:T * 48].rearrange("p (t c) -> p t c", c=48)
                link(dve.tensor_tensor(cl[:, :, 0:16], lg[:, :, 0:16], p1[:], ALU.add))
                link(dve.tensor_scalar(cl[:, :, 16:48], lg[:, :, 16:48], 20.0, -20.0, ALU.min, ALU.max))
                dve.tensor_scalar(cl[:, :, 0:16], cl[:, :, 0:16], 20.0, -20.0, ALU.min, ALU.max)\
                    .then_inc(S["clipped"], 1)
                dve.wait_ge(S["ex"], 1)
                cross, diag, extra = ex[:, :, 0:16], ex[:, :, 16:32], ex[:, :, 32:48]
                link(dve.memset(rsum[:, 0], 0.0))
                for t in range(T - 1):
                    ins = dve.tensor_tensor(rsum[:, t + 1], rsum[:, t], cross[:, t], ALU.add)
                    if t < T - 2:
                        link(ins)
                ins.then_inc(S["rs"], 1)
                link(dve.tensor_tensor(alpha, p2e[:], extra, ALU.mult))
                dve.wait_ge(S["den_ps"], 1)
                link(dve.tensor_tensor(den0, PS[:, 5, 0:T * H0].rearrange("p (t h) -> p t h", h=H0), alpha, ALU.mult))
                link(dve.tensor_tensor(den0, den0, diag, ALU.add))
                link(dve.reciprocal(den0, den0))
                link(dve.tensor_tensor(Aw, alpha, den0, ALU.mult))
                dve.tensor_tensor(Bw, diag, den0, ALU.mult).then_inc(S["ab"], 1)
                dve.wait_ge(S["ab"], 1)

                def heads(v):
                    return v.rearrange("p (h a) -> p h a", a=A0)
                full = [P, H0, A0]
                for t in range(T + 1):
                    if t < T:
                        dve.wait_ge(S["v_ps"], t + 1)
                        if t >= 2:
                            dve.wait_ge(S["cum_ps"], t - 1)
                            dve.wait_ge(S["o"], t - 1)
                        v_ps = heads(pair(2 * (t % 2)))
                        dve.tensor_tensor(heads(cv[:, t % 2]), v_ps, bc(cross[:, t], full, 2), ALU.mult)\
                            .then_inc(S["cv"], 1)
                        dve.tensor_tensor(heads(ub[:, t % 2]), v_ps, bc(Bw[:, t], full, 2), ALU.mult)\
                            .then_inc(S["u"], 1)
                    if t >= 1:
                        k = t - 1
                        dve.wait_ge(S["csb"], k + 1)
                        dve.tensor_tensor(heads(o_all[:, k]), heads(csb[:, k % 2]), bc(Aw[:, k], full, 2), ALU.mult)\
                            .then_inc(S["t1"], 1)

                for l in range(LOOPS):
                    zs = xn if l == 0 else zz
                    if l:
                        dve.wait_ge(S["z"], E * l)
                    for t in range(T):
                        ins = dve.tensor_tensor_reduce(tmp[:, t], zs[:, t], zs[:, t], 1.0, 0.0, ALU.mult, ALU.add,
                                                       var[:, t:t + 1])
                    link(ins)
                    link(dve.tensor_scalar(var[:], var[:], 1.0 / W, 1e-6, ALU.mult, ALU.add))
                    rsqrt(var[:], nr_y[:], nr_t[:])
                    for t in range(T):
                        dve.tensor_scalar(tmp2[:, t], zs[:, t], nr_y[:, t:t + 1], None, ALU.mult)\
                            .then_inc(S["xr"], 1)
                    dve.wait_ge(S["rt"], l + 1)
                    dve.wait_ge(S["s"], T)
                    dve.tensor_copy(lr.rearrange("p t c -> p (t c)"), PS[:, 2, 0:T * 12]).then_inc(S["rt_read"], 1)
                    dve.wait_ge(S["rt_read"], l + 1)
                    mac, mic = lr[:, :, 0:NG], lr[:, :, NG:12].rearrange("p t (g e) -> p t g e", e=EPG)
                    emac, emic = re[:, :, 0:NG], re[:, :, NG:12].rearrange("p t (g e) -> p t g e", e=EPG)
                    pmac, pmic = rp[:, :, 0:NG], rp[:, :, NG:12].rearrange("p t (g e) -> p t g e", e=EPG)
                    link(dve.tensor_reduce(rsm[:, :, 0], mac, AX, ALU.max))
                    link(dve.tensor_reduce(rsm[:, :, 1:5], mic, AX, ALU.max))
                    link(dve.tensor_tensor(emac, mac, bc(rsm[:, :, 0], [P, T, NG], 2), ALU.subtract))
                    dve.tensor_tensor(emic, mic, bc(rsm[:, :, 1:5], [P, T, NG, EPG], 3), ALU.subtract)\
                        .then_inc(S["rt_in"], 1)
                    dve.wait_ge(S["rt_ex"], l + 1)
                    link(dve.tensor_reduce(rsm[:, :, 0], emac, AX, ALU.add))
                    link(dve.tensor_reduce(rsm[:, :, 1:5], emic, AX, ALU.add))
                    link(dve.reciprocal(rinv, rsm))
                    link(dve.tensor_tensor(pmac, emac, bc(rinv[:, :, 0], [P, T, NG], 2), ALU.mult))
                    link(dve.tensor_tensor(pmic, emic, bc(rinv[:, :, 1:5], [P, T, NG, EPG], 3), ALU.mult))
                    sq4 = [P, T, NG, NG]
                    link(dve.tensor_tensor(cmp1, bc(pmac, sq4, 2), bc(pmac, sq4, 3), ALU.is_gt))
                    link(dve.tensor_tensor(cmp2, bc(pmac, sq4, 2), bc(pmac, sq4, 3), ALU.is_equal))
                    link(dve.tensor_tensor(cmp2, cmp2, bc(res["before"][:], sq4, 1), ALU.mult))
                    link(dve.tensor_tensor(cmp1, cmp1, cmp2, ALU.add))
                    link(dve.tensor_reduce(rank, cmp1, AX, ALU.add))
                    link(dve.tensor_scalar(rank, rank, 2.0, None, ALU.is_lt))
                    link(dve.tensor_tensor(selw, pmac, rank, ALU.mult))
                    link(dve.tensor_reduce(sw, selw, AX, ALU.add))
                    link(dve.tensor_scalar(sw, sw, 1e-9, None, ALU.add))
                    link(dve.reciprocal(sw, sw))
                    link(dve.tensor_tensor(selw, selw, bc(sw, [P, T, NG], 2), ALU.mult))
                    link(dve.tensor_reduce(um, pmic, AX, ALU.max))
                    link(dve.tensor_scalar(ue, um, 1e-9, None, ALU.add))
                    link(dve.reciprocal(ue, ue))
                    link(dve.tensor_tensor(um, um, ue, ALU.mult))
                    link(dve.tensor_tensor(selw, selw, um, ALU.mult))
                    link(dve.tensor_tensor(first, pmic[:, :, :, 0], pmic[:, :, :, 1], ALU.is_ge))
                    link(dve.tensor_tensor(comb[:, :, :, 0], selw, first, ALU.mult))
                    link(dve.tensor_tensor(comb[:, :, :, 1], selw, comb[:, :, :, 0], ALU.subtract))
                    for e in range(E):
                        n = l * E + e
                        dve.wait_ge(S["y"], n + 1)
                        if n >= 2:
                            dve.wait_ge(S["z"], n - 1)
                        dve.tensor_tensor(ym[:, e % 2], pair(4 + 2 * (e % 2)).rearrange("p (t w) -> p t w", w=W),
                                          bc(comb[:, :, e // EPG, e % EPG], [P, T, W], 2), ALU.mult)\
                            .then_inc(S["ym"], 1)

                dve.wait_ge(S["g0"], 1)
                link(dve.tensor_tensor(tmp[:], tmp[:], s_at[:], ALU.mult))
                dve.tensor_tensor(x1[:], x_in[:], tmp[:], ALU.add).then_inc(S["x1"], 1)
                dve.wait_ge(S["x1"], 1)
                layer_norm(x1, xn2, 1e-5, "xn2")
                dve.wait_ge(S["xn2"], T)

                dve.tensor_tensor(xa[:], xn2[:], pe_tok[:], ALU.add).then_inc(S["xa"], 1)
                for qk in range(2):
                    dve.wait_ge(S["bf1"], qk + 1)
                    dve.tensor_tensor(qkr[:, qk], qkf[:, qk], qk3[:, qk, 0], ALU.subtract).then_inc(S["r1"], 1)
                for i in range(2):
                    dve.wait_ge(S["v1_ps"], 1)
                    dve.wait_ge(S["cleared"], 4)
                    dve.tensor_tensor(vaug[:, 4 * i:4 * i + 4, :, 0:DK],
                                      PS[:, 6 + i, :].rearrange("p (t h c) -> p t h c", t=4, c=DK),
                                      bc(res["bv"].rearrange("p (h c) -> p h c", c=DK), [P, 4, H1, DK], 1), ALU.add)\
                        .then_inc(S["vaug"], 1)
                for qk in range(2):
                    dve.wait_ge(S["bf2"], qk + 1)
                    dve.tensor_tensor(qk3[:, qk, 2], qkr[:, qk], qk3[:, qk, 1], ALU.subtract).then_inc(S["bf3"], 1)
                for g in range(NGRP):
                    for n in range(GH * T * 2):
                        j, t, hf = n // (2 * T), n // 2 % T, n % 2
                        dve.wait_ge(S["mx_ps"], g * 64 + n + 1)
                        dve.tensor_reduce(mxp[:, g % 2, j, t, hf:hf + 1], PS[:, 6 + n % 2, :], AX, ALU.max)\
                            .then_inc(S["mx"], 1)
                    dve.wait_ge(S["mx"], (g + 1) * 64)
                    link(dve.tensor_reduce(mneg[:, g % 2], mxp[:, g % 2].rearrange("p j t f -> p (j t) f"),
                                           AX, ALU.max))
                    dve.tensor_scalar(mneg[:, g % 2], mneg[:, g % 2], -1.0, None, ALU.mult).then_inc(S["mneg"], 1)
                    dve.wait_ge(S["mT_ps"], g + 1)
                    if g >= 2:
                        dve.wait_ge(S["m_scr"], 16 * (g - 1))
                    rows = slice(0, GH * T)
                    link(dve.tensor_copy(mrs[rows, 0], PS[rows, 6, 0:P]))
                    link(dve.tensor_copy(msp[rows, g % 2, 0], mrs[rows, 0]))
                    link(dve.tensor_tensor(mrs[rows, 1], mrs[rows, 0], msp[rows, g % 2, 0], ALU.subtract))
                    link(dve.tensor_copy(msp[rows, g % 2, 1], mrs[rows, 1]))
                    dve.tensor_tensor(msp[rows, g % 2, 2], mrs[rows, 1], msp[rows, g % 2, 1], ALU.subtract)\
                        .then_inc(S["msp"], 1)
                dve.wait_ge(S["msp"], NGRP)
                dve.wait_ge(S["on_moved"], 128 * NGRP)
                link(dve.reciprocal(den_t, den_t))
                dve.scalar_tensor_tensor(o_t, o_t, ofac, den_t, ALU.mult, ALU.mult).then_inc(S["otn"], 1)
                dve.wait_ge(S["op_ps"], 1)
                link(dve.tensor_tensor(tmp.rearrange("p t w -> p (t w)"), pair(0), xa.rearrange("p t w -> p (t w)"),
                                       ALU.add))
                link(dve.tensor_tensor(tmp[:], tmp[:], bc(res["bo"][:], [P, T, W], 1), ALU.add))
                layer_norm(tmp, tmp2, epsr, "x2")
                dve.wait_ge(S["x2"], T)
                link(dve.tensor_tensor(tmp2[:], tmp2[:], bc(gam[:], [P, T, W], 1), ALU.mult))
                dve.tensor_tensor(s1[:], tmp2[:], bc(res["ln_beta"][:], [P, T, W], 1), ALU.add).then_inc(S["s1"], 1)
                dve.wait_ge(S["s1"], 1)

                for l in range(DEPTH):
                    xs = xn2 if l == 0 else xf
                    dve.wait_ge(S["sh_ps"], 2 * l + 1)
                    dve.tensor_copy(tmp[:, :, 64:W], PS[:, 0, :].rearrange("p (t c) -> p t c", c=64))\
                        .then_inc(S["hcp_v"], 1)

                    def rotate(t):
                        u = l * T + t
                        dve.wait_ge(S["qkv_ps"], u + 1)
                        if u >= 4:
                            dve.wait_ge(S["kq_ps"], 2 * u - 6)
                        if u >= 2:
                            dve.wait_ge(S["rot"], u - 1)
                        qk_ps = pair(2 * (t % 2))
                        shape = [P, 2, HL, DL]
                        dve.tensor_tensor(qk_a[u % 4].rearrange("p (q h c) -> p q h c", q=2, c=DL),
                                          qk_ps.rearrange("p (q h c) -> p q h c", q=2, c=DL),
                                          bc(rot_c[:, l, t], shape, 2), ALU.mult)
                        for hf in range(2):
                            o = qk_b[u % 2].rearrange("p (q h f c) -> p q h f c", q=2, h=HL, f=2)[:, :, :, hf]
                            v = qk_ps.rearrange("p (q h f c) -> p q h f c", q=2, h=HL, f=2)[:, :, :, 1 - hf]
                            w = rot_s[:, l, t].rearrange("p q (f c) -> p q f c", f=2)[:, :, hf]
                            ins = dve.tensor_tensor(o, v, bc(w, [P, 2, HL, DL // 2], 2), ALU.mult)
                        ins.then_inc(S["rotb"], 1)

                    for t in range(T + 2):
                        u = l * T + t
                        if t < T:
                            rotate(t)
                        if 1 <= t <= T:
                            k = (u - 1) % 4
                            dve.wait_ge(S["sq"], u)
                            link(dve.tensor_reduce(ssq[:, k], qk_sq[(u - 1) % 2].rearrange("p (h c) -> p h c", c=DL),
                                                   AX, ALU.add))
                            dve.tensor_scalar(ssq[:, k], ssq[:, k], 1e-24, None, ALU.max).then_inc(S["ssq"], 1)
                        if t >= 2:
                            k = (u - 2) % 4
                            y, v, w = rq[:, k], ssq[:, k], rqt[:, k]
                            dve.wait_ge(S["rq0"], u - 1)
                            link(dve.scalar_tensor_tensor(w, y, -0.5, y, ALU.mult, ALU.mult))
                            link(dve.tensor_tensor(w, w, v, ALU.mult))
                            link(dve.scalar_tensor_tensor(y, w, 1.5, y, ALU.add, ALU.mult))
                            dve.tensor_scalar(rq[:, k, 0:HL], rq[:, k, 0:HL], 8.0, None, ALU.mult)\
                                .then_inc(S["rqe"], 1)

                    for u in range(2 * T + 3):
                        n = 2 * T * l + u
                        if u < 2 * T:
                            sv = PS[:, 2 * (n % 2):2 * (n % 2) + 2, 0:2 * KEYS].rearrange("p a (h c) -> p a h c", h=2)
                            dve.wait_ge(S["s_lps"], n + 1)
                            if n >= 2:
                                dve.wait_ge(S["p_exp"], 4 * (n - 1))
                            link(dve.tensor_reduce(ml[:, n % 2].rearrange("p (a h) -> p a h", a=2), sv, AX, ALU.max))
                            dve.tensor_scalar(ml[:, n % 2], ml[:, n % 2], -1.0, None, ALU.mult).then_inc(S["ml"], 1)
                        if 1 <= u <= 2 * T:
                            m = n - 1
                            dve.wait_ge(S["p_exp"], 4 * (m + 1))
                            link(dve.reciprocal(rl[:, m % 2], sl[:, m % 2]))
                            v = pl[:, m % 2, WIN:WIN + 4 * KEYS].rearrange("p (h c) -> p h c", c=KEYS)
                            dve.tensor_tensor(v, v, bc(rl[:, m % 2], [P, 4, KEYS], 2), ALU.mult).then_inc(S["pn"], 1)
                        if u >= 4 and u % 2 == 0:
                            t = (u - 4) // 2
                            dve.wait_ge(S["ol_ps"], l * T + t + 1)
                            dve.tensor_tensor(xf[:, t], xs[:, t], PS[:, 7, 0:W], ALU.add).then_inc(S["xf"], 1)
                    dve.wait_ge(S["sh_ps"], 2 * l + 2)
                    dve.tensor_copy(tmp[:, :, 64:W], PS[:, 0, :].rearrange("p (t c) -> p t c", c=64))\
                        .then_inc(S["hcp_v"], 1)
                    dve.wait_ge(S["hcp_v"], 2 * l + 2)
                    dve.wait_ge(S["hcp_a"], 2 * l + 2)
                    layer_norm(tmp, s_at, 1e-5, "ffn_tile")
                    for i, (c, m) in enumerate(HC):
                        n = l * 3 + i
                        dve.wait_ge(S["gl"], n + 1)
                        dve.wait_ge(S["a_ps"], n + 1)
                        dve.scalar_tensor_tensor(hg[0:m, i], PS[0:m, 5:7, :].rearrange("p a n -> p (a n)"),
                                                 res["b1a"][0:m, n:n + 1], gl[0:m, n % 2], ALU.add, ALU.mult)\
                            .then_inc(S["hg"], 1)
                    dve.wait_ge(S["xb"], l + 1)
                    for i in range(2):
                        dve.wait_ge(S["y2_ps"], 2 * l + i + 1)
                        v = tmp2[:, 4 * i:4 * i + 4].rearrange("p t w -> p (t w)")
                        o = xf[:, 4 * i:4 * i + 4].rearrange("p t w -> p (t w)")
                        dve.tensor_tensor(o, v, PS[:, 7 if i == 0 else 0, :], ALU.add).then_inc(S["xf"], T // 2)
                    dve.wait_ge(S["xf"], 2 * T * (l + 1))
                dve.wait_ge(S["gfin"], 1)
                link(dve.tensor_tensor(tmp[:], tmp[:], s1[:], ALU.mult))
                dve.tensor_tensor(tmp2[:], tmp[:], x1[:], ALU.add).then_inc(S["obuf"], 1)
                meet(dve, b)

        @block.tensor
        def _(pe):
            def mm(o, w, v, start=True, stop=True, **kw):
                return pe.matmul(o, w, v, start=start, stop=stop, **kw)

            pe.wait_ge(S0["w_loaded"], 16 * len(RESIDENT))
            for i in range(2):
                for c in range(CH):
                    n = i * CH + c
                    pe.wait_ge(S0["sn"], n + 1)
                    for t in range(T):
                        ins = mm(PS[:, i, H0 * t:H0 * t + H0], sinb[:, n % 2, P * t:P * t + P], res["c_blk"][:, c],
                                 start=(c == 0 and t == 0), stop=(c == CH - 1), skip_group_check=True)
                    ins.then_inc(S0["p_ps"], 1)
            pe.wait_ge(S0["p_read2"], 1)

            def transposes(src, bank, ready, done, base=0):
                for t in range(T):
                    if ready:
                        pe.wait_ge(S[ready], base + t + 1)
                    pe.transpose(PS[:, bank + t // 4, P * (t % 4):P * (t % 4) + P], src[:, t], ident[:])\
                        .then_inc(S[done], 1)

            with pe.Fori(0, B) as b:
                transposes(xn, 6, "xn_tile", "xnT_ps")
                pe.wait_ge(S["xnT"], 2)
                for t in range(T):
                    ins = mm(PS[:, 4, 48 * t:48 * t + 48], xT[:, P * t:P * t + P], res["k123"][:])
                ins.then_inc(S["lg"], 1)

                def values(t):
                    if t >= 2:
                        pe.wait_ge(S["u"], t - 1)
                    for hf in range(2):
                        ins = mm(PS[:, 2 * (t % 2) + hf, :], xT[:, P * t:P * t + P],
                                 res["vw"][:, HALF * hf:HALF * hf + HALF])
                    ins.then_inc(S["v_ps"], 1)

                values(0)
                values(1)
                pe.wait_ge(S["rs"], 1)
                mm(PS[:, 5, 0:T * H0], upper[:], ex[:, :, 0:16], stop=False)
                mm(PS[:, 5, 0:T * H0], ones[:], rsum, start=False).then_inc(S["den_ps"], 1)
                for t in range(T):
                    pe.wait_ge(S["cv"], t + 1)
                    if t == 0:
                        pe.wait_ge(S["ab"], 1)
                    if t >= 2:
                        pe.wait_ge(S["csb"], t - 1)
                    bank = 4 + 2 * (t % 2)
                    for hf in range(2):
                        ins = mm(PS[:, bank + hf, :], upper[:], cv[:, t % 2, HALF * hf:HALF * hf + HALF], stop=(t == 0))
                    if t:
                        pe.wait_ge(S["csb"], t)
                        for hf in range(2):
                            ins = mm(PS[:, bank + hf, :], last_row[:],
                                     csb[:, (t - 1) % 2, HALF * hf:HALF * hf + HALF], start=False)
                    ins.then_inc(S["cum_ps"], 1)
                    if t + 2 < T:
                        values(t + 2)

                def out_transposes(t):
                    pe.wait_ge(S["o"], t + 1)
                    if t == 1:
                        pe.wait_ge(S["u"], T)
                    if t >= 2:
                        pe.wait_ge(S["oT"], t - 1)
                    for c in range(CH):
                        ins = pe.transpose(PS[:, 2 * (t % 2) + c // 4, P * (c % 4):P * (c % 4) + P],
                                           o_all[:, t, P * c:P * c + P], ident[:])
                    ins.then_inc(S["oT_ps"], 1)

                out_transposes(0)
                pe.wait_ge(S["csb"], T)
                for t in range(T):
                    if t + 1 < T:
                        out_transposes(t + 1)
                    pe.wait_ge(S["oT"], t + 1)
                    for c in range(CH):
                        ins = mm(PS[:, 4 + t // 4, W * (t % 4):W * (t % 4) + W], oT[:, t % 2, c], res["wo0"][:, c],
                                 start=(c == 0), stop=(c == CH - 1))
                    ins.then_inc(S["s_ps"], 1)

                for l in range(LOOPS):
                    transposes(tmp2, 0, "xr", "xrT_ps", base=T * l)
                    pe.wait_ge(S["xrT"], 2 * l + 2)
                    for t in range(T):
                        ins = mm(PS[:, 2, 12 * t:12 * t + 12], xT[:, P * t:P * t + P], res["w_route"][:])
                    ins.then_inc(S["rt"], 1)

                    def up(c):
                        n = l * FC + c
                        if n >= 2:
                            pe.wait_ge(S["hs"], n - 1)
                        if c == 1:
                            pe.wait_ge(S["rt_read"], l + 1)
                        for i in range(2):
                            ins = mm(PS[:, 2 * (c % 2) + i, :], res["w1e"][:, P * c:P * c + P],
                                     xT[:, HALF * i:HALF * i + HALF])
                        ins.then_inc(S["up_ps"], 1)

                    def down(e):
                        n = l * E + e
                        pe.wait_ge(S["hs"], 2 * n + 2)
                        if n >= 2:
                            pe.wait_ge(S["ym"], n - 1)
                        else:
                            pe.wait_ge(S["s"], T)
                        for t in range(T):
                            for i in range(2):
                                c = 2 * e + i
                                ins = mm(PS[:, 4 + 2 * (e % 2) + t // 4, W * (t % 4):W * (t % 4) + W],
                                         hs[:, c % 4, P * t:P * t + P], res["w2e"][:, c], start=(i == 0), stop=(i == 1))
                        ins.then_inc(S["y"], 1)

                    up(0)
                    up(1)
                    for e in range(E):
                        if e + 1 < E:
                            up(2 * e + 2)
                            up(2 * e + 3)
                        down(e)

                pe.wait_ge(S["xa"], 1)
                transposes(xa, 0, None, "xaT_ps")
                pe.wait_ge(S["xaT"], 2)
                for i in range(2):
                    ins = mm(PS[:, 2 + i, :], res["wq"][:], xT[:, HALF * i:HALF * i + HALF])
                ins.then_inc(S["q_ps"], 1)
                for i in range(2):
                    ins = mm(PS[:, 4 + i, :], res["wk"][:], xT[:, HALF * i:HALF * i + HALF])
                ins.then_inc(S["k_ps"], 1)
                for t in range(T):
                    ins = mm(PS[:, 6 + t // 4, W * (t % 4):W * (t % 4) + W], xT[:, P * t:P * t + P], res["wv"][:])
                ins.then_inc(S["v1_ps"], 1)
                pe.wait_ge(S["vaug"], 2)
                pe.wait_ge(S["qkf"], 2)

                def maxima(g, lo, hi):
                    for n in range(lo, hi):
                        j, t, hf = n // (2 * T), n // 2 % T, n % 2
                        if n == 0:
                            pe.wait_ge(S["qs_loaded"], 16 * 18 * (g + 1))
                        if g * 64 + n >= 2:
                            pe.wait_ge(S["mx"], g * 64 + n - 1)
                        if n == 0 and g:
                            pe.wait_ge(S["msp"], g)
                        mm(PS[:, 6 + n % 2, :], QS[0:KM, g % 2, j, P * t:P * t + P],
                           KS[0:KM, g % 2, j, HALF * hf:HALF * hf + HALF]).then_inc(S["mx_ps"], 1)
                    if hi == 64:
                        pe.wait_ge(S["mneg"], g + 1)
                        pe.transpose(PS[0:GH * T, 6, 0:P], mneg[:, g % 2], ident[:]).then_inc(S["mT_ps"], 1)

                maxima(0, 0, 64)
                for g in range(NGRP):
                    pe.wait_ge(S["m_row"], 16 * (g + 1))
                    for kt in range(T + 1):
                        for j in range(GH):
                            if kt < T:
                                n = (g * T + kt) * GH + j
                                if n >= 2:
                                    pe.wait_ge(S["p"], n - 1)
                                for i in range(2):
                                    ins = mm(PS[:, 2 * (n % 2) + i, :], KS[:, g % 2, j, P * kt:P * kt + P],
                                             QS[:, g % 2, j, HALF * i:HALF * i + HALF])
                                ins.then_inc(S["st_ps"], 1)
                                if g + 1 < NGRP:
                                    maxima(g + 1, 8 * kt + 2 * j, 8 * kt + 2 * j + 2)
                            if kt >= 1 and j % 2 == 1:
                                k = kt - 1
                                i = j // 2
                                if i == 0:
                                    pe.wait_ge(S["p"], (g * T + k + 1) * GH)
                                if k == 0 and g:
                                    pe.wait_ge(S["on"], g)
                                for h in range(GH):
                                    n = (g * T + k) * GH + h
                                    ins = mm(PS[32 * h:32 * h + 32, 4 + i, :], vaug[:, k, GH * g + h],
                                             pb[:, n % 8, HALF * i:HALF * i + HALF], start=(k == 0), stop=(k == T - 1),
                                             tile_position=(0, 32 * h))
                                if i == 1:
                                    ins.then_inc(S["pv"], 1)
                pe.wait_ge(S["otn"], 1)
                pe.wait_ge(S["p"], NGRP * T * GH)
                for t in range(T):
                    ins = mm(PS[:, t // 4, W * (t % 4):W * (t % 4) + W], o_t[:, P * t:P * t + P], res["wo1"][:])
                ins.then_inc(S["op_ps"], 1)

                pe.wait_ge(S["s1"], 1)
                for l in range(DEPTH):
                    xs = xn2 if l == 0 else xf

                    def shifted(src):
                        for t in range(T):
                            o = PS[:, 0, 64 * t:64 * t + 64]
                            ins = mm(o, shift[:], src[:, t, 64:W], stop=(t == 0))
                            if t:
                                ins = mm(o, shift_in[:], src[:, t - 1, 64:W], start=False)
                        ins.then_inc(S["sh_ps"], 1)

                    if l:
                        pe.wait_ge(S["xf"], 2 * T * l)
                    shifted(xs)
                    pe.wait_ge(S["hcp_v"], 2 * l + 1)
                    pe.wait_ge(S["hcp_a"], 2 * l + 1)
                    transposes(tmp, 1, None, "hT_ps")
                    pe.wait_ge(S["hT"], 4 * l + 2)

                    def qkv(t):
                        u = l * T + t
                        if t >= 2:
                            pe.wait_ge(S["vl"], u - 1)
                        w = res["wqkv"][:, l]
                        for i, bank in enumerate((2 * (t % 2), 2 * (t % 2) + 1, 4 + t % 2)):
                            ins = mm(PS[:, bank, :], xT[:, P * t:P * t + P], w[:, HALF * i:HALF * i + HALF])
                        ins.then_inc(S["qkv_ps"], 1)

                    def kq(t):
                        u = l * T + t
                        pe.wait_ge(S["qkr"], u + 1)
                        for i in range(2):
                            if u:
                                pe.wait_ge(S["kq"], 3 * u - 2 + 2 * i)
                            for c in range(4):
                                ins = pe.transpose(PS[:, 6 + i, P * c:P * c + P],
                                                   qk_a[u % 4][:, HALF * i + P * c:HALF * i + P * c + P], ident[:])
                            ins.then_inc(S["kq_ps"], 1)

                    def scores(u):
                        t, hf = u // 2, u % 2
                        n = 2 * T * l + u
                        if n >= 2:
                            pe.wait_ge(S["p_exp"], 4 * (n - 1))
                        for a in range(2):
                            bank = 2 * (n % 2) + a
                            mm(PS[:, bank, 0:2 * KEYS], identb[:], band[:, 0 if t == 0 else 1], stop=False)
                            for k in range(2):
                                h = 4 * hf + 2 * a + k
                                ins = mm(PS[:, bank, KEYS * k:KEYS * k + KEYS], qT[:, h // 2, P * t:P * t + P],
                                         kz[:, h, P * t:P * t + KEYS], start=False, stop=(k == 1))
                        ins.then_inc(S["s_lps"], 1)

                    for t in range(T + 3):
                        if t < T:
                            qkv(t)
                        if t >= 3:
                            kq(t - 3)
                    pe.wait_ge(S["kq"], 3 * T * (l + 1))
                    for u in range(2 * T + 3):
                        n = 2 * T * l + u
                        if u < 2 * T:
                            scores(u)
                        if 1 <= u <= 2 * T:
                            m = n - 1
                            pe.wait_ge(S["pn"], m + 1)
                            for i in range(2):
                                if m:
                                    pe.wait_ge(S["pt"], 2 * m - 1 + i)
                                for k in range(4):
                                    c = KEYS * k + (0 if i == 0 else P)
                                    ins = pe.transpose(PS[:, 4 + i, P * k:P * k + P], pl[:, m % 2, c:c + P], ident[:])
                                ins.then_inc(S["pt_ps"], 1)
                        if 2 <= u <= 2 * T + 1:
                            m = n - 2
                            t, hf = (u - 2) // 2, u % 2
                            q = l * T + t
                            pe.wait_ge(S["pt"], 2 * m + 2)
                            if hf == 0 and q:
                                pe.wait_ge(S["olT"], q)
                            for c in range(2):
                                for i in range(0 if t else 1, 2):
                                    for r in range(2):
                                        k = 2 * c + r
                                        col = 64 * (4 * hf + k)
                                        ins = mm(PS[64 * r:64 * r + 64, 6, P * (2 * hf + c):P * (2 * hf + c) + P],
                                                 vl[:, t - 1 + i, col:col + 64], (ptA if i == 0 else ptB)[:, m % 2, k],
                                                 start=(i == 1 and t == 0) or i == 0, stop=(i == 1),
                                                 tile_position=(0, 64 * r))
                            ins.then_inc(S["o_lps"], 1)
                        if u >= 4 and u % 2 == 0:
                            t = (u - 4) // 2
                            q = l * T + t
                            pe.wait_ge(S["olT"], q + 1)
                            pe.wait_ge(S["xf"], 2 * T * l + t)
                            for c in range(4):
                                ins = mm(PS[:, 7, 0:W], olT[:, q % 2, c], res["wol"][:, l, c],
                                         start=(c == 0), stop=(c == 3))
                            ins.then_inc(S["ol_ps"], 1)
                    pe.wait_ge(S["xf"], (2 * l + 1) * T)
                    shifted(xf)
                    transposes(s_at, 1, "ffn_tile", "hT_ps", base=T * l)
                    pe.wait_ge(S["hT"], 4 * l + 4)
                    for i, (c, m) in enumerate(HC):
                        n = l * 3 + i
                        if n:
                            pe.wait_ge(S["gl"], n)
                            pe.wait_ge(S["hg"], n)
                        for part, bank, done in ((HID, 3, "g_ps"), (0, 5, "a_ps")):
                            for k in range(2):
                                ins = mm(PS[0:m, bank + k, :], res["wf1"][:, l, part + c:part + c + m],
                                         xT[:, HALF * k:HALF * k + HALF])
                            ins.then_inc(S[done], 1)
                    pe.wait_ge(S["hg"], 3 * l + 3)
                    for i in range(2):
                        for t in range(4 * i, 4 * i + 4):
                            for k, (c, m) in enumerate(HC):
                                ins = mm(PS[:, 7 if i == 0 else 0, W * (t % 4):W * (t % 4) + W],
                                         hg[0:m, k, P * t:P * t + P], res["wf2"][0:m, l, k],
                                         start=(k == 0), stop=(k == 2))
                        ins.then_inc(S["y2_ps"], 1)
                meet(pe, b)


RESIDENT = [
    ("ident", (P,), F32), ("upper", (P,), F32), ("last_row", (P,), F32), ("ones", (P,), F32),
    ("shift", (P,), F32), ("shift_in", (P,), F32), ("before", (NG, NG), F32),
    ("pos", (T,), F32), ("pe_base", (W // 2,), F32),
    ("k123", (48,), F32), ("vw", (HA,), F32), ("wo0", (CH, W), F32), ("pos_ab", (4, CH), F32), ("c_blk", (CH, H0), F32),
    ("norm_w", (1,), F32), ("w_route", (12,), F32), ("w1e", (E * F,), F32), ("w2e", (FC, W), F32),
    ("rby", (3,), F32), ("wq", (W,), F32), ("wk", (W,), F32), ("wv", (W,), F32), ("wo1", (W,), F32),
    ("bq", (1,), F32), ("bk", (1,), F32), ("bv", (W,), F32), ("bo", (W,), F32),
    ("ln_gamma", (W,), F32), ("ln_beta", (W,), F32),
    ("wqkv", (DEPTH, 3 * INNER), F32), ("qk_scale", (DEPTH, 2, 2, DL), F32), ("wol", (DEPTH, 4, W), F32),
    ("ln_g", (DEPTH,), F32), ("ln_b", (DEPTH,), F32), ("wf1", (DEPTH, 2 * HID), F32), ("wf2", (DEPTH, 3, W), F32),
    ("b1a", (DEPTH * 3,), F32), ("b1g", (DEPTH * 3,), F32), ("b2f", (DEPTH, W), F32),
]


def constants():
    c = {}
    f = np.float32
    c["ident"] = np.eye(P, dtype=f)
    c["upper"] = np.triu(np.ones((P, P), f))
    c["last_row"] = np.zeros((P, P), f)
    c["last_row"][P - 1] = 1
    c["ones"] = np.ones((P, P), f)
    c["shift"] = np.eye(P, k=1, dtype=f)
    c["shift_in"] = np.zeros((P, P), f)
    c["shift_in"][P - 1, 0] = 1
    q, k = np.arange(P)[:, None], np.arange(KEYS)[None, :]
    seen = (k >= q) & (k <= q + WIN)
    band = np.tile(np.stack([seen & (k >= WIN), seen], 1), 2)
    c["band"] = np.where(band, 0.0, -3e38).astype(f)
    g = np.arange(NG)
    c["before"] = np.broadcast_to((g[None, :] < g[:, None]).astype(f), (P, NG, NG)).copy()
    c["pos"] = (np.arange(T)[None, :] * P + np.arange(P)[:, None]).astype(f)
    i_even = np.arange(0, W, 2).astype(f)
    c["pe_base"] = np.broadcast_to(np.power(f(10000.0), f(2.0) * i_even / f(W)).astype(f), (P, W // 2)).copy()
    c["nrow"] = np.broadcast_to(np.linspace(0.0, 1.0, N, dtype=f), (P, N)).copy()
    half = np.arange(0, DL, 2).astype(f)
    inv = (f(1.0) / np.power(f(10000.0), half / f(DL))).astype(f)
    t = np.arange(N).astype(f)
    fr = (t[:, None] * inv[None, :]).astype(np.float64)
    fr = np.concatenate([fr, fr], -1)
    base = ((half + f(0.4 * DL)) / f(1.4 * DL)).astype(np.float64)
    power = ((t - N // 2) / f(WIN // 2)).astype(np.float64)
    s = base[None, :] ** power[:, None]
    s = np.concatenate([s, s], -1)
    sign = np.concatenate([-np.ones(DL // 2), np.ones(DL // 2)])
    tab = np.stack([np.cos(fr) * s, np.sin(fr) * s * sign, np.cos(fr) / s, np.sin(fr) / s * sign], 1)
    c["rot_src"] = np.ascontiguousarray(tab.astype(f).reshape(T, P, 4, DL).transpose(1, 0, 2, 3))
    return c


def layouts(i):
    f = np.float32

    def rows(v):
        return np.broadcast_to(np.asarray(v)[None], (P,) + np.asarray(v).shape).copy()

    def chunks(v, n):
        return np.ascontiguousarray(v.reshape((n, P) + v.shape[1:]).swapaxes(0, 1))

    a = {k: np.asarray(v) for k, v in i.items()}
    r = {}
    r["x"] = a["L0_attn_x"]
    r["k123"] = np.concatenate([a["L0_attn_k1"], a["L0_attn_k2"], a["L0_attn_k3"]], 0).T
    r["vw"] = a["L0_attn_value_weight"].transpose(1, 0, 2).reshape(W, HA)
    r["wo0"] = chunks(a["L0_attn_output_weight"].transpose(0, 2, 1).reshape(HA, W), CH)
    r["pos_ab"] = np.stack([a[f"L0_attn_{n}"].reshape(CH, P).T for n in ("a1", "b1", "a2", "b2")], 1)
    cb = np.zeros((P, CH, H0), f)
    cc = a["L0_attn_c"].reshape(H0, NPOS)
    for h in range(H0):
        cb[NPOS * (h % 2):NPOS * (h % 2) + NPOS, h // 2, h] = cc[h]
    r["c_blk"] = cb
    r["norm_w"] = a["L0_ffn_norm_w"][:, None]
    r["w_route"] = np.concatenate([a["L0_ffn_w_macro"], a["L0_ffn_w_micro"].reshape(E, W)], 0).T
    r["w1e"] = a["L0_ffn_w1"].reshape(E * F, W).T
    r["w2e"] = chunks(a["L0_ffn_w2"].transpose(0, 2, 1).reshape(E * F, W), FC)
    r["rby"] = rows(a["L1_attn_rby"])
    for n in "qkv":
        r["w" + n] = a["L1_attn_W" + n].T
    r["wo1"] = a["L1_attn_Wo"].T
    r["bq"], r["bk"] = a["L1_attn_bq"][:, None], a["L1_attn_bk"][:, None]
    r["bv"], r["bo"] = rows(a["L1_attn_bv"]), rows(a["L1_attn_bo"])
    r["ln_gamma"], r["ln_beta"] = rows(a["L1_attn_ln_gamma"]), rows(a["L1_attn_ln_beta"])
    r["wqkv"] = a["L1_ffn_wqkv"].transpose(1, 0, 2)
    qs = np.stack([a["L1_ffn_q_scale"], a["L1_ffn_k_scale"]], 1)
    r["qk_scale"] = rows(np.stack([qs, np.roll(qs, DL // 2, -1)], 2))
    r["wol"] = a["L1_ffn_wo"].reshape(DEPTH, 4, P, W).transpose(2, 0, 1, 3)
    r["ln_g"], r["ln_b"] = a["L1_ffn_ln_g"].T, a["L1_ffn_ln_b"].T
    r["wf1"] = a["L1_ffn_w1"].transpose(1, 0, 2)
    w2 = np.zeros((DEPTH, 3 * P, W), f)
    w2[:, :HID] = a["L1_ffn_w2"]
    r["wf2"] = w2.reshape(DEPTH, 3, P, W).transpose(2, 0, 1, 3)
    for n, lo in (("b1a", 0), ("b1g", HID)):
        v = np.zeros((DEPTH, 3 * P), f)
        v[:, :HID] = a["L1_ffn_b1"][:, lo:lo + HID]
        r[n] = v.reshape(DEPTH * 3, P).T
    r["b2f"] = rows(a["L1_ffn_b2"])
    return {k: np.ascontiguousarray(v) for k, v in r.items()}


def kernel(**inputs):
    import concourse.bacc as _bacc
    from concourse.bass_utils import run_bass_kernel_spmd as _run

    nc = _bacc.Bacc("TRN2", target_bir_lowering=False, num_devices=1)
    arrays, d = {}, {}
    for name, v in {**constants(), **layouts(inputs)}.items():
        arrays[f"in_{name}"] = v
        d[name] = nc.dram_tensor(f"in_{name}", v.shape, mybir.dt.from_np(v.dtype), kind="ExternalInput").ap()
    d["scr_qk"] = nc.dram_tensor("scr_qk", (2, 3, P, N), BF16, kind="Internal").ap()
    d["scr_m"] = nc.dram_tensor("scr_m", (2, 3, GH * N), BF16, kind="Internal").ap()
    out = nc.dram_tensor("out_x", (B, N, W), F32, kind="ExternalOutput").ap()
    build(nc, d, out)
    r = _run(nc, [arrays], core_ids=[0])
    return r.results[0]["out_x"]
```

```python
from contextlib import ExitStack

import numpy as np
import concourse.bass as bass
from concourse import mybir
from concourse.alu_op_type import AluOpType as ALU

ACT = mybir.ActivationFunctionType
F32 = mybir.dt.float32
BF16 = mybir.dt.bfloat16
I32 = mybir.dt.int32
AX = mybir.AxisListType.X

B, N, W = 4, 1024, 128
P = 128
T = N // P
HALF = 512
H0, A0 = 16, 64
NPOS = 64
HA = H0 * A0
CH = HA // P
E, F = 8, 256
NG, EPG = 4, 2
LOOPS = 2
FC = E * F // P
H1, DK = 16, 8
GH, NGRP = 4, 4
PARTS_W = 8
KM = 96
MROW = 96
HL, DL, WIN = 8, 64, 64
INNER = HL * DL
HID = W * 4 * 2 // 3
DEPTH = 2
HC = [(c, min(P, HID - c)) for c in range(0, HID, P)]
KEYS = WIN + P
TWO_PI = 2.0 * np.pi
MAGIC = 1.5 * 2.0 ** 23
RSQRT_SEED = float(0x5F3759DF)
PM = 0.1 * float(np.sin(2.0 * np.pi * 0.25))
EPS_ADAPTIVE = 0.1 * float(np.sin(2.0 * np.pi * 0.5))

ENGINES = 4


def build(nc, d, out):
    with ExitStack() as ctx:
        def sb(name, shape, dt=F32):
            return ctx.enter_context(nc.sbuf_tensor(name, shape, dt))

        def sem(name):
            return ctx.enter_context(nc.semaphore(name))

        PS = ctx.enter_context(nc.psum_tensor("PS", [P, 8, HALF], F32))

        def pair(i):
            return PS[:, i:i + 2, :].rearrange("p a n -> p (a n)")

        res = {}
        for name, shape, dt in RESIDENT:
            res[name] = sb(name, [P] + list(shape), dt)
        ident, upper, last_row, ones = res["ident"], res["upper"], res["last_row"], res["ones"]
        shift, shift_in = res["shift"], res["shift_in"]

        identb = sb("identb", [P, P], BF16)
        band = sb("band", [P, 2, 2 * KEYS], BF16)

        p1 = sb("p1", [P, T, H0])
        p2e = sb("p2e", [P, T, H0])
        pe_tok = sb("pe_tok", [P, T, W])
        rot_c = sb("rot_c", [P, DEPTH, T, 2, DL])
        rot_s = sb("rot_s", [P, DEPTH, T, 2, DL])
        sc = sb("sc", [P, 16])
        cq, ofac, epsr = sc[:, 0:1], sc[:, 1:2], sc[:, 2:3]
        bqc = sc[:, 4:5]
        gam = sb("gam", [P, W])

        x_in = sb("x_in", [P, T, W])
        xf = sb("xf", [P, T, W])
        s_at = sb("s_at", [P, T, W])
        zz = sb("zz", [P, T, W])
        x1 = sb("x1", [P, T, W])
        xn2 = sb("xn2", [P, T, W])
        tmp = sb("tmp", [P, T, W])
        tmp2 = sb("tmp2", [P, T, W])
        xa, s1 = s_at, zz
        xn = xn2
        xT = sb("xT", [P, N])
        st6 = sb("st6", [P, T, 6])
        mv = sb("mv", [P, T, 2])
        var = sb("var", [P, T])
        nr_y = sb("nr_y", [P, T])
        nr_t = sb("nr_t", [P, T])
        nmr = sb("nmr", [P, T])

        arena = sb("arena", [P, 22528])
        used = [0]

        def take(shape, dt=F32, at=None):
            n = int(np.prod(shape))
            words = n if dt == F32 else (n + 1) // 2
            if at is None:
                at = used[0]
                used[0] += words
            assert at + words <= 22528, (shape, at, words)
            v = arena[:, at:at + words]
            if dt == BF16:
                v = v.bitcast(BF16)
            names = " ".join(f"d{i}" for i in range(len(shape)))
            return v.rearrange(f"p ({names}) -> p {names}", **{f"d{i}": s for i, s in enumerate(shape)})

        nrow = take([N])
        u_a = take([2, N])
        u_k = take([2, N])
        sinb = take([2, N])
        ang = take([T, W // 2])
        ang_k = take([T, W // 2])
        rot_src = take([T, 4, DL])
        p2s = take([T, H0])
        band_f = take([2, 2 * KEYS])
        used[0] = 0
        cl = take([T, 48])
        ex = take([T, 48])
        rsum = take([T, H0])
        alpha = take([T, H0])
        den0 = take([T, H0])
        Aw = take([T, H0])
        Bw = take([T, H0])
        cv = take([2, HA])
        csb = take([2, HA])
        ub = take([2, HA])
        o_all = take([T, HA])
        oT = take([2, CH, P])
        used[0] = 0
        hs = take([4, N])
        ym = take([2, T, W])
        lr = take([T, 12])
        re = take([T, 12])
        rp = take([T, 12])
        rsm = take([T, 5])
        rinv = take([T, 5])
        cmp1 = take([T, NG, NG])
        cmp2 = take([T, NG, NG])
        rank = take([T, NG])
        selw = take([T, NG])
        sw = take([T])
        um = take([T, NG])
        ue = take([T, NG])
        first = take([T, NG])
        comb = take([T, NG, EPG])
        used[0] = 0
        QS = take([2, GH, N], BF16)
        KS = take([2, GH, N], BF16)
        vaug = take([T, H1, 32])
        pb_at = used[0]
        pb = take([8, N])
        at = pb_at
        qkf = take([2, N], F32, at); at += 2 * N
        qkr = take([2, N], F32, at); at += 2 * N
        qk3 = take([2, 3, N], BF16, at)
        on = tmp[:].rearrange("p t w -> p (t w)")
        den_t = tmp2[:].rearrange("p t w -> p (t w)")
        o_t = xT[:]
        mxp = take([2, GH, T, 2])
        mneg = take([2, GH * T])
        mrs = take([2, P])
        msp = take([2, 3, P], BF16)
        ks3 = take([2, N], BF16)
        q3a, q3b, k3a = [v[:].rearrange("p t w -> p (t w)").bitcast(BF16).rearrange("p (h n) -> p h n", n=N)
                         for v in (x_in, xf, zz)]
        Q_PIECES = [[QS[:, 0]], [QS[:, 1]], [q3a, q3b]]
        K_PIECES = [[KS[:, 0]], [KS[:, 1]], [k3a, ks3]]

        def slot(g):
            return g % 3

        def stacked(pieces, g, j):
            ps = pieces[slot(g)]
            per = GH // len(ps)
            return ps[j // per][:, j % per]

        def row_loads(g):
            return sum(len(Q_PIECES[slot(k)]) for k in range(g + 1))
        used[0] = 0
        kz = take([HL, WIN + N])
        qT = take([4, N])
        vl = take([T, INNER])
        ssq = take([T, 2 * HL])
        rq = take([T, 2 * HL])
        rqt = take([T, 2 * HL])
        ml = take([2, 4])
        sl = take([3, 4])
        rl = take([3, 4])
        after = used[0]
        pl = take([3, WIN + 4 * KEYS])
        ptA = take([2, 4, P])
        ptB = take([2, 4, P])
        olT = x_in[:].rearrange("p (q c) n -> p q c n", c=4)
        part = [take([2 * INNER], F32, after + i * 2 * INNER) for i in range(4)]
        hT = take([N], F32, after + 4 * 2 * INNER)
        flat = [v[:].rearrange("p t w -> p (t w)") for v in (tmp, x_in, s_at, tmp2)]
        qk_a = part[0:2] + flat[0:2]
        qk_b = flat[2:4]
        qk_sq = part[2:4]
        used[0] = HL * (WIN + N)
        gl = take([2, N])
        hg = take([3, N])

        names = """out_gone xnT_ps xnT lg clipped ex rs den_ps ab v_ps cv u cum_ps csb t1 o oT_ps oT s_ps s
        xr xrT_ps xrT rt rt_read rt_in rt_ex up_ps hs y ym z g0 x1 xn2
        xa xaT_ps xaT q_ps k_ps v1_ps qkf bf1 r1 bf2 bf3 vaug scr_w qs_loaded0 qs_loaded1 qs_loaded2 qs_loaded3 mx_ps mx mneg mT_ps m_read msp m_scr m_row
        st_ps p pv on on_moved otn xab op_ps x2 s1
        sh_ps hcp_v hT_ps hT hT_late qkv_ps sq rotb rqe qkr kq_ps kq vl s_lps ml p_exp pn ssq ssq_ok rq0 rot padded pt_ps pt o_lps olT ol_ps xf
        ffn_tile g_ps a_ps gl hg y2_ps xb gfin obuf
        cleared dve_step act_step arrive""".split()
        l0_names = names[1:names.index("x1")]
        S = {n: sem(n) for n in names}
        go, x_loaded, out_done, xn_tiles = sem("go"), sem("x_loaded"), sem("out_done"), sem("xn_tiles")
        S0 = {n: sem(n) for n in "w_loaded k_loaded dve0 act0 u_ready sn p_ps p_read2".split()}

        def stepper(eng, s):
            n = [0]

            def link(ins):
                n[0] += 1
                ins.then_inc(s, 1)
                eng.wait_ge(s, n[0])
            return link

        def max_bank(g, n):
            return n % 8 if g == 0 else 6 + n % 2

        def bc(v, shape, axis):
            return v.unsqueeze(axis).broadcast_to(shape)

        def meet(eng, b):
            eng.drain().then_inc(S["arrive"], 1)
            eng.wait_ge(go, b + 1)

        block = ctx.enter_context(nc.Block())

        @block.sync
        def _(sp):
            for name, _, _ in RESIDENT:
                sp.dma_start(res[name][:], d[name]).then_inc(S0["w_loaded"], 16)
            sp.dma_start(nrow, d["nrow"]).then_inc(S0["k_loaded"], 16)
            sp.dma_start(rot_src, d["rot_src"]).then_inc(S0["k_loaded"], 16)
            sp.dma_start(band_f, d["band"]).then_inc(S0["k_loaded"], 16)

            scr_q, scr_k, scr_m = d["scr_q"], d["scr_k"], d["scr_m"]
            sp.dma_start(x_in[:], d["x"][0].rearrange("(t p) w -> p t w", p=P)).then_inc(x_loaded, 16)
            sp.sem_inc(S["out_gone"], 1)
            with sp.Fori(0, B) as b:
                x_next = d["x"][bass.ds(b + 1, 1)].rearrange("a (t p) w -> p (a t) w", p=P)
                ob_ = out[bass.ds(b, 1)].rearrange("a (t p) w -> p (a t) w", p=P)
                for qk in range(2):
                    for i in range(3):
                        sp.wait_ge(S["bf%d" % (i + 1)], qk + 1)
                        for k in range(i, 3 if qk == 0 else 5, 3):
                            sp.dma_start((scr_k if qk else scr_q)[:, k], qk3[:, qk, i, :]).then_inc(S["scr_w"], 16)
                sp.wait_ge(S["scr_w"], 16 * PARTS_W)

                def load_group(g):
                    if g >= 3:
                        sp.wait_ge(S["on"], g - 2)
                    for qk, pieces in ((0, Q_PIECES[slot(g)]), (1, K_PIECES[slot(g)])):
                        per = GH // len(pieces)
                        for n, dst in enumerate(pieces):
                            h = GH * g + per * n
                            for i in range(3):
                                src = scr_k[h:h + per, i:i + 3] if qk else scr_q[h:h + per]
                                v = src.rearrange("h i c n -> (i c) h n")
                                sp.dma_start(dst[3 * DK * i:3 * DK * (i + 1)], v)\
                                    .then_inc(S["qs_loaded%d" % g], 16)

                def load_max(g):
                    sp.wait_ge(S["msp"], g + 1)
                    sp.dma_start(scr_m[g % 2].rearrange("i (r c) -> r i c", c=P), msp[0:GH * T, g % 2])\
                        .then_inc(S["m_scr"], 16)
                    sp.wait_ge(S["m_scr"], 16 * (g + 1))
                    pieces = Q_PIECES[slot(g)]
                    per = GH // len(pieces)
                    for n, dst in enumerate(pieces):
                        sp.dma_start(dst[MROW:MROW + 3],
                                     scr_m[g % 2, :, per * N * n:per * N * (n + 1)].rearrange("i (h n) -> i h n", n=N))\
                            .then_inc(S["m_row"], 16)

                def move_out(g):
                    sp.wait_ge(S["on"], g + 1)
                    for j in range(GH):
                        h = GH * g + j
                        sp.dma_start(o_t[DK * h:DK * h + DK], on[32 * j:32 * j + DK]).then_inc(S["on_moved"], 16)
                        sp.dma_start(den_t[DK * h:DK * h + DK], on[32 * j + DK:32 * j + 2 * DK])\
                            .then_inc(S["on_moved"], 16)

                sp.wait_ge(S["cleared"], 3)
                load_group(0)
                load_group(1)
                sp.wait_ge(S["cleared"], 10)
                load_group(2)
                load_max(0)
                load_max(1)
                move_out(0)
                load_group(3)
                load_max(2)
                move_out(1)
                load_max(3)
                move_out(2)
                move_out(3)
                for n in l0_names:
                    sp.sem_clear(S[n])
                sp.wait_ge(S["xf"], (2 * DEPTH - 1) * T)
                sp.dma_start(x_in[:], x_next).then_inc(x_loaded, 16)
                sp.wait_ge(S["obuf"], 1)
                sp.dma_start(ob_, tmp2[:]).then_inc(out_done, 16)
                sp.wait_ge(S["arrive"], ENGINES)
                for n in names:
                    if n not in l0_names:
                        sp.sem_clear(S[n])
                sp.sem_inc(go, 1)
                sp.wait_ge(out_done, b * 16 + 16)
                sp.sem_inc(S["out_gone"], 1)
            sp.wait_ge(x_loaded, 16 * (B + 1))

        @block.gpsimd
        def _(pool):
            with pool.Fori(0, B) as b:
                for t in range(T):
                    pool.wait_ge(S["t1"], t + 1)
                    pool.wait_ge(S["u"], t + 1)
                    pool.tensor_tensor(o_all[:, t], o_all[:, t], ub[:, t % 2], ALU.add).then_inc(S["o"], 1)
                for l in range(LOOPS):
                    for e in range(E - 1):
                        pool.wait_ge(S["ym"], l * E + e + 1)
                        if l * E + e:
                            pool.wait_ge(S["z"], l * E + e)
                        src = xn if l == 0 and e == 0 else zz
                        pool.tensor_tensor(zz[:], src[:], ym[:, e % 2], ALU.add).then_inc(S["z"], 1)
                pool.wait_ge(S["x1"], 1)
                pool.memset(QS[64:P], 0.0).then_inc(S["cleared"], 1)
                pool.wait_ge(S["cleared"], 1)
                pool.memset(KS[64:96], 0.0).then_inc(S["cleared"], 1)
                pool.wait_ge(S["cleared"], 2)
                pool.memset(KS[96:P], 1.0).then_inc(S["cleared"], 1)
                pool.wait_ge(S["cleared"], 3)
                pool.memset(vaug[:, :, :, DK:32], 1.0).then_inc(S["cleared"], 1)
                pool.wait_ge(S["cleared"], 4)
                cleared = 4
                for v, lo, hi, value in ((q3a, 64, P, 0.0), (q3b, 64, P, 0.0), (k3a, 64, 96, 0.0), (k3a, 96, P, 1.0),
                                         (ks3, 64, 96, 0.0), (ks3, 96, P, 1.0)):
                    pool.memset(v[lo:hi], value).then_inc(S["cleared"], 1)
                    cleared += 1
                    pool.wait_ge(S["cleared"], cleared)
                pool.wait_ge(S["xaT_ps"], T)
                pool.tensor_tensor(xa[:], xa[:], bc(res["bo"][:], [P, T, W], 1), ALU.add).then_inc(S["xab"], 1)
                pool.wait_ge(S["on"], NGRP)
                pool.memset(kz, 0.0).then_inc(S["cleared"], 1)
                pool.wait_ge(S["cleared"], 11)
                for l in range(DEPTH):
                    for t in range(T + 2):
                        u = l * T + t
                        if t < T:
                            v = qk_a[u % 4]
                            pool.wait_ge(S["rotb"], u + 1)
                            pool.tensor_tensor(v, v, qk_b[u % 2], ALU.add).then_inc(S["rot"], 1)
                        if t >= 2:
                            k = u - 2
                            pool.wait_ge(S["rot"], k + 1)
                            pool.wait_ge(S["rqe"], k + 1)
                            v = qk_a[k % 4][:, INNER:].rearrange("p (h c) -> p h c", c=DL)
                            pool.tensor_tensor(v, v, bc(rq[:, t - 2, HL:], [P, HL, DL], 2), ALU.mult)\
                                .then_inc(S["qkr"], 1)
                    pool.wait_ge(S["kq_ps"], 2 * T * (l + 1))
                    pool.memset(pl[:, :, 0:WIN], 0.0).then_inc(S["padded"], 1)
                    pool.wait_ge(S["padded"], 2 * l + 1)
                    pool.memset(ptA[0:WIN], 0.0).then_inc(S["padded"], 1)
                    if l == 0:
                        pool.wait_ge(S["x2"], T)
                        pool.tensor_tensor(s1[:], s1[:], bc(gam[:], [P, T, W], 1), ALU.mult).then_inc(S["s1"], 1)
                        pool.wait_ge(S["s1"], 1)
                        pool.tensor_tensor(s1[:], s1[:], bc(res["ln_beta"][:], [P, T, W], 1), ALU.add)\
                            .then_inc(S["s1"], 1)
                    pool.wait_ge(S["xf"], (2 * l + 1) * T)
                    pool.wait_ge(S["hT"], 4 * l + 4)
                    pool.tensor_tensor(tmp2[:], xf[:], bc(res["b2f"][:, l], [P, T, W], 1), ALU.add)\
                        .then_inc(S["xb"], 1)
                meet(pool, b)

        @block.scalar
        def _(act):
            act.wait_ge(S0["dve0"], 1)
            for i in range(2):
                for c in range(CH):
                    n = i * CH + c
                    act.wait_ge(S0["u_ready"], n + 1)
                    if n >= 2:
                        act.wait_ge(S0["p_ps"], n - 1)
                    act.activation(sinb[:, n % 2], u_a[:, n % 2], ACT.Sin, scale=6.283185).then_inc(S0["sn"], 1)
            act.wait_ge(S0["u_ready"], 2 * CH + 1)
            act.activation(pe_tok.rearrange("p t (f s) -> p t f s", s=2)[:, :, :, 0], ang, ACT.Sin)\
                .then_inc(S0["act0"], 1)
            act.activation(pe_tok.rearrange("p t (f s) -> p t f s", s=2)[:, :, :, 1], ang_k, ACT.Sin)\
                .then_inc(S0["act0"], 1)
            act.wait_ge(S0["p_read2"], 1)
            act.activation(p2e[:], p2s, ACT.Exp).then_inc(S0["act0"], 1)
            act.wait_ge(S0["act0"], 3)

            with act.Fori(0, B) as b:
                link = stepper(act, S["act_step"])

                for i in range(2):
                    act.wait_ge(S["xnT_ps"], 4 * i + 4)
                    act.copy(xT[:, i * HALF:i * HALF + HALF], PS[:, 6 + i, :]).then_inc(S["xnT"], 1)
                act.wait_ge(S["clipped"], 1)
                act.activation(ex, cl, ACT.Exp).then_inc(S["ex"], 1)
                for t in range(T):
                    act.wait_ge(S["cum_ps"], t + 1)
                    if t >= 2:
                        act.wait_ge(S["t1"], t - 1)
                    act.copy(csb[:, t % 2], pair(4 + 2 * (t % 2))).then_inc(S["csb"], 1)
                for t in range(T):
                    act.wait_ge(S["oT_ps"], t + 1)
                    if t >= 2:
                        act.wait_ge(S["s_ps"], t - 1)
                    act.copy(oT[:, t % 2].rearrange("p c n -> p (c n)"), pair(2 * (t % 2))).then_inc(S["oT"], 1)
                    if t % 4 == 3:
                        act.wait_ge(S["s_ps"], t + 1)
                        act.copy(s_at[:, t - 3:t + 1].rearrange("p t w -> p (t w)"), PS[:, 4 + t // 4, :])\
                            .then_inc(S["s"], 4)
                for l in range(LOOPS):
                    for i in range(2):
                        act.wait_ge(S["xrT_ps"], 8 * l + 4 * i + 4)
                        act.activation(xT[:, i * HALF:i * HALF + HALF], PS[:, i, :], ACT.Identity,
                                       scale=res["norm_w"][:, 0:1]).then_inc(S["xrT"], 1)
                    act.wait_ge(S["rt_in"], l + 1)
                    act.activation(re, re, ACT.Exp).then_inc(S["rt_ex"], 1)
                    for c in range(FC):
                        n = l * FC + c
                        act.wait_ge(S["up_ps"], n + 1)
                        if n >= 4:
                            act.wait_ge(S["y"], n // 2 - 1)
                        act.activation(hs[:, c % 4], pair(2 * (c % 2)), ACT.Silu).then_inc(S["hs"], 1)
                act.wait_ge(S["z"], LOOPS * E)
                act.activation(tmp[:], zz[:], ACT.Silu).then_inc(S["g0"], 1)
                for i in range(2):
                    act.wait_ge(S["xaT_ps"], 4 * i + 4)
                    act.copy(xT[:, i * HALF:i * HALF + HALF], PS[:, i, :]).then_inc(S["xaT"], 1)
                for qk in range(2):
                    act.wait_ge(S["q_ps" if qk == 0 else "k_ps"], 1)
                    if qk == 0:
                        act.activation(qkf[:, 0], pair(2), ACT.Identity, bias=bqc, scale=cq).then_inc(S["qkf"], 1)
                    else:
                        act.activation(qkf[:, 1], pair(4), ACT.Identity, bias=res["bk"][:, 0:1]).then_inc(S["qkf"], 1)
                for qk in range(2):
                    act.wait_ge(S["qkf"], qk + 1)
                    act.copy(qk3[:, qk, 0], qkf[:, qk]).then_inc(S["bf1"], 1)
                for qk in range(2):
                    act.wait_ge(S["r1"], qk + 1)
                    act.copy(qk3[:, qk, 1], qkr[:, qk]).then_inc(S["bf2"], 1)
                act.wait_ge(S["scr_w"], 16 * PARTS_W)
                for q in range(NGRP * T + 1):
                    for n in range(GH * q, GH * (q + 1)):
                        if q < NGRP * T:
                            act.wait_ge(S["st_ps"], n + 1)
                            if n >= 8:
                                act.wait_ge(S["pv"], n // GH - 1)
                            act.activation(pb[:, n % 8], pair(2 * (n % 2)), ACT.Exp).then_inc(S["p"], 1)
                    if q and q % T == 0:
                        g = q // T - 1
                        act.wait_ge(S["pv"], q)
                        if g:
                            act.wait_ge(S["on_moved"], 128 * g)
                        act.copy(on, pair(4)).then_inc(S["on"], 1)
                for l in range(DEPTH):
                    for i in range(2):
                        act.wait_ge(S["hT_ps"], 16 * l + 4 * i + 4)
                        act.copy(hT[0:64, i * HALF:i * HALF + HALF], PS[0:64, 1 + i, :]).then_inc(S["hT"], 1)

                    if l == 0:
                        act.wait_ge(S["cleared"], 11)
                    for t in range(T + 4):
                        u = l * T + t
                        if t >= 4:
                            k, tt = u - 4, t - 4
                            act.wait_ge(S["kq_ps"], 2 * k + 1)
                            act.copy(qT[:, :, P * tt:P * tt + P], PS[:, 6, :].rearrange("p (c n) -> p c n", c=4))\
                                .then_inc(S["kq"], 1)
                            act.wait_ge(S["kq_ps"], 2 * k + 2)
                            for r in range(2):
                                act.copy(kz.rearrange("p (c r) n -> p r c n", r=2)[64 * r:64 * r + 64, r, :,
                                                                                   WIN + P * tt:WIN + P * tt + P],
                                         PS[64 * r:64 * r + 64, 7, :].rearrange("p (c n) -> p c n", c=4))\
                                    .then_inc(S["kq"], 1)
                        if t < T:
                            act.wait_ge(S["rotb"], u + 1)
                            if u >= 2:
                                act.wait_ge(S["ssq"], u - 1)
                            act.activation(qk_sq[u % 2], pair(2 * (t % 2)), ACT.Square).then_inc(S["sq"], 1)
                            act.copy(vl[:, t], PS[:, 4 + t % 2, :]).then_inc(S["vl"], 1)
                        if 2 <= t <= T and t % 2 == 0:
                            k = t - 2
                            act.wait_ge(S["ssq_ok"], u // 2)
                            act.activation(rqt[:, k:k + 2], ssq[:, k:k + 2], ACT.Sqrt).then_inc(S["rq0"], 1)
                    act.wait_ge(S["padded"], 2 * (l + 1))
                    for u in range(2 * T + 4):
                        n = 2 * T * l + u
                        if u >= 5 and u % 2 == 1:
                            q = (n - 5) // 2
                            act.wait_ge(S["o_lps"], n - 3)
                            if q >= 2:
                                act.wait_ge(S["ol_ps"], q - 1)
                            act.copy(olT[:, q % 2], PS[:, 6, :].rearrange("p (c n) -> p c n", c=4))\
                                .then_inc(S["olT"], 1)
                        if u < 2 * T:
                            act.wait_ge(S["ml"], n + 1)
                            if n >= 3:
                                act.wait_ge(S["pt_ps"], 2 * n - 4)
                            for k in range(4):
                                act.activation(pl[:, n % 3, WIN + KEYS * k:WIN + KEYS * (k + 1)],
                                               PS[:, 2 * (n % 2) + k // 2, KEYS * (k % 2):KEYS * (k % 2) + KEYS],
                                               ACT.Exp, bias=ml[:, n % 2, k:k + 1],
                                               scale=rq[:, u // 2, 4 * (u % 2) + k:4 * (u % 2) + k + 1],
                                               accum_out=sl[:, n % 3, k:k + 1]).then_inc(S["p_exp"], 1)
                        if 2 <= u <= 2 * T + 1:
                            m = n - 2
                            if m >= 2:
                                act.wait_ge(S["o_lps"], m - 1)
                            act.wait_ge(S["pt_ps"], 2 * m + 1)
                            act.copy(ptA[WIN:P, m % 2], PS[WIN:P, 4, :].rearrange("p (c n) -> p c n", c=4))\
                                .then_inc(S["pt"], 1)
                            act.wait_ge(S["pt_ps"], 2 * m + 2)
                            act.copy(ptB[:, m % 2], PS[:, 5, :].rearrange("p (c n) -> p c n", c=4)).then_inc(S["pt"], 1)
                    for i in range(2):
                        act.wait_ge(S["hT_ps"], 16 * l + 8 + 4 * i + 4)
                        act.activation(xT[:, i * HALF:i * HALF + HALF], PS[:, 1 + i, :], ACT.Identity,
                                       bias=res["ln_b"][:, l:l + 1], scale=res["ln_g"][:, l:l + 1])\
                            .then_inc(S["hT"], 1)
                    for i, (c, m) in enumerate(HC):
                        n = l * 3 + i
                        act.wait_ge(S["g_ps"], n + 1)
                        if n >= 2:
                            act.wait_ge(S["hg"], n - 1)
                        act.activation(gl[0:m, n % 2], PS[0:m, 3:5, :].rearrange("p a n -> p (a n)"), ACT.Gelu,
                                       bias=res["b1g"][0:m, l * 3 + i:l * 3 + i + 1]).then_inc(S["gl"], 1)
                act.wait_ge(S["xf"], 2 * T * DEPTH)
                act.activation(tmp[:], xf[:], ACT.Silu).then_inc(S["gfin"], 1)
                meet(act, b)

        @block.vector
        def _(dve):
            dve.memset(sc[:], 0.0).then_inc(S0["dve0"], 1)
            dve.wait_ge(S0["dve0"], 1)
            dve.wait_ge(S0["w_loaded"], 16 * len(RESIDENT))
            dve.wait_ge(S0["k_loaded"], 48)
            k0 = [1]

            def link(ins):
                k0[0] += 1
                ins.then_inc(S0["dve0"], 1)
                dve.wait_ge(S0["dve0"], k0[0])

            link(dve.tensor_copy(identb[:], ident[:]))
            link(dve.tensor_copy(band[:], band_f))
            pa = res["pos_ab"]
            link(dve.tensor_scalar(pa[:], pa[:], 1.0 / TWO_PI, None, ALU.mult))
            for i in range(2):
                for c in range(CH):
                    n = i * CH + c
                    if n >= 2:
                        dve.wait_ge(S0["sn"], n - 1)
                    a, o = pa[:, 2 * i, c:c + 1], pa[:, 2 * i + 1, c:c + 1]
                    link(dve.tensor_scalar(u_a[:, n % 2], nrow, a, o, ALU.mult, ALU.add))
                    link(dve.tensor_scalar(u_k[:, n % 2], u_a[:, n % 2], MAGIC, MAGIC, ALU.add, ALU.subtract))
                    dve.tensor_tensor(u_a[:, n % 2], u_a[:, n % 2], u_k[:, n % 2], ALU.subtract)\
                        .then_inc(S0["u_ready"], 1)
            rby = res["rby"]
            link(dve.tensor_scalar(sc[:, 5:6], rby[:, 2:3], PM, 1.0, ALU.mult, ALU.add))
            link(dve.tensor_scalar(res["pe_base"][:], res["pe_base"][:], sc[:, 5:6], None, ALU.mult))
            link(dve.reciprocal(res["pe_base"][:], res["pe_base"][:]))
            link(dve.tensor_tensor(ang, bc(res["pos"][:], [P, T, W // 2], 2), bc(res["pe_base"][:], [P, T, W // 2], 1),
                                   ALU.mult))
            link(dve.tensor_scalar(ang_k, ang, 1.0 / TWO_PI, MAGIC, ALU.mult, ALU.add))
            link(dve.tensor_scalar(ang_k, ang_k, MAGIC, None, ALU.subtract))
            link(dve.scalar_tensor_tensor(ang, ang_k, -6.28125, ang, ALU.mult, ALU.add))
            link(dve.scalar_tensor_tensor(ang, ang_k, -(TWO_PI - 6.28125), ang, ALU.mult, ALU.add))
            link(dve.tensor_scalar(ang, ang, 3.1415925, -3.1415925, ALU.min, ALU.max))
            link(dve.tensor_scalar(ang_k, ang, -1.0, None, ALU.mult))
            link(dve.tensor_tensor(ang_k, ang_k, ang, ALU.min))
            dve.tensor_scalar(ang_k, ang_k, float(np.pi / 2), None, ALU.add).then_inc(S0["u_ready"], 1)
            link(dve.tensor_scalar(sc[:, 6:7], rby[:, 0:1], 0.1, 1.0, ALU.mult, ALU.add))
            link(dve.tensor_scalar(sc[:, 7:8], rby[:, 1:2], 0.05, None, ALU.mult))
            link(dve.tensor_tensor(sc[:, 8:9], sc[:, 6:7], sc[:, 7:8], ALU.add))
            link(dve.tensor_scalar(sc[:, 9:10], rby[:, 2:3], 0.15, None, ALU.mult))
            link(dve.tensor_tensor(sc[:, 8:9], sc[:, 8:9], sc[:, 9:10], ALU.add))
            link(dve.tensor_scalar(cq, sc[:, 8:9], 1.0 / float(np.sqrt(DK)), None, ALU.mult))
            link(dve.tensor_scalar(bqc, res["bq"][:, 0:1], cq, None, ALU.mult))
            link(dve.tensor_scalar(ofac, rby[:, 2:3], EPS_ADAPTIVE, 1.0, ALU.mult, ALU.add))
            link(dve.tensor_scalar(epsr, rby[:, 1:2], 0.1, 1.0, ALU.mult, ALU.add))
            link(dve.tensor_scalar(epsr, epsr, 1e-5, None, ALU.mult))
            link(dve.tensor_scalar(sc[:, 10:11], rby[:, 2:3], 0.05, None, ALU.mult))
            link(dve.tensor_tensor(sc[:, 10:11], sc[:, 10:11], sc[:, 6:7], ALU.add))
            link(dve.tensor_scalar(gam[:], res["ln_gamma"][:], sc[:, 10:11], None, ALU.mult))
            for l in range(DEPTH):
                for qk in range(2):
                    if qk == 0:
                        link(dve.tensor_scalar(res["qk_scale"][:, l, 0], res["qk_scale"][:, l, 0], 8.0, None, ALU.mult))
                    link(dve.tensor_tensor(rot_c[:, l, :, qk], rot_src[:, :, 2 * qk],
                                           bc(res["qk_scale"][:, l, qk, 0], [P, T, DL], 1), ALU.mult))
                    link(dve.tensor_tensor(rot_s[:, l, :, qk], rot_src[:, :, 2 * qk + 1],
                                           bc(res["qk_scale"][:, l, qk, 1], [P, T, DL], 1), ALU.mult))
            dve.wait_ge(S0["p_ps"], 2 * CH)
            link(dve.tensor_copy(p1.rearrange("p t h -> p (t h)"), PS[:, 0, 0:T * H0]))
            dve.tensor_scalar(p2s.rearrange("p t h -> p (t h)"), PS[:, 1, 0:T * H0], 20.0, -20.0, ALU.min, ALU.max)\
                .then_inc(S0["p_read2"], 1)
            dve.wait_ge(S0["act0"], 3)

            def rsqrt(v, y, t_, steps=3):
                link(dve.tensor_scalar(t_.bitcast(I32), v.bitcast(I32), 1, None, ALU.logical_shift_right))
                link(dve.tensor_scalar(y.bitcast(I32), t_.bitcast(I32), -1.0, RSQRT_SEED, ALU.mult, ALU.add))
                for _ in range(steps):
                    link(dve.scalar_tensor_tensor(t_, y, -0.5, y, ALU.mult, ALU.mult))
                    link(dve.tensor_tensor(t_, t_, v, ALU.mult))
                    link(dve.scalar_tensor_tensor(y, t_, 1.5, y, ALU.add, ALU.mult))

            def norm_scales(src, eps):
                if src is not None:
                    for t in range(T):
                        ins = dve.bn_stats(st6[:, t], src[:, t])
                    link(ins)
                for t in range(T):
                    ins = dve.bn_aggr(mv[:, t], st6[:, t])
                link(ins)
                link(dve.tensor_scalar(var[:], mv[:, :, 1], eps, None, ALU.add))
                rsqrt(var[:], nr_y[:], nr_t[:])
                link(dve.scalar_tensor_tensor(nmr[:], mv[:, :, 0], -1.0, nr_y[:], ALU.mult, ALU.mult))

            def norm_apply(src, dst, done):
                for t in range(T):
                    dve.tensor_scalar(dst[:, t], src[:, t], nr_y[:, t:t + 1], nmr[:, t:t + 1],
                                      ALU.mult, ALU.add).then_inc(done, 1)

            def layer_norm(src, dst, eps, done):
                norm_scales(src, eps)
                norm_apply(src, dst, S[done])

            dve.wait_ge(x_loaded, 16)
            norm_scales(x_in, 1e-5)
            norm_apply(x_in, xn, xn_tiles)

            with dve.Fori(0, B) as b:
                link = stepper(dve, S["dve_step"])

                dve.wait_ge(S["lg"], 1)
                lg = PS[:, 4, 0:T * 48].rearrange("p (t c) -> p t c", c=48)
                link(dve.tensor_tensor(cl[:, :, 0:16], lg[:, :, 0:16], p1[:], ALU.add))
                link(dve.tensor_scalar(cl[:, :, 16:48], lg[:, :, 16:48], 20.0, -20.0, ALU.min, ALU.max))
                dve.tensor_scalar(cl[:, :, 0:16], cl[:, :, 0:16], 20.0, -20.0, ALU.min, ALU.max)\
                    .then_inc(S["clipped"], 1)
                dve.wait_ge(S["ex"], 1)
                cross, diag, extra = ex[:, :, 0:16], ex[:, :, 16:32], ex[:, :, 32:48]
                link(dve.memset(rsum[:, 0], 0.0))
                for t in range(T - 1):
                    ins = dve.tensor_tensor(rsum[:, t + 1], rsum[:, t], cross[:, t], ALU.add)
                    if t < T - 2:
                        link(ins)
                ins.then_inc(S["rs"], 1)
                link(dve.tensor_tensor(alpha, p2e[:], extra, ALU.mult))
                dve.wait_ge(S["den_ps"], 1)
                link(dve.tensor_tensor(den0, PS[:, 5, 0:T * H0].rearrange("p (t h) -> p t h", h=H0), alpha, ALU.mult))
                link(dve.tensor_tensor(den0, den0, diag, ALU.add))
                link(dve.reciprocal(den0, den0))
                link(dve.tensor_tensor(Aw, alpha, den0, ALU.mult))
                dve.tensor_tensor(Bw, diag, den0, ALU.mult).then_inc(S["ab"], 1)
                dve.wait_ge(S["ab"], 1)

                def heads(v):
                    return v.rearrange("p (h a) -> p h a", a=A0)
                full = [P, H0, A0]
                for t in range(T + 1):
                    if t < T:
                        dve.wait_ge(S["v_ps"], t + 1)
                        if t >= 2:
                            dve.wait_ge(S["cum_ps"], t - 1)
                            dve.wait_ge(S["o"], t - 1)
                        v_ps = heads(pair(2 * (t % 2)))
                        dve.tensor_tensor(heads(cv[:, t % 2]), v_ps, bc(cross[:, t], full, 2), ALU.mult)\
                            .then_inc(S["cv"], 1)
                        dve.tensor_tensor(heads(ub[:, t % 2]), v_ps, bc(Bw[:, t], full, 2), ALU.mult)\
                            .then_inc(S["u"], 1)
                    if t >= 1:
                        k = t - 1
                        dve.wait_ge(S["csb"], k + 1)
                        dve.tensor_tensor(heads(o_all[:, k]), heads(csb[:, k % 2]), bc(Aw[:, k], full, 2), ALU.mult)\
                            .then_inc(S["t1"], 1)

                for l in range(LOOPS):
                    zs = xn if l == 0 else zz
                    if l:
                        dve.wait_ge(S["z"], E * l)
                    for t in range(T):
                        ins = dve.tensor_tensor_reduce(tmp[:, t], zs[:, t], zs[:, t], 1.0, 0.0, ALU.mult, ALU.add,
                                                       var[:, t:t + 1])
                    link(ins)
                    link(dve.tensor_scalar(var[:], var[:], 1.0 / W, 1e-6, ALU.mult, ALU.add))
                    rsqrt(var[:], nr_y[:], nr_t[:])
                    if l == 0:
                        dve.wait_ge(S["out_gone"], 1)
                    for t in range(T):
                        dve.tensor_scalar(tmp2[:, t], zs[:, t], nr_y[:, t:t + 1], None, ALU.mult)\
                            .then_inc(S["xr"], 1)
                    dve.wait_ge(S["rt"], l + 1)
                    dve.wait_ge(S["s"], T)
                    dve.tensor_copy(lr.rearrange("p t c -> p (t c)"), PS[:, 2, 0:T * 12]).then_inc(S["rt_read"], 1)
                    dve.wait_ge(S["rt_read"], l + 1)
                    mac, mic = lr[:, :, 0:NG], lr[:, :, NG:12].rearrange("p t (g e) -> p t g e", e=EPG)
                    emac, emic = re[:, :, 0:NG], re[:, :, NG:12].rearrange("p t (g e) -> p t g e", e=EPG)
                    pmac, pmic = rp[:, :, 0:NG], rp[:, :, NG:12].rearrange("p t (g e) -> p t g e", e=EPG)
                    link(dve.tensor_reduce(rsm[:, :, 0], mac, AX, ALU.max))
                    link(dve.tensor_reduce(rsm[:, :, 1:5], mic, AX, ALU.max))
                    link(dve.tensor_tensor(emac, mac, bc(rsm[:, :, 0], [P, T, NG], 2), ALU.subtract))
                    dve.tensor_tensor(emic, mic, bc(rsm[:, :, 1:5], [P, T, NG, EPG], 3), ALU.subtract)\
                        .then_inc(S["rt_in"], 1)
                    dve.wait_ge(S["rt_ex"], l + 1)
                    link(dve.tensor_reduce(rsm[:, :, 0], emac, AX, ALU.add))
                    link(dve.tensor_reduce(rsm[:, :, 1:5], emic, AX, ALU.add))
                    link(dve.reciprocal(rinv, rsm))
                    link(dve.tensor_tensor(pmac, emac, bc(rinv[:, :, 0], [P, T, NG], 2), ALU.mult))
                    link(dve.tensor_tensor(pmic, emic, bc(rinv[:, :, 1:5], [P, T, NG, EPG], 3), ALU.mult))
                    sq4 = [P, T, NG, NG]
                    link(dve.tensor_tensor(cmp1, bc(pmac, sq4, 2), bc(pmac, sq4, 3), ALU.is_gt))
                    link(dve.tensor_tensor(cmp2, bc(pmac, sq4, 2), bc(pmac, sq4, 3), ALU.is_equal))
                    link(dve.tensor_tensor(cmp2, cmp2, bc(res["before"][:], sq4, 1), ALU.mult))
                    link(dve.tensor_tensor(cmp1, cmp1, cmp2, ALU.add))
                    link(dve.tensor_reduce(rank, cmp1, AX, ALU.add))
                    link(dve.tensor_scalar(rank, rank, 2.0, None, ALU.is_lt))
                    link(dve.tensor_tensor(selw, pmac, rank, ALU.mult))
                    link(dve.tensor_reduce(sw, selw, AX, ALU.add))
                    link(dve.tensor_scalar(sw, sw, 1e-9, None, ALU.add))
                    link(dve.reciprocal(sw, sw))
                    link(dve.tensor_tensor(selw, selw, bc(sw, [P, T, NG], 2), ALU.mult))
                    link(dve.tensor_reduce(um, pmic, AX, ALU.max))
                    link(dve.tensor_scalar(ue, um, 1e-9, None, ALU.add))
                    link(dve.reciprocal(ue, ue))
                    link(dve.tensor_tensor(um, um, ue, ALU.mult))
                    link(dve.tensor_tensor(selw, selw, um, ALU.mult))
                    link(dve.tensor_tensor(first, pmic[:, :, :, 0], pmic[:, :, :, 1], ALU.is_ge))
                    link(dve.tensor_tensor(comb[:, :, :, 0], selw, first, ALU.mult))
                    link(dve.tensor_tensor(comb[:, :, :, 1], selw, comb[:, :, :, 0], ALU.subtract))
                    for e in range(E):
                        n = l * E + e
                        dve.wait_ge(S["y"], n + 1)
                        if n >= 2:
                            dve.wait_ge(S["z"], n - 1)
                        dve.tensor_tensor(ym[:, e % 2], pair(4 + 2 * (e % 2)).rearrange("p (t w) -> p t w", w=W),
                                          bc(comb[:, :, e // EPG, e % EPG], [P, T, W], 2), ALU.mult)\
                            .then_inc(S["ym"], 1)
                    dve.wait_ge(S["ym"], (l + 1) * E)
                    dve.wait_ge(S["z"], (l + 1) * E - 1)
                    dve.tensor_tensor(zz[:], zz[:], ym[:, (E - 1) % 2], ALU.add).then_inc(S["z"], 1)

                dve.wait_ge(S["g0"], 1)
                link(dve.tensor_tensor(tmp[:], tmp[:], s_at[:], ALU.mult))
                dve.tensor_tensor(x1[:], x_in[:], tmp[:], ALU.add).then_inc(S["x1"], 1)
                dve.wait_ge(S["x1"], 1)
                layer_norm(x1, xn2, 1e-5, "xn2")
                dve.wait_ge(S["xn2"], T)

                dve.tensor_tensor(xa[:], xn2[:], pe_tok[:], ALU.add).then_inc(S["xa"], 1)
                for qk in range(2):
                    dve.wait_ge(S["bf1"], qk + 1)
                    dve.tensor_tensor(qkr[:, qk], qkf[:, qk], qk3[:, qk, 0], ALU.subtract).then_inc(S["r1"], 1)
                for i in range(2):
                    dve.wait_ge(S["v1_ps"], 1)
                    dve.wait_ge(S["cleared"], 4)
                    dve.tensor_tensor(vaug[:, 4 * i:4 * i + 4, :, 0:DK],
                                      PS[:, 6 + i, :].rearrange("p (t h c) -> p t h c", t=4, c=DK),
                                      bc(res["bv"].rearrange("p (h c) -> p h c", c=DK), [P, 4, H1, DK], 1), ALU.add)\
                        .then_inc(S["vaug"], 1)
                for qk in range(2):
                    dve.wait_ge(S["bf2"], qk + 1)
                    dve.tensor_tensor(qk3[:, qk, 2], qkr[:, qk], qk3[:, qk, 1], ALU.subtract).then_inc(S["bf3"], 1)
                for g in range(NGRP):
                    for n in range(GH * T * 2):
                        j, t, hf = n // (2 * T), n // 2 % T, n % 2
                        dve.wait_ge(S["mx_ps"], g * 64 + n + 1)
                        dve.tensor_reduce(mxp[:, g % 2, j, t, hf:hf + 1], PS[:, max_bank(g, n), :], AX, ALU.max)\
                            .then_inc(S["mx"], 1)
                    dve.wait_ge(S["mx"], (g + 1) * 64)
                    link(dve.tensor_reduce(mneg[:, g % 2], mxp[:, g % 2].rearrange("p j t f -> p (j t) f"),
                                           AX, ALU.max))
                    dve.tensor_scalar(mneg[:, g % 2], mneg[:, g % 2], -1.0, None, ALU.mult).then_inc(S["mneg"], 1)
                    dve.wait_ge(S["mT_ps"], g + 1)
                    if g >= 2:
                        dve.wait_ge(S["m_scr"], 16 * (g - 1))
                    rows = slice(0, GH * T)
                    dve.tensor_copy(mrs[rows, 0], PS[rows, 6, 0:P]).then_inc(S["m_read"], 1)
                    dve.wait_ge(S["m_read"], g + 1)
                    link(dve.tensor_copy(msp[rows, g % 2, 0], mrs[rows, 0]))
                    link(dve.tensor_tensor(mrs[rows, 1], mrs[rows, 0], msp[rows, g % 2, 0], ALU.subtract))
                    link(dve.tensor_copy(msp[rows, g % 2, 1], mrs[rows, 1]))
                    dve.tensor_tensor(msp[rows, g % 2, 2], mrs[rows, 1], msp[rows, g % 2, 1], ALU.subtract)\
                        .then_inc(S["msp"], 1)
                dve.wait_ge(S["msp"], NGRP)
                dve.wait_ge(S["on"], NGRP)

                def shifted_half(l):
                    dve.memset(hT[64:P, 0:1], 0.0).then_inc(S["hT_late"], 1)
                    for i in range(2):
                        dve.wait_ge(S["hT_ps"], 16 * l + 4 * i + 4)
                        n = HALF - i
                        dve.tensor_copy(hT[64:P, HALF * i + 1:HALF * i + 1 + n], PS[64:P, 1 + i, 0:n])\
                            .then_inc(S["hT_late"], 1)

                shifted_half(0)
                dve.wait_ge(S["on_moved"], 128 * NGRP)
                link(dve.reciprocal(den_t, den_t))
                dve.scalar_tensor_tensor(o_t, o_t, ofac, den_t, ALU.mult, ALU.mult).then_inc(S["otn"], 1)
                dve.wait_ge(S["op_ps"], 1)
                dve.wait_ge(S["xab"], 1)
                link(dve.tensor_tensor(tmp.rearrange("p t w -> p (t w)"), pair(6), xa.rearrange("p t w -> p (t w)"),
                                       ALU.add))
                layer_norm(tmp, s1, epsr, "x2")
                dve.wait_ge(S["x2"], T)

                for l in range(DEPTH):
                    xs = xn2 if l == 0 else xf
                    if l:
                        shifted_half(l)

                    def rotate(t):
                        u = l * T + t
                        dve.wait_ge(S["qkv_ps"], u + 1)
                        if u >= 4:
                            dve.wait_ge(S["kq_ps"], 2 * u - 6)
                        if u >= 2:
                            dve.wait_ge(S["rot"], u - 1)
                        qk_ps = pair(2 * (t % 2))
                        shape = [P, 2, HL, DL]
                        dve.tensor_tensor(qk_a[u % 4].rearrange("p (q h c) -> p q h c", q=2, c=DL),
                                          qk_ps.rearrange("p (q h c) -> p q h c", q=2, c=DL),
                                          bc(rot_c[:, l, t], shape, 2), ALU.mult)
                        for hf in range(2):
                            o = qk_b[u % 2].rearrange("p (q h f c) -> p q h f c", q=2, h=HL, f=2)[:, :, :, hf]
                            v = qk_ps.rearrange("p (q h f c) -> p q h f c", q=2, h=HL, f=2)[:, :, :, 1 - hf]
                            w = rot_s[:, l, t].rearrange("p q (f c) -> p q f c", f=2)[:, :, hf]
                            ins = dve.tensor_tensor(o, v, bc(w, [P, 2, HL, DL // 2], 2), ALU.mult)
                        ins.then_inc(S["rotb"], 1)

                    for t in range(T + 1):
                        u = l * T + t
                        if t < T:
                            rotate(t)
                        if t >= 1:
                            k = t - 1
                            dve.wait_ge(S["sq"], u)
                            dve.tensor_reduce(ssq[:, k], qk_sq[(u - 1) % 2].rearrange("p (h c) -> p h c", c=DL),
                                              AX, ALU.add).then_inc(S["ssq"], 1)
                        if 2 <= t and t % 2 == 0:
                            k = t - 2
                            y, v, w = rq[:, k:k + 2], ssq[:, k:k + 2], rqt[:, k:k + 2]
                            dve.wait_ge(S["ssq"], u)
                            dve.tensor_scalar(v, v, 1e-24, None, ALU.max).then_inc(S["ssq_ok"], 1)
                            dve.wait_ge(S["rq0"], u // 2)
                            link(dve.reciprocal(y, w))
                            link(dve.scalar_tensor_tensor(w, y, -0.5, y, ALU.mult, ALU.mult))
                            link(dve.tensor_tensor(w, w, v, ALU.mult))
                            dve.scalar_tensor_tensor(y, w, 1.5, y, ALU.add, ALU.mult).then_inc(S["rqe"], 2)

                    def late_half(t):
                        dve.wait_ge(S["sh_ps"], l * T + t + 1)
                        dve.tensor_copy(tmp[:, t, 64:W], PS[:, 7, W:W + 64]).then_inc(S["hcp_v"], 1)
                        dve.wait_ge(S["xf"], 2 * T * l + t + 1)
                        dve.tensor_copy(tmp[:, t, 0:64], xf[:, t, 0:64]).then_inc(S["hcp_v"], 1)

                    def late_stats(t):
                        dve.wait_ge(S["hcp_v"], 2 * (l * T + t + 1))
                        return dve.bn_stats(st6[:, t], tmp[:, t])

                    for u in range(2 * T + 5):
                        n = 2 * T * l + u
                        if u < 2 * T:
                            sv = PS[:, 2 * (n % 2):2 * (n % 2) + 2, 0:2 * KEYS].rearrange("p a (h c) -> p a h c", h=2)
                            dve.wait_ge(S["s_lps"], n + 1)
                            if n >= 2:
                                dve.wait_ge(S["p_exp"], 4 * (n - 1))
                            link(dve.tensor_reduce(ml[:, n % 2].rearrange("p (a h) -> p a h", a=2), sv, AX, ALU.max))
                            dve.scalar_tensor_tensor(ml[:, n % 2], ml[:, n % 2], -1.0,
                                                     rq[:, u // 2, 4 * (u % 2):4 * (u % 2) + 4],
                                                     ALU.mult, ALU.mult).then_inc(S["ml"], 1)
                        if 1 <= u <= 2 * T:
                            m = n - 1
                            dve.wait_ge(S["p_exp"], 4 * (m + 1))
                            link(dve.reciprocal(rl[:, m % 3], sl[:, m % 3]))
                            v = pl[:, m % 3, WIN:WIN + 4 * KEYS].rearrange("p (h c) -> p h c", c=KEYS)
                            dve.tensor_tensor(v, v, bc(rl[:, m % 3], [P, 4, KEYS], 2), ALU.mult).then_inc(S["pn"], 1)
                        if u >= 6 and u % 2 == 0:
                            t = (u - 6) // 2
                            dve.wait_ge(S["ol_ps"], l * T + t + 1)
                            if t:
                                late_half(t - 1)
                            dve.tensor_tensor(xf[:, t], xs[:, t], PS[:, 7, 0:W], ALU.add).then_inc(S["xf"], 1)
                            if t:
                                late_stats(t - 1)
                    late_half(T - 1)
                    link(late_stats(T - 1))
                    norm_scales(None, 1e-5)
                    norm_apply(tmp, s_at, S["ffn_tile"])
                    if l == DEPTH - 1:
                        dve.wait_ge(x_loaded, b * 16 + 32)
                        dve.wait_ge(S["ffn_tile"], T * DEPTH)
                        norm_scales(x_in, 1e-5)
                    for i, (c, m) in enumerate(HC):
                        n = l * 3 + i
                        dve.wait_ge(S["gl"], n + 1)
                        dve.wait_ge(S["a_ps"], n + 1)
                        dve.scalar_tensor_tensor(hg[0:m, i], PS[0:m, 5:7, :].rearrange("p a n -> p (a n)"),
                                                 res["b1a"][0:m, n:n + 1], gl[0:m, n % 2], ALU.add, ALU.mult)\
                            .then_inc(S["hg"], 1)
                        if l == DEPTH - 1 and i == 1:
                            norm_apply(x_in, xn, xn_tiles)
                    dve.wait_ge(S["xb"], l + 1)
                    for i in range(2):
                        dve.wait_ge(S["y2_ps"], 2 * l + i + 1)
                        v = tmp2[:, 4 * i:4 * i + 4].rearrange("p t w -> p (t w)")
                        o = xf[:, 4 * i:4 * i + 4].rearrange("p t w -> p (t w)")
                        dve.tensor_tensor(o, v, PS[:, 7 if i == 0 else 0, :], ALU.add).then_inc(S["xf"], T // 2)
                    dve.wait_ge(S["xf"], 2 * T * (l + 1))
                dve.wait_ge(S["gfin"], 1)
                dve.wait_ge(S["s1"], 2)
                link(dve.tensor_tensor(tmp[:], tmp[:], s1[:], ALU.mult))
                dve.tensor_tensor(tmp2[:], tmp[:], x1[:], ALU.add).then_inc(S["obuf"], 1)
                meet(dve, b)

        @block.tensor
        def _(pe):
            def mm(o, w, v, start=True, stop=True, **kw):
                return pe.matmul(o, w, v, start=start, stop=stop, **kw)

            pe.wait_ge(S0["w_loaded"], 16 * len(RESIDENT))
            for i in range(2):
                for c in range(CH):
                    n = i * CH + c
                    pe.wait_ge(S0["sn"], n + 1)
                    for t in range(T):
                        ins = mm(PS[:, i, H0 * t:H0 * t + H0], sinb[:, n % 2, P * t:P * t + P], res["c_blk"][:, c],
                                 start=(c == 0 and t == 0), stop=(c == CH - 1), skip_group_check=True)
                    ins.then_inc(S0["p_ps"], 1)
            pe.wait_ge(S0["p_read2"], 1)

            def transposes(src, bank, ready, done, base=0):
                for t in range(T):
                    if ready:
                        pe.wait_ge(S[ready], base + t + 1)
                    pe.transpose(PS[:, bank + t // 4, P * (t % 4):P * (t % 4) + P], src[:, t], ident[:])\
                        .then_inc(S[done], 1)

            with pe.Fori(0, B) as b:
                pe.wait_ge(xn_tiles, b * T + T)
                transposes(xn, 6, None, "xnT_ps")
                pe.wait_ge(S["xnT"], 2)
                for t in range(T):
                    ins = mm(PS[:, 4, 48 * t:48 * t + 48], xT[:, P * t:P * t + P], res["k123"][:])
                ins.then_inc(S["lg"], 1)

                def values(t):
                    if t >= 2:
                        pe.wait_ge(S["u"], t - 1)
                    for hf in range(2):
                        ins = mm(PS[:, 2 * (t % 2) + hf, :], xT[:, P * t:P * t + P],
                                 res["vw"][:, HALF * hf:HALF * hf + HALF])
                    ins.then_inc(S["v_ps"], 1)

                values(0)
                values(1)
                pe.wait_ge(S["rs"], 1)
                mm(PS[:, 5, 0:T * H0], upper[:], ex[:, :, 0:16], stop=False)
                mm(PS[:, 5, 0:T * H0], ones[:], rsum, start=False).then_inc(S["den_ps"], 1)
                for t in range(T):
                    pe.wait_ge(S["cv"], t + 1)
                    if t == 0:
                        pe.wait_ge(S["ab"], 1)
                    if t >= 2:
                        pe.wait_ge(S["csb"], t - 1)
                    bank = 4 + 2 * (t % 2)
                    for hf in range(2):
                        ins = mm(PS[:, bank + hf, :], upper[:], cv[:, t % 2, HALF * hf:HALF * hf + HALF], stop=(t == 0))
                    if t:
                        pe.wait_ge(S["csb"], t)
                        for hf in range(2):
                            ins = mm(PS[:, bank + hf, :], last_row[:],
                                     csb[:, (t - 1) % 2, HALF * hf:HALF * hf + HALF], start=False)
                    ins.then_inc(S["cum_ps"], 1)
                    if t + 2 < T:
                        values(t + 2)

                def out_transposes(t):
                    pe.wait_ge(S["o"], t + 1)
                    if t == 1:
                        pe.wait_ge(S["u"], T)
                    if t >= 2:
                        pe.wait_ge(S["oT"], t - 1)
                    for c in range(CH):
                        ins = pe.transpose(PS[:, 2 * (t % 2) + c // 4, P * (c % 4):P * (c % 4) + P],
                                           o_all[:, t, P * c:P * c + P], ident[:])
                    ins.then_inc(S["oT_ps"], 1)

                out_transposes(0)
                pe.wait_ge(S["csb"], T)
                for t in range(T):
                    if t + 1 < T:
                        out_transposes(t + 1)
                    pe.wait_ge(S["oT"], t + 1)
                    for c in range(CH):
                        ins = mm(PS[:, 4 + t // 4, W * (t % 4):W * (t % 4) + W], oT[:, t % 2, c], res["wo0"][:, c],
                                 start=(c == 0), stop=(c == CH - 1))
                    ins.then_inc(S["s_ps"], 1)

                for l in range(LOOPS):
                    transposes(tmp2, 0, "xr", "xrT_ps", base=T * l)
                    pe.wait_ge(S["xrT"], 2 * l + 2)
                    for t in range(T):
                        ins = mm(PS[:, 2, 12 * t:12 * t + 12], xT[:, P * t:P * t + P], res["w_route"][:])
                    ins.then_inc(S["rt"], 1)

                    def up(c):
                        n = l * FC + c
                        if n >= 2:
                            pe.wait_ge(S["hs"], n - 1)
                        if c == 1:
                            pe.wait_ge(S["rt_read"], l + 1)
                        for i in range(2):
                            ins = mm(PS[:, 2 * (c % 2) + i, :], res["w1e"][:, P * c:P * c + P],
                                     xT[:, HALF * i:HALF * i + HALF])
                        ins.then_inc(S["up_ps"], 1)

                    def down(e):
                        n = l * E + e
                        pe.wait_ge(S["hs"], 2 * n + 2)
                        if n >= 2:
                            pe.wait_ge(S["ym"], n - 1)
                        else:
                            pe.wait_ge(S["s"], T)
                        for t in range(T):
                            for i in range(2):
                                c = 2 * e + i
                                ins = mm(PS[:, 4 + 2 * (e % 2) + t // 4, W * (t % 4):W * (t % 4) + W],
                                         hs[:, c % 4, P * t:P * t + P], res["w2e"][:, c], start=(i == 0), stop=(i == 1))
                        ins.then_inc(S["y"], 1)

                    up(0)
                    up(1)
                    for e in range(E):
                        if e + 1 < E:
                            up(2 * e + 2)
                            up(2 * e + 3)
                        down(e)

                pe.wait_ge(S["xa"], 1)
                transposes(xa, 0, None, "xaT_ps")
                pe.wait_ge(S["xaT"], 2)
                for i in range(2):
                    ins = mm(PS[:, 2 + i, :], res["wq"][:], xT[:, HALF * i:HALF * i + HALF])
                ins.then_inc(S["q_ps"], 1)
                for i in range(2):
                    ins = mm(PS[:, 4 + i, :], res["wk"][:], xT[:, HALF * i:HALF * i + HALF])
                ins.then_inc(S["k_ps"], 1)
                for t in range(T):
                    ins = mm(PS[:, 6 + t // 4, W * (t % 4):W * (t % 4) + W], xT[:, P * t:P * t + P], res["wv"][:])
                ins.then_inc(S["v1_ps"], 1)
                pe.wait_ge(S["vaug"], 2)
                pe.wait_ge(S["qkf"], 2)

                def maxima(lo, hi):
                    for m in range(lo, hi):
                        g, n = m // 64, m % 64
                        j, t, hf = n // (2 * T), n // 2 % T, n % 2
                        if n == 0:
                            pe.wait_ge(S["qs_loaded%d" % g], 16 * 6 * len(Q_PIECES[slot(g)]))
                            if g:
                                pe.wait_ge(S["m_read"], g)
                        if n >= (2 if g else 8):
                            pe.wait_ge(S["mx"], m - (1 if g else 7))
                        mm(PS[:, max_bank(g, n), :], stacked(Q_PIECES, g, j)[0:KM, P * t:P * t + P],
                           stacked(K_PIECES, g, j)[0:KM, HALF * hf:HALF * hf + HALF]).then_inc(S["mx_ps"], 1)
                        if n == 63:
                            pe.wait_ge(S["mx"], m + 1)
                            pe.wait_ge(S["mneg"], g + 1)
                            pe.transpose(PS[0:GH * T, 6, 0:P], mneg[:, g % 2], ident[:]).then_inc(S["mT_ps"], 1)

                ahead = 64 + 12
                maxima(0, ahead)
                for q in range(NGRP * T + 1):
                    if q < NGRP * T and q % T == 0:
                        pe.wait_ge(S["m_row"], 16 * row_loads(q // T))
                    for j in range(GH):
                        n = GH * q + j
                        if q < NGRP * T:
                            g, kt = q // T, q % T
                            m = ahead + 2 * n
                            maxima(min(m, 64 * NGRP), min(m + 1, 64 * NGRP))
                            if n >= 2:
                                pe.wait_ge(S["p"], n - 1)
                            for i in range(2):
                                ins = mm(PS[:, 2 * (n % 2) + i, :], stacked(K_PIECES, g, j)[:, P * kt:P * kt + P],
                                         stacked(Q_PIECES, g, j)[:, HALF * i:HALF * i + HALF])
                            ins.then_inc(S["st_ps"], 1)
                            maxima(min(m + 1, 64 * NGRP), min(m + 2, 64 * NGRP))
                        if q and j % 2 == 1:
                            g, k, i = (q - 1) // T, (q - 1) % T, j // 2
                            if i == 0:
                                pe.wait_ge(S["p"], GH * q)
                            if k == 0 and g:
                                pe.wait_ge(S["on"], g)
                            for h in range(GH):
                                ins = mm(PS[32 * h:32 * h + 32, 4 + i, :], vaug[:, k, GH * g + h],
                                         pb[:, (GH * (q - 1) + h) % 8, HALF * i:HALF * i + HALF],
                                         start=(k == 0), stop=(k == T - 1), tile_position=(0, 32 * h))
                            if i == 1:
                                ins.then_inc(S["pv"], 1)
                pe.wait_ge(S["p"], NGRP * T * GH)

                def out_products():
                    pe.wait_ge(S["otn"], 1)
                    for t in range(T):
                        ins = mm(PS[:, 6 + t // 4, W * (t % 4):W * (t % 4) + W], o_t[:, P * t:P * t + P], res["wo1"][:])
                    ins.then_inc(S["op_ps"], 1)

                for l in range(DEPTH):
                    xs = xn2 if l == 0 else xf

                    def shifted(t):
                        o = PS[:, 7, W:W + 64]
                        ins = mm(o, shift[:], xf[:, t, 64:W], stop=(t == 0))
                        if t:
                            ins = mm(o, shift_in[:], xf[:, t - 1, 64:W], start=False)
                        ins.then_inc(S["sh_ps"], 1)

                    if l:
                        pe.wait_ge(S["xf"], 2 * T * l)
                    else:
                        pe.wait_ge(S["xn2"], T)
                    transposes(xs, 1, None, "hT_ps")
                    pe.wait_ge(S["hT"], 4 * l + 2)
                    pe.wait_ge(S["hT_late"], 3 * l + 3)
                    if l == 0:
                        pe.wait_ge(S["on"], NGRP)

                    def qkv(t):
                        u = l * T + t
                        if t >= 2:
                            pe.wait_ge(S["vl"], u - 1)
                        w = res["wqkv"][:, l]
                        for i, bank in enumerate((2 * (t % 2), 2 * (t % 2) + 1, 4 + t % 2)):
                            ins = mm(PS[:, bank, :], hT[:, P * t:P * t + P], w[:, HALF * i:HALF * i + HALF])
                        ins.then_inc(S["qkv_ps"], 1)

                    def kq(t):
                        u = l * T + t
                        for i in range(2):
                            pe.wait_ge(S["qkr" if i else "rot"], u + 1)
                            if u:
                                pe.wait_ge(S["kq"], 3 * u - 2 + 2 * i)
                            for c in range(4):
                                ins = pe.transpose(PS[:, 6 + i, P * c:P * c + P],
                                                   qk_a[u % 4][:, HALF * i + P * c:HALF * i + P * c + P], ident[:])
                            ins.then_inc(S["kq_ps"], 1)

                    def scores(u):
                        t, hf = u // 2, u % 2
                        n = 2 * T * l + u
                        if n >= 2:
                            pe.wait_ge(S["p_exp"], 4 * (n - 1))
                        for a in range(2):
                            bank = 2 * (n % 2) + a
                            mm(PS[:, bank, 0:2 * KEYS], identb[:], band[:, 0 if t == 0 else 1], stop=False)
                            for k in range(2):
                                h = 4 * hf + 2 * a + k
                                ins = mm(PS[:, bank, KEYS * k:KEYS * k + KEYS], qT[:, h // 2, P * t:P * t + P],
                                         kz[:, h, P * t:P * t + KEYS], start=False, stop=(k == 1))
                        ins.then_inc(S["s_lps"], 1)

                    for t in range(T + 3):
                        if t < T:
                            qkv(t)
                        if l == 0 and t == 1:
                            out_products()
                        if t == 2 and l == 0:
                            pe.wait_ge(S["x2"], T)
                        if t >= 3:
                            kq(t - 3)
                    pe.wait_ge(S["kq"], 3 * T * (l + 1))
                    for u in range(2 * T + 4):
                        n = 2 * T * l + u
                        if u < 2 * T:
                            scores(u)
                        if 2 <= u <= 2 * T + 1:
                            m = n - 2
                            pe.wait_ge(S["pn"], m + 1)
                            for i in range(2):
                                if m:
                                    pe.wait_ge(S["pt"], 2 * m - 1 + i)
                                for k in range(4):
                                    c = KEYS * k + (0 if i == 0 else P)
                                    ins = pe.transpose(PS[:, 4 + i, P * k:P * k + P], pl[:, m % 3, c:c + P], ident[:])
                                ins.then_inc(S["pt_ps"], 1)
                        if 3 <= u <= 2 * T + 2:
                            m = n - 3
                            t, hf = (u - 3) // 2, (u - 3) % 2
                            q = l * T + t
                            pe.wait_ge(S["pt"], 2 * m + 2)
                            if hf == 0 and q:
                                pe.wait_ge(S["olT"], q)
                            for c in range(2):
                                for i in range(0 if t else 1, 2):
                                    for r in range(2):
                                        k = 2 * c + r
                                        col = 64 * (4 * hf + k)
                                        ins = mm(PS[64 * r:64 * r + 64, 6, P * (2 * hf + c):P * (2 * hf + c) + P],
                                                 vl[:, t - 1 + i, col:col + 64], (ptA if i == 0 else ptB)[:, m % 2, k],
                                                 start=(i == 1 and t == 0) or i == 0, stop=(i == 1),
                                                 tile_position=(0, 64 * r))
                            ins.then_inc(S["o_lps"], 1)
                        if u >= 5 and u % 2 == 1:
                            t = (u - 5) // 2
                            q = l * T + t
                            pe.wait_ge(S["olT"], q + 1)
                            pe.wait_ge(S["xf"], 2 * T * l + t)
                            if t > 1 or l:
                                pe.wait_ge(S["hcp_v"], 2 * (l * T + max(t - 1, 0)))
                            if t:
                                shifted(t - 1)
                            for c in range(4):
                                ins = mm(PS[:, 7, 0:W], olT[:, q % 2, c], res["wol"][:, l, c],
                                         start=(c == 0), stop=(c == 3))
                            ins.then_inc(S["ol_ps"], 1)
                    pe.wait_ge(S["xf"], (2 * l + 1) * T)
                    pe.wait_ge(S["hcp_v"], 2 * (l * T + T - 1))
                    shifted(T - 1)
                    transposes(s_at, 1, "ffn_tile", "hT_ps", base=T * l)
                    pe.wait_ge(S["hT"], 4 * l + 4)
                    def second(k):
                        pe.wait_ge(S["hg"], 3 * l + k + 1)
                        c, m = HC[k]
                        for t in range(T):
                            ins = mm(PS[:, 7 if t < 4 else 0, W * (t % 4):W * (t % 4) + W], hg[0:m, k, P * t:P * t + P],
                                     res["wf2"][0:m, l, k], start=(k == 0 and t % 4 == 0), stop=(k == 2),
                                     skip_group_check=True)
                            if k == 2 and t % 4 == 3:
                                ins.then_inc(S["y2_ps"], 1)

                    for i, (c, m) in enumerate(HC):
                        n = l * 3 + i
                        for part, bank, done, read in ((HID, 3, "g_ps", "gl"), (0, 5, "a_ps", "hg")):
                            if n:
                                pe.wait_ge(S[read], n)
                            for k in range(2):
                                ins = mm(PS[0:m, bank + k, :], res["wf1"][:, l, part + c:part + c + m],
                                         xT[:, HALF * k:HALF * k + HALF])
                            ins.then_inc(S[done], 1)
                        if i:
                            second(i - 1)
                    second(2)
                meet(pe, b)


RESIDENT = [
    ("ident", (P,), F32), ("upper", (P,), F32), ("last_row", (P,), F32), ("ones", (P,), F32),
    ("shift", (P,), F32), ("shift_in", (P,), F32), ("before", (NG, NG), F32),
    ("pos", (T,), F32), ("pe_base", (W // 2,), F32),
    ("k123", (48,), F32), ("vw", (HA,), F32), ("wo0", (CH, W), F32), ("pos_ab", (4, CH), F32), ("c_blk", (CH, H0), F32),
    ("norm_w", (1,), F32), ("w_route", (12,), F32), ("w1e", (E * F,), F32), ("w2e", (FC, W), F32),
    ("rby", (3,), F32), ("wq", (W,), F32), ("wk", (W,), F32), ("wv", (W,), F32), ("wo1", (W,), F32),
    ("bq", (1,), F32), ("bk", (1,), F32), ("bv", (W,), F32), ("bo", (W,), F32),
    ("ln_gamma", (W,), F32), ("ln_beta", (W,), F32),
    ("wqkv", (DEPTH, 3 * INNER), F32), ("qk_scale", (DEPTH, 2, 2, DL), F32), ("wol", (DEPTH, 4, W), F32),
    ("ln_g", (DEPTH,), F32), ("ln_b", (DEPTH,), F32), ("wf1", (DEPTH, 2 * HID), F32), ("wf2", (DEPTH, 3, W), F32),
    ("b1a", (DEPTH * 3,), F32), ("b1g", (DEPTH * 3,), F32), ("b2f", (DEPTH, W), F32),
]


def constants():
    c = {}
    f = np.float32
    c["ident"] = np.eye(P, dtype=f)
    c["upper"] = np.triu(np.ones((P, P), f))
    c["last_row"] = np.zeros((P, P), f)
    c["last_row"][P - 1] = 1
    c["ones"] = np.ones((P, P), f)
    c["shift"] = np.eye(P, k=1, dtype=f)
    c["shift_in"] = np.zeros((P, P), f)
    c["shift_in"][P - 1, 0] = 1
    q, k = np.arange(P)[:, None], np.arange(KEYS)[None, :]
    seen = (k >= q) & (k <= q + WIN)
    band = np.tile(np.stack([seen & (k >= WIN), seen], 1), 2)
    c["band"] = np.where(band, 0.0, -3e38).astype(f)
    g = np.arange(NG)
    c["before"] = np.broadcast_to((g[None, :] < g[:, None]).astype(f), (P, NG, NG)).copy()
    c["pos"] = (np.arange(T)[None, :] * P + np.arange(P)[:, None]).astype(f)
    i_even = np.arange(0, W, 2).astype(f)
    c["pe_base"] = np.broadcast_to(np.power(f(10000.0), f(2.0) * i_even / f(W)).astype(f), (P, W // 2)).copy()
    c["nrow"] = np.broadcast_to(np.linspace(0.0, 1.0, N, dtype=f), (P, N)).copy()
    half = np.arange(0, DL, 2).astype(f)
    inv = (f(1.0) / np.power(f(10000.0), half / f(DL))).astype(f)
    t = np.arange(N).astype(f)
    fr = (t[:, None] * inv[None, :]).astype(np.float64)
    fr = np.concatenate([fr, fr], -1)
    base = ((half + f(0.4 * DL)) / f(1.4 * DL)).astype(np.float64)
    power = ((t - N // 2) / f(WIN // 2)).astype(np.float64)
    s = base[None, :] ** power[:, None]
    s = np.concatenate([s, s], -1)
    sign = np.concatenate([-np.ones(DL // 2), np.ones(DL // 2)])
    tab = np.stack([np.cos(fr) * s, np.sin(fr) * s * sign, np.cos(fr) / s, np.sin(fr) / s * sign], 1)
    c["rot_src"] = np.ascontiguousarray(tab.astype(f).reshape(T, P, 4, DL).transpose(1, 0, 2, 3))
    return c


def layouts(i):
    f = np.float32

    def rows(v):
        return np.broadcast_to(np.asarray(v)[None], (P,) + np.asarray(v).shape).copy()

    def chunks(v, n):
        return np.ascontiguousarray(v.reshape((n, P) + v.shape[1:]).swapaxes(0, 1))

    a = {k: np.asarray(v) for k, v in i.items()}
    r = {}
    r["x"] = np.concatenate([a["L0_attn_x"], a["L0_attn_x"][:1]], 0)
    r["k123"] = np.concatenate([a["L0_attn_k1"], a["L0_attn_k2"], a["L0_attn_k3"]], 0).T
    r["vw"] = a["L0_attn_value_weight"].transpose(1, 0, 2).reshape(W, HA)
    r["wo0"] = chunks(a["L0_attn_output_weight"].transpose(0, 2, 1).reshape(HA, W), CH)
    r["pos_ab"] = np.stack([a[f"L0_attn_{n}"].reshape(CH, P).T for n in ("a1", "b1", "a2", "b2")], 1)
    cb = np.zeros((P, CH, H0), f)
    cc = a["L0_attn_c"].reshape(H0, NPOS)
    for h in range(H0):
        cb[NPOS * (h % 2):NPOS * (h % 2) + NPOS, h // 2, h] = cc[h]
    r["c_blk"] = cb
    r["norm_w"] = a["L0_ffn_norm_w"][:, None]
    r["w_route"] = np.concatenate([a["L0_ffn_w_macro"], a["L0_ffn_w_micro"].reshape(E, W)], 0).T
    r["w1e"] = a["L0_ffn_w1"].reshape(E * F, W).T
    r["w2e"] = chunks(a["L0_ffn_w2"].transpose(0, 2, 1).reshape(E * F, W), FC)
    r["rby"] = rows(a["L1_attn_rby"])
    for n in "qkv":
        r["w" + n] = a["L1_attn_W" + n].T
    r["wo1"] = a["L1_attn_Wo"].T
    r["bq"], r["bk"] = a["L1_attn_bq"][:, None], a["L1_attn_bk"][:, None]
    r["bv"], r["bo"] = rows(a["L1_attn_bv"]), rows(a["L1_attn_bo"])
    r["ln_gamma"], r["ln_beta"] = rows(a["L1_attn_ln_gamma"]), rows(a["L1_attn_ln_beta"])
    r["wqkv"] = a["L1_ffn_wqkv"].transpose(1, 0, 2)
    qs = np.stack([a["L1_ffn_q_scale"], a["L1_ffn_k_scale"]], 1)
    r["qk_scale"] = rows(np.stack([qs, np.roll(qs, DL // 2, -1)], 2))
    r["wol"] = a["L1_ffn_wo"].reshape(DEPTH, 4, P, W).transpose(2, 0, 1, 3)
    r["ln_g"], r["ln_b"] = a["L1_ffn_ln_g"].T, a["L1_ffn_ln_b"].T
    r["wf1"] = a["L1_ffn_w1"].transpose(1, 0, 2)
    w2 = np.zeros((DEPTH, 3 * P, W), f)
    w2[:, :HID] = a["L1_ffn_w2"]
    r["wf2"] = w2.reshape(DEPTH, 3, P, W).transpose(2, 0, 1, 3)
    for n, lo in (("b1a", 0), ("b1g", HID)):
        v = np.zeros((DEPTH, 3 * P), f)
        v[:, :HID] = a["L1_ffn_b1"][:, lo:lo + HID]
        r[n] = v.reshape(DEPTH * 3, P).T
    r["b2f"] = rows(a["L1_ffn_b2"])
    return {k: np.ascontiguousarray(v) for k, v in r.items()}


def kernel(**inputs):
    import concourse.bacc as _bacc
    from concourse.bass_utils import run_bass_kernel_spmd as _run

    nc = _bacc.Bacc("TRN2", target_bir_lowering=False, num_devices=1)
    arrays, d = {}, {}
    for name, v in {**constants(), **layouts(inputs)}.items():
        arrays[f"in_{name}"] = v
        d[name] = nc.dram_tensor(f"in_{name}", v.shape, mybir.dt.from_np(v.dtype), kind="ExternalInput").ap()
    d["scr_q"] = nc.dram_tensor("scr_q", (H1, 3, DK, N), BF16, kind="Internal").ap()
    d["scr_k"] = nc.dram_tensor("scr_k", (H1, 5, DK, N), BF16, kind="Internal").ap()
    d["scr_m"] = nc.dram_tensor("scr_m", (2, 3, GH * N), BF16, kind="Internal").ap()
    out = nc.dram_tensor("out_x", (B, N, W), F32, kind="ExternalOutput").ap()
    build(nc, d, out)
    r = _run(nc, [arrays], core_ids=[0])
    return r.results[0]["out_x"]
```
